# Optimizing a Trainium2 kernel written in Bass

```python
import numpy as np
import jax
import jax.numpy as jnp

def _softmax(x, axis=-1):
    return jax.nn.softmax(x, axis=axis)

def _gelu(x):
    return jax.nn.gelu(x, approximate=True)

def _silu(x):
    return jax.nn.silu(x)

def _sigmoid(x):
    return jax.nn.sigmoid(x)

def _layernorm(x, axis=-1, eps=1e-05):
    m = jnp.mean(x, axis=axis, keepdims=True)
    v = jnp.var(x, axis=axis, keepdims=True)
    return (x - m) / jnp.sqrt(v + eps)

def _scatter_add(tgt, idx, src, axis=0):
    return tgt.at[idx].add(src)

def _segment_sum(src, seg, n):
    return jax.ops.segment_sum(src, seg, n)
kernel_name = 'mk_gps_d1_gnn_r32_0d728b'

def setup_inputs(seed: int=0):
    np.random.seed(seed)
    _w = jnp.asarray

    def _rec_inputs():
        import jax
        import jax.numpy as jnp
        _gk = jax.random.key(seed)
        x = -0.0002117 + 1 * jax.random.normal(jax.random.fold_in(_gk, 1), (3125, 256), jnp.float32)
        src = jax.random.randint(jax.random.fold_in(_gk, 2), (50000,), 0, 3125, jnp.int32)
        dst = jnp.minimum((3125 * jax.random.uniform(jax.random.fold_in(_gk, 3), (50000,)) ** 2.0).astype(jnp.int32), 99999)
        _o = jnp.argsort(dst, stable=True)
        src = src[_o]
        dst = dst[_o]
        edge_weight = jax.random.uniform(jax.random.fold_in(_gk, 12), (50000,), jnp.float32, 0.0, 0.999998)
        edge_weight_n2 = jax.random.uniform(jax.random.fold_in(_gk, 13), (50000,), jnp.float32, 0.0, 0.999998)
        return (x, src, dst, edge_weight, edge_weight_n2)
    x, src, dst, edge_weight, edge_weight_n2 = _rec_inputs()

    def _L0_gnn_setup():
        import jax, jax.numpy as jnp
        import numpy as np
        N_NODES = 3125
        N_EDGES = 25000
        DIM = 256
        EPS = 1e-05
        key = jax.random.key(seed)
        ks = jax.random.split(key, 12)
        H = DIM
        s = 1.0 / np.sqrt(H)
        s2 = 1.0 / np.sqrt(2 * H)
        return {'feat': jax.random.normal(ks[0], (N_NODES, DIM), dtype=jnp.float32), 'src': jax.random.randint(ks[1], (N_EDGES,), 0, N_NODES, dtype=jnp.int32), 'dst': jax.random.randint(ks[2], (N_EDGES,), 0, N_NODES, dtype=jnp.int32), 'iw': jax.random.uniform(ks[3], (N_EDGES,), dtype=jnp.float32), 'ow': jax.random.uniform(ks[4], (N_EDGES,), dtype=jnp.float32), 'gamma': jnp.ones((DIM,), jnp.float32), 'beta': jnp.zeros((DIM,), jnp.float32), 'W_in': jax.random.uniform(ks[5], (H, H), jnp.float32, -s, s), 'b_in': jax.random.uniform(ks[6], (H,), jnp.float32, -s, s), 'W_out': jax.random.uniform(ks[7], (H, H), jnp.float32, -s, s), 'b_out': jax.random.uniform(ks[8], (H,), jnp.float32, -s, s), 'W_x2i': jax.random.uniform(ks[9], (2 * H, 2 * H), jnp.float32, -s2, s2), 'b_x2i': jax.random.uniform(ks[10], (2 * H,), jnp.float32, -s2, s2), 'W_h2h': jax.random.uniform(ks[11], (H, 2 * H), jnp.float32, -s, s)}
    _L0_gnn_all = _L0_gnn_setup()
    _L0_gnn_in = {k: v for k, v in _L0_gnn_all.items() if k in ('gamma', 'beta', 'W_in', 'b_in', 'W_out', 'b_out', 'W_x2i', 'b_x2i', 'W_h2h')}
    del _L0_gnn_all

    def _L0_mix_setup():
        import jax, jax.numpy as jnp
        import numpy as np
        B, N, C, H = (8, 512, 256, 8)
        D = C // H
        GH = C // 4
        key = jax.random.key(seed)
        ks = jax.random.split(key, 6)
        s = 0.02
        return {'x': jax.random.normal(ks[0], (B, N, C), dtype=jnp.float32), 'Wqkv': jax.random.normal(ks[1], (C, 3 * C), dtype=jnp.float32) * s, 'Wproj': jax.random.normal(ks[2], (C, C), dtype=jnp.float32) * s, 'bproj': jnp.zeros((C,), dtype=jnp.float32), 'ln_g': jnp.ones((C,), dtype=jnp.float32), 'ln_b': jnp.zeros((C,), dtype=jnp.float32), 'Wg1': jax.random.normal(ks[3], (C, GH), dtype=jnp.float32) * s, 'bg1': jnp.zeros((GH,), dtype=jnp.float32), 'Wg2': jax.random.normal(ks[4], (GH, C), dtype=jnp.float32) * s, 'bg2': jnp.zeros((C,), dtype=jnp.float32)}
    _L0_mix_all = _L0_mix_setup()
    _L0_mix_in = {k: v for k, v in _L0_mix_all.items() if k in ('Wqkv', 'Wproj', 'bproj', 'ln_g', 'ln_b', 'Wg1', 'bg1', 'Wg2', 'bg2')}
    del _L0_mix_all

    def _L0_ffn_setup():
        import jax, jax.numpy as jnp
        import numpy as np
        B, A = (128, 8)
        IN, OUT = (256, 256)
        SH1, SH2 = (256, 128)
        EH1, EH2 = (128, 64)
        E, TOPK = (4, 2)

        def _shared_mlp(x, W1, b1, W2, b2, W3, b3):
            h = jax.nn.relu(x @ W1 + b1)
            h = jax.nn.relu(h @ W2 + b2)
            return h @ W3 + b3

        def _experts_mlp(x, eW1, eb1, eW2, eb2, eW3, eb3):
            h = jax.nn.relu(jnp.einsum('baf,efh->ebah', x, eW1) + eb1[:, None, None, :])
            h = jax.nn.relu(jnp.einsum('ebah,ehg->ebag', h, eW2) + eb2[:, None, None, :])
            o = jnp.einsum('ebag,ego->ebao', h, eW3) + eb3[:, None, None, :]
            return jnp.moveaxis(o, 0, -1)
        key = jax.random.key(seed)
        ks = jax.random.split(key, 16)
        s = 0.05
        return {'x': jax.random.normal(ks[0], (B, A, IN), jnp.float32), 'sW1': jax.random.normal(ks[1], (IN, SH1), jnp.float32) * s, 'sb1': jnp.zeros((SH1,), jnp.float32), 'sW2': jax.random.normal(ks[2], (SH1, SH2), jnp.float32) * s, 'sb2': jnp.zeros((SH2,), jnp.float32), 'sW3': jax.random.normal(ks[3], (SH2, OUT), jnp.float32) * s, 'sb3': jnp.zeros((OUT,), jnp.float32), 'eW1': jax.random.normal(ks[4], (E, IN, EH1), jnp.float32) * s, 'eb1': jnp.zeros((E, EH1), jnp.float32), 'eW2': jax.random.normal(ks[5], (E, EH1, EH2), jnp.float32) * s, 'eb2': jnp.zeros((E, EH2), jnp.float32), 'eW3': jax.random.normal(ks[6], (E, EH2, OUT), jnp.float32) * s, 'eb3': jnp.zeros((E, OUT), jnp.float32), 'gW': jax.random.normal(ks[7], (IN, E), jnp.float32) * s, 'gb': jnp.zeros((E,), jnp.float32)}
    _L0_ffn_all = _L0_ffn_setup()
    _L0_ffn_in = {k: v for k, v in _L0_ffn_all.items() if k in ('sW1', 'sb1', 'sW2', 'sb2', 'sW3', 'sb3', 'eW1', 'eb1', 'eW2', 'eb2', 'eW3', 'eb3', 'gW', 'gb')}
    del _L0_ffn_all
    return {'x': x, 'src': src, 'dst': dst, 'edge_weight': edge_weight, 'edge_weight_n2': edge_weight_n2, 'L0_gnn_gamma': _L0_gnn_in['gamma'], 'L0_gnn_beta': _L0_gnn_in['beta'], 'L0_gnn_W_in': _L0_gnn_in['W_in'], 'L0_gnn_b_in': _L0_gnn_in['b_in'], 'L0_gnn_W_out': _L0_gnn_in['W_out'], 'L0_gnn_b_out': _L0_gnn_in['b_out'], 'L0_gnn_W_x2i': _L0_gnn_in['W_x2i'], 'L0_gnn_b_x2i': _L0_gnn_in['b_x2i'], 'L0_gnn_W_h2h': _L0_gnn_in['W_h2h'], 'L0_mix_Wqkv': _L0_mix_in['Wqkv'], 'L0_mix_Wproj': _L0_mix_in['Wproj'], 'L0_mix_bproj': _L0_mix_in['bproj'], 'L0_mix_ln_g': _L0_mix_in['ln_g'], 'L0_mix_ln_b': _L0_mix_in['ln_b'], 'L0_mix_Wg1': _L0_mix_in['Wg1'], 'L0_mix_bg1': _L0_mix_in['bg1'], 'L0_mix_Wg2': _L0_mix_in['Wg2'], 'L0_mix_bg2': _L0_mix_in['bg2'], 'L0_ffn_sW1': _L0_ffn_in['sW1'], 'L0_ffn_sb1': _L0_ffn_in['sb1'], 'L0_ffn_sW2': _L0_ffn_in['sW2'], 'L0_ffn_sb2': _L0_ffn_in['sb2'], 'L0_ffn_sW3': _L0_ffn_in['sW3'], 'L0_ffn_sb3': _L0_ffn_in['sb3'], 'L0_ffn_eW1': _L0_ffn_in['eW1'], 'L0_ffn_eb1': _L0_ffn_in['eb1'], 'L0_ffn_eW2': _L0_ffn_in['eW2'], 'L0_ffn_eb2': _L0_ffn_in['eb2'], 'L0_ffn_eW3': _L0_ffn_in['eW3'], 'L0_ffn_eb3': _L0_ffn_in['eb3'], 'L0_ffn_gW': _L0_ffn_in['gW'], 'L0_ffn_gb': _L0_ffn_in['gb']}

def reference(x, src, dst, edge_weight, edge_weight_n2, L0_gnn_gamma, L0_gnn_beta, L0_gnn_W_in, L0_gnn_b_in, L0_gnn_W_out, L0_gnn_b_out, L0_gnn_W_x2i, L0_gnn_b_x2i, L0_gnn_W_h2h, L0_mix_Wqkv, L0_mix_Wproj, L0_mix_bproj, L0_mix_ln_g, L0_mix_ln_b, L0_mix_Wg1, L0_mix_bg1, L0_mix_Wg2, L0_mix_bg2, L0_ffn_sW1, L0_ffn_sb1, L0_ffn_sW2, L0_ffn_sb2, L0_ffn_sW3, L0_ffn_sb3, L0_ffn_eW1, L0_ffn_eb1, L0_ffn_eW2, L0_ffn_eb2, L0_ffn_eW3, L0_ffn_eb3, L0_ffn_gW, L0_ffn_gb):
    import jax
    import jax.numpy as jnp

    def _L0_gnn_ref(feat, src, dst, iw, ow, gamma, beta, W_in, b_in, W_out, b_out, W_x2i, b_x2i, W_h2h):
        import jax, jax.numpy as jnp
        import numpy as np
        N_NODES = 3125
        N_EDGES = 25000
        DIM = 256
        EPS = 1e-05
        N = feat.shape[0]
        num_steps = 1
        mean = jnp.mean(feat, axis=0)
        var = jnp.var(feat, axis=0)
        h = (feat - mean) * jax.lax.rsqrt(var + EPS) * gamma + beta
        for _ in range(num_steps):
            feat_in = h @ W_in + b_in
            feat_out = h @ W_out + b_out
            a_in = jax.ops.segment_sum(feat_in[src] * iw[:, None], dst, num_segments=N)
            a_out = jax.ops.segment_sum(feat_out[dst] * ow[:, None], src, num_segments=N)
            a = jnp.concatenate((a_in, a_out), axis=1)
            xi = a @ W_x2i + b_x2i
            hh = h @ W_h2h
            i_i, i_n = jnp.split(xi, 2, axis=1)
            h_i, h_n = jnp.split(hh, 2, axis=1)
            input_gate = jax.nn.sigmoid(i_i + h_i)
            new_gate = jnp.tanh(i_n + h_n)
            h = new_gate + input_gate * (h - new_gate)
        return h

    def _L0_mix_ref(x, Wqkv, Wproj, bproj, ln_g, ln_b, Wg1, bg1, Wg2, bg2):
        import jax, jax.numpy as jnp
        import numpy as np
        B, N, C, H = (8, 512, 256, 8)
        D = C // H
        GH = C // 4
        b, n, c = x.shape
        h, d = (H, D)
        qkv = (x @ Wqkv).reshape(b, n, 3, h, d)
        q, k, v = (qkv[:, :, 0], qkv[:, :, 1], qkv[:, :, 2])
        k = jax.nn.softmax(k, axis=1)
        context = jnp.einsum('bnhd,bnhv->bhdv', k, v)
        out = jnp.einsum('bnhd,bhdv->bnhv', q, context).reshape(b, n, c)
        mu = jnp.mean(x, axis=-1, keepdims=True)
        var = jnp.var(x, axis=-1, keepdims=True)
        xn = (x - mu) * jax.lax.rsqrt(var + 1e-05) * ln_g + ln_b
        hgate = jax.nn.gelu(xn @ Wg1 + bg1, approximate=False)
        gate = jax.nn.sigmoid(hgate @ Wg2 + bg2)
        return out * gate @ Wproj + bproj

    def _L0_ffn_ref(x, sW1, sb1, sW2, sb2, sW3, sb3, eW1, eb1, eW2, eb2, eW3, eb3, gW, gb):
        import jax, jax.numpy as jnp
        import numpy as np
        B, A = (128, 8)
        IN, OUT = (256, 256)
        SH1, SH2 = (256, 128)
        EH1, EH2 = (128, 64)
        E, TOPK = (4, 2)

        def _shared_mlp(x, W1, b1, W2, b2, W3, b3):
            h = jax.nn.relu(x @ W1 + b1)
            h = jax.nn.relu(h @ W2 + b2)
            return h @ W3 + b3

        def _experts_mlp(x, eW1, eb1, eW2, eb2, eW3, eb3):
            h = jax.nn.relu(jnp.einsum('baf,efh->ebah', x, eW1) + eb1[:, None, None, :])
            h = jax.nn.relu(jnp.einsum('ebah,ehg->ebag', h, eW2) + eb2[:, None, None, :])
            o = jnp.einsum('ebag,ego->ebao', h, eW3) + eb3[:, None, None, :]
            return jnp.moveaxis(o, 0, -1)
        all_out = _experts_mlp(x, eW1, eb1, eW2, eb2, eW3, eb3)
        shared = _shared_mlp(x, sW1, sb1, sW2, sb2, sW3, sb3)
        gates = jax.nn.softmax(x @ gW + gb, axis=-1)
        topv, topi = jax.lax.top_k(gates, TOPK)
        topw = jax.nn.softmax(topv, axis=-1)
        sel = jnp.take_along_axis(all_out, topi[:, :, None, :], axis=-1)
        gated = jnp.sum(sel * topw[:, :, None, :], axis=-1)
        return shared + gated
    xn = _layernorm(x, axis=-1)
    x = x + _L0_gnn_ref(xn, src, dst, edge_weight, edge_weight_n2, L0_gnn_gamma, L0_gnn_beta, L0_gnn_W_in, L0_gnn_b_in, L0_gnn_W_out, L0_gnn_b_out, L0_gnn_W_x2i, L0_gnn_b_x2i, L0_gnn_W_h2h) + _L0_mix_ref(xn[None], L0_mix_Wqkv, L0_mix_Wproj, L0_mix_bproj, L0_mix_ln_g, L0_mix_ln_b, L0_mix_Wg1, L0_mix_bg1, L0_mix_Wg2, L0_mix_bg2)[0]
    x = x + _L0_ffn_ref(_layernorm(x, axis=-1)[None], L0_ffn_sW1, L0_ffn_sb1, L0_ffn_sW2, L0_ffn_sb2, L0_ffn_sW3, L0_ffn_sb3, L0_ffn_eW1, L0_ffn_eb1, L0_ffn_eW2, L0_ffn_eb2, L0_ffn_eW3, L0_ffn_eb3, L0_ffn_gW, L0_ffn_gb)[0]
    return x

_drawn_inputs = setup_inputs


def setup_inputs(seed=0):
    import zlib

    import numpy as np

    out = dict(_drawn_inputs(seed))
    spreads = {'L0_gnn_gamma': (1.0, 0.6),
     'L0_gnn_beta': (0.0, 0.8),
     'L0_mix_bproj': (0.0, 0.8),
     'L0_mix_ln_g': (1.0, 0.6),
     'L0_mix_ln_b': (0.0, 0.8),
     'L0_mix_bg1': (0.0, 0.8),
     'L0_mix_bg2': (0.0, 0.8),
     'L0_ffn_sb1': (0.0, 2.0),
     'L0_ffn_sb2': (0.0, 2.0),
     'L0_ffn_sb3': (0.0, 2.0),
     'L0_ffn_eb1': (0.0, 2.0),
     'L0_ffn_eb2': (0.0, 2.0),
     'L0_ffn_eb3': (0.0, 2.0),
     'L0_ffn_gb': (0.0, 2.0)}
    factors = {'L0_gnn_b_x2i': 51.08,
     'L0_mix_Wqkv': 8.0,
     'L0_mix_Wproj': 8.0,
     'L0_mix_Wg1': 8.0,
     'L0_mix_Wg2': 8.0,
     'edge_weight': 7.704,
     'edge_weight_n2': 7.354,
     'L0_gnn_W_in': 3.71,
     'L0_gnn_b_in': 8.0,
     'L0_gnn_W_out': 3.663,
     'L0_gnn_b_out': 8.0,
     'L0_gnn_W_h2h': 3.57,
     'L0_ffn_sW1': 6.324,
     'L0_ffn_sW2': 4.991,
     'L0_ffn_sW3': 3.469,
     'L0_ffn_eW1': 8.0,
     'L0_ffn_eW2': 8.0,
     'L0_ffn_eW3': 5.959,
     'L0_ffn_gW': 8.0}
    for name, (base, spread) in spreads.items():
        noise = np.random.default_rng([zlib.crc32(name.encode()), seed]).standard_normal(out[name].shape)
        drawn = base * np.exp(spread * noise) if base else spread * noise
        out[name] = jnp.asarray(drawn.astype(out[name].dtype))
    for name, factor in factors.items():
        out[name] = (out[name] * factor).astype(out[name].dtype)
    return out
```

```python
import concourse.bass as bass
from concourse import mybir
from contextlib import ExitStack

N, C, E = 3125, 256, 50000
P = 128
NB = -(-N // P)
NP = NB * P
LAST = N - (NB - 1) * P
KC = C // P
GB = 5
NG = NB // GB
GN = GB * P
HN = GN // 2
EC = -(-E // P)
STEPS = EC + NB
NEXP, EH1, EH2 = 4, 128, 64
GH = C // 4
HEADS, HD = 8, 32
FS = 23
FS_A = 12
SQ = 400
EPS = 1e-5
FAR = -1e30
FIRST_LOADS, LAST_LOADS = 13, 22
GR = 16
SORT_ORDER = (1, 0)
GATHER_ORDER = (0, 1)


class Tally:

    def __init__(self, sem):
        self.sem, self.n, self.i, self.per = sem, 0, None, 0

    def value(self):
        return self.n if self.i is None else self.i * self.per + (self.n - self.per)

    def made(self, ins, k=1):
        ins.then_inc(self.sem, k)
        self.n += k
        return ins

    def want(self, eng, k=1):
        self.n += k
        eng.wait_ge(self.sem, self.value())

    def again(self, eng, k=0):
        if self.i is not None or self.n > k:
            eng.wait_ge(self.sem, self.value() - k if k else self.value())

    def link(self, eng, ins):
        self.made(ins)
        eng.wait_ge(self.sem, self.value())


def run_turns(eng, turns, body, tallies):
    before = [t.n for t in tallies]
    body(0)
    pers = [t.n - n for t, n in zip(tallies, before)]
    with eng.Fori(1, turns) as i:
        starts = [t.n for t in tallies]
        for t, per in zip(tallies, pers):
            t.i, t.per = i, per
        body(i)
        for t, per, n in zip(tallies, pers, starts):
            assert t.n - n == per
            t.i = None
    for t, per in zip(tallies, pers):
        t.n += per * (turns - 2)


def gps_layer(nc, x, src, dst, ew_in, ew_out, gamma, beta, W_in, b_in, W_out, b_out, W_x2i, b_x2i,
              W_h2h, Wqkv, Wproj, bproj, ln_g, ln_b, Wg1, bg1, Wg2, bg2, sW1, sb1, sW2, sb2, sW3,
              sb3, eW1, eb1, eW2, eb2, eW3, eb3, gW, gb, out):
    f32, i32, bf16 = mybir.dt.float32, mybir.dt.int32, mybir.dt.bfloat16
    ALU, ACT, AX = mybir.AluOpType, mybir.ActivationFunctionType, mybir.AxisListType
    On = bass.IndirectOffsetOnAxis
    ds = bass.ds
    ctx = ExitStack()
    with ctx:
        def sb(name, shape, dt=f32):
            return ctx.enter_context(nc.sbuf_tensor(name, shape, dt))

        def sem(name):
            return ctx.enter_context(nc.semaphore(name))

        rec_dram = [nc.dram_tensor(f"rec_{d}", (P * EC, 3), f32, kind="Internal").ap() for d in ("to_dst", "to_src")]
        table = [nc.dram_tensor(f"table_{d}", (NP, C), f32, kind="Internal").ap() for d in ("in", "out")]

        XH = sb("XH", [P, KC, NP])
        OG = sb("OG", [P, KC, NP])
        AGG = [sb("AGG_in", [P, KC, NP]), sb("AGG_out", [P, KC, NP + NB])]
        FLAT = [a[:, :, :].rearrange("p k n -> p (k n)") for a in AGG]
        KROW = FLAT[0].rearrange("p (b c) -> p b c", b=NB)
        VROW = FLAT[1].rearrange("p (b k c) -> p b k c", b=NB, k=KC)
        ident = sb("ident", [P, P])
        ramp = sb("ramp", [P, P])
        steps_ramp = sb("steps_ramp", [P, STEPS])
        REC = [sb("REC_in", [P, EC, 3]), sb("REC_out", [P, EC, 3])]
        ADDR = [sb("ADDR_in", [P, EC], i32), sb("ADDR_out", [P, EC], i32)]
        step_off = [sb("step_off_in", [P, STEPS]), sb("step_off_out", [P, STEPS])]
        unsorted = sb("unsorted", [1, 1], i32)
        tile_no = sb("tile_no", [1, 2, STEPS], i32)
        acc_col = sb("acc_col", [1, 2, STEPS], i32)
        SREC = sb("SREC", [P, FS, 3])
        SADR = sb("SADR", [P, FS], i32)
        small = sb("small", [P, 900])
        upper = sb("upper", [P, P])
        onesm = sb("onesm", [P, P])
        diffm = sb("diffm", [NB + 1, NB + 1])
        headm = sb("headm", [P, P])
        CTX = sb("CTX", [P, KC, P])
        KMAX = sb("KMAX", [P, C])

        RSIZE = 19000
        R = sb("region", [P, RSIZE])

        def cutter(*spans):
            state = [list(s) for s in spans]

            def cut(*shape):
                size = 1
                for n in shape:
                    size *= n
                for s in state:
                    if s[0] + size <= s[1]:
                        v = R[:, s[0]:s[0] + size]
                        s[0] += size
                        if len(shape) == 2:
                            v = v.rearrange("p (a b) -> p a b", a=shape[0])
                        if len(shape) == 3:
                            v = v.rearrange("p (a b c) -> p a b c", a=shape[0], b=shape[1])
                        return v
                raise ValueError(shape)
            return cut

        cut = cutter((0, RSIZE))
        XROW = cut(NB, C)
        Wq = cut(KC, 3 * C)
        Wg1s = cut(KC, GH)
        Wg2s = cut(C)
        Wio = cut(KC, 2 * C)
        bio = cut(2 * C)
        XNR = cut(GB, C)
        XNNR = cut(GB, C)
        XTR = cut(KC, GN)
        XNT = cut(KC, GN)
        HG = cut(GN)
        QT = XNR.rearrange("p a b -> p (a b)").rearrange("p (k n) -> p k n", k=KC)
        HT = XNNR.rearrange("p a b -> p (a b)").rearrange("p (k n) -> p k n", k=KC)
        cut = cutter((0, NB * C))
        FSTAGE = cut(GB, 2 * C)
        cut = cutter((0, NB * C))
        GATH = cut(GR, C)
        ONEHOT = cut(8, P)
        RR = cut(GR, 3)
        REL = cut(GR)
        IR = cut(GR).bitcast(i32)
        LW = 8640
        cut = cutter((LW, LW + 6990))
        Wx = cut(6, 2 * C)
        Wp = cut(KC, C)
        W1s = cut(KC, 256)
        W2s = cut(2, 128)
        W3s = cut(C)
        W1e = cut(KC, NEXP, EH1)
        W2e = cut(NEXP, EH2)
        W3e = cut(2, C)
        B3 = cut(C)
        bp_row = cut(C)
        Wgate = cut(KC, NEXP)
        gb_row = cut(NEXP)
        bx = cut(4)
        bxh = cut(2)
        b1s = cut(2)
        b2s = cut(1)
        b1e = cut(NEXP)
        b2e = cut(2)
        cut = cutter((0, LW), (LW + 6990, RSIZE))
        E1 = cut(NEXP, GN)
        OGR = E1[:, 0:2, :]
        IG = E1[:, 2:4, :]
        GNN = cut(KC, GN)
        WGX = GNN.rearrange("p k n -> p (k n)").rearrange("p (j m c) -> p j m c", j=GB, m=2)
        X1 = cut(GB, C)
        XN1 = cut(GB, C)
        OUTR = XN1
        XT1 = cut(KC, GN)
        S1 = cut(2, GN)
        S2 = cut(GN)
        E2 = cut(2, GN)
        WGT = cut(GN)

        ONEB = FLAT[0][:, 0:(NB * EC + 1) // 2].bitcast(bf16)[:, 0:NB * EC].rearrange("p (b c) -> p b c", b=NB)
        GT = FLAT[0][0:NB + 1, 4900:4900 + STEPS]
        ddrep = FLAT[0][0:NB + 1, 5400:5400 + P]
        GTMP = FLAT[0][0:1, 5600:5600 + STEPS]
        EF = FLAT[1][:, 0:2048].rearrange("p (a b c) -> p a b c", a=4, b=4)
        EI = FLAT[1].bitcast(i32)[:, 2048:3072].rearrange("p (a b c) -> p a b c", a=2, b=4)
        KEYI, LOI, HII = (FLAT[1].bitcast(i32)[:, o:o + EC] for o in (3072, 5472, 5872))
        KEYB, ZERO, SLOT = (FLAT[1][:, o:o + EC] for o in (3472, 3872, 5072))
        SCAN = [FLAT[1][:, o:o + EC] for o in (4272, 4672)]

        SEQ = [XTR.rearrange("p k n -> p (k n)").bitcast(i32)[0:E // SQ, o:o + SQ] for o in (0, SQ)]

        FALL = XNT.rearrange("p k n -> p (k n)")[0:E // SQ, 0:SQ]

        at = [0]

        def few(n):
            at[0] += n
            assert at[0] <= 900
            return small[:, at[0] - n:at[0]]

        stats = few(NB * 6).rearrange("p (b s) -> p b s", s=6)
        mean, var, rstd, ws1, ws2 = few(NB), few(NB), few(NB), few(NB), few(NB)
        padneg, eps_col = few(NB), few(1)
        cnt = few(NB + 2)
        total, incl, base, zero_f = (few(NB + 1) for _ in range(4))
        colw = few(8)
        coli = few(2).bitcast(i32)
        gamma_c, beta_c, lng_c, lnb_c = few(KC), few(KC), few(KC), few(KC)
        bg1_c, bg2_c, bg2_h = few(1), few(KC), few(KC)
        h_scale, h_shift, rsum = few(KC), few(KC), few(KC)
        cs = few(7 * 6).rearrange("p (b s) -> p b s", s=6)
        bnmv = few(KC * 2).rearrange("p (k s) -> p k s", s=2)
        neghalf = few(GB)
        pref = few(NEXP)
        t_log, t_exp, t_g, t_sc, t_o1, t_o2, t_w = (few(GB * NEXP).rearrange("p (j e) -> p j e", e=NEXP) for _ in range(7))
        t_w5 = few(GB * (NEXP + 1)).rearrange("p (j e) -> p j e", e=NEXP + 1)
        t_m, t_m1, t_m2, t_gap, t_gap_e, t_wt = (few(GB) for _ in range(6))
        t_mean, t_var, t_rstd, t_a, t_c = (few(GB) for _ in range(5))

        bank = [ctx.enter_context(nc.psum_tensor(f"bank{b}", [P, 512], f32)) for b in range(8)]

        s_full = [sem(f"bank_full{b}") for b in range(8)]
        s_free = [sem(f"bank_free{b}") for b in range(8)]
        both = ("in", "out")
        s_const = sem("constants_ready")
        s_pad = sem("edge_pads_set")
        s_xz = sem("x_pad_zeroed")
        s_edges = sem("edges_loaded")
        s_eflt = sem("edges_float")
        s_seq = sem("dst_sequence_loaded")
        s_flag = sem("unsorted_known")
        s_rank = sem("in_rank_steps")
        s_x = sem("x_loaded")
        s_w1 = sem("first_weights_loaded")
        s_w2 = sem("last_weights_loaded")
        s_cnt = sem("counts_ready")
        s_list = [sem(f"work_list_ready_{d}") for d in both]
        s_addr = [sem(f"places_ready_{d}") for d in both]
        s_copied = [sem(f"records_staged_{d}") for d in both]
        s_scat = [[sem(f"scattered_{d}{h}") for h in "ab"] for d in both]
        s_rel = [sem(f"ordered_{d}") for d in both]
        s_gp = sem("gpsimd_steps")
        s_dve = sem("vector_steps")
        s_act = sem("scalar_steps")
        s_apart = sem("standalone_waits")
        s_var = sem("variances_ready")
        s_sd = sem("deviations_ready")
        s_xn = sem("xn_ready")
        s_xnr = sem("xn_rows_staged")
        s_xnnr = sem("xnn_rows_staged")
        s_xh = sem("xn_kept")
        s_kmax = sem("kmax_ready")
        s_kshift = sem("k_shifted")
        s_kexp = sem("k_exp_done")
        s_vrow = sem("v_rows_done")
        s_ht = sem("h_group_ready")
        s_hk = sem("h_kept")
        s_ogd = sem("gated_output_done")
        s_fst = sem("table_rows_staged")
        s_tab = sem("table_written")
        s_g = [[sem(f"gathered_{d}{k}") for k in range(4)] for d in both]
        s_rr = [sem(f"step_records_{d}") for d in both]
        s_ri = [sem(f"step_rows_{d}") for d in both]
        s_m = [sem(f"onehot_{d}") for d in both]
        s_agg = [sem(f"tile_multiplied_{d}") for d in both]
        s_add = [sem(f"tile_added_{d}") for d in both]
        s_gates = sem("gates_ready")
        s_gnn = sem("gnn_ready")
        s_xr = sem("x_rows_back")
        s_v1 = sem("ffn_variance_ready")
        s_r1 = sem("ffn_rstd_ready")
        s_xn1 = sem("ffn_rows_ready")
        s_gx = sem("gate_logits_shifted")
        s_gexp = sem("gate_exp")
        s_g2 = sem("gate_gap")
        s_g2e = sem("gate_gap_exp")
        s_wg = sem("expert_weights_ready")
        s_out = sem("out_rows_ready")
        s_st = sem("out_stored")

        block = ctx.enter_context(nc.Block())

        B_XN, B_XNN, B_HG = [0, 1, 2], [3, 4, 5], [6, 7]
        B_K, B_V, B_G = [0, 1, 2], [3, 4, 5], [6, 7, 0, 1]
        PLAN1 = B_XN + B_XNN + B_HG + B_K + B_V + B_G
        B_Q, B_F, B_O = [0, 1, 2, 3], [4, 5, 6, 7, 0], [1, 2, 3, 4]
        PLAN3 = B_Q + B_F + B_O
        T_X = [0, 1, 2, 3, 4, 5, 6, 7]
        T_R = [0, 1, 2, 3, 4]
        T_T = [5, 6, 7]
        T_L = [0]
        T_S1 = [1, 2, 3, 4]
        T_E1 = [5, 6, 7, 0, 1, 2, 3, 4]
        T_S2 = [5, 6]
        T_E2 = [7, 0, 1, 2]
        T_W = [3, 4, 5, 6, 7]
        T_O = [0, 1, 2, 3, 4]
        PLAN5 = T_X + T_R + T_T + T_L + T_S1 + T_E1 + T_S2 + T_E2 + T_W + T_O

        def tallies(sems):
            return [Tally(s) for s in sems]

        def skip(full, plan):
            for b in plan:
                full[b].n += 1

        def static(i):
            return isinstance(i, int)

        def apart(eng, i):
            if not static(i):
                eng.sem_inc(s_apart, 1)

        def col(v, c=P):
            return v.rearrange("(k p) -> p k", p=c)

        @block.sync
        def _(sp):
            sp.wait_ge(s_pad, 1)
            for k, (a, tile) in enumerate(((src, EI[:, 0]), (dst, EI[:, 1]), (ew_in, EF[:, 2]), (ew_out, EF[:, 3]))):
                whole = P * P * 3
                rest = (E - whole) // P
                sp.dma_start(tile[:, 0:3, :], a[0:whole].rearrange("(b q r) -> q b r", b=3, q=P)).then_inc(s_edges, 16)
                sp.dma_start(tile[0:rest, 3, :], a[whole:whole + rest * P].rearrange("(q r) -> q r", r=P)).then_inc(s_edges, 16)
                sp.dma_start(tile[rest:rest + 1, 3, 0:E - whole - rest * P],
                             a[whole + rest * P:E].rearrange("(a r) -> a r", a=1)).then_inc(s_edges, 16)
            sp.dma_start(SEQ[0], dst[0:E].rearrange("(q r) -> q r", r=SQ)).then_inc(s_seq, 16)
            sp.dma_start(SEQ[1][0:E // SQ - 1, :], dst[1:E - SQ + 1].rearrange("(q r) -> q r", r=SQ)).then_inc(s_seq, 16)
            sp.dma_start(SEQ[1][E // SQ - 1:E // SQ, 0:SQ - 1], dst[E - SQ + 1:E].rearrange("(a r) -> a r", a=1)).then_inc(s_seq, 16)
            sp.wait_ge(s_xz, 1)
            sp.dma_start(XROW[:, 0:NB - 1, :], x[0:(NB - 1) * P, :].rearrange("(b p) c -> p b c", p=P)).then_inc(s_x, 16)
            sp.dma_start(XROW[0:LAST, NB - 1, :], x[(NB - 1) * P:N, :]).then_inc(s_x, 16)

            def first(dst_, src_):
                sp.dma_start(dst_, src_).then_inc(s_w1, 16)

            first(Wq, Wqkv.rearrange("(k p) n -> p k n", p=P))
            first(Wg1s, Wg1.rearrange("(k p) n -> p k n", p=P))
            first(Wg2s[0:GH, :], Wg2)
            first(Wio[:, :, 0:C], W_in.rearrange("(k p) n -> p k n", p=P))
            first(Wio[:, :, C:2 * C], W_out.rearrange("(k p) n -> p k n", p=P))
            first(bio[:, 0:C], b_in.partition_broadcast(P))
            first(bio[:, C:2 * C], b_out.partition_broadcast(P))
            with nc.allow_non_contiguous_dma("per-channel vectors, a few hundred numbers each"):
                for t, v in ((gamma_c, gamma), (beta_c, beta), (lng_c, ln_g), (lnb_c, ln_b), (bg2_c, bg2)):
                    first(t, col(v))
                first(bg1_c[0:GH, :], col(bg1, GH))

            rows = [t.rearrange("(b p) c -> p b c", p=P) for t in table]
            fst = Tally(s_fst)
            for g in range(NG):
                fst.want(sp)
                for d in range(2):
                    sp.dma_start(rows[d][:, g * GB:(g + 1) * GB, :], FSTAGE[:, :, d * C:(d + 1) * C]).then_inc(s_tab, 16)

            sp.wait_ge(s_ogd, NG)
            sp.wait_ge(s_hk, NG)
            n_last = [0]

            def last(dst_, src_):
                sp.dma_start(dst_, src_).then_inc(s_w2, 16)
                n_last[0] += 1

            last(Wx[:, 0:4, :], W_x2i.rearrange("(k p) n -> p k n", p=P))
            last(Wx[:, 4:6, :], W_h2h.rearrange("(k p) n -> p k n", p=P))
            last(Wp, Wproj.rearrange("(k p) n -> p k n", p=P))
            last(W1s, sW1.rearrange("(k p) n -> p k n", p=P))
            last(W2s, sW2.rearrange("(k p) n -> p k n", p=P))
            last(W3s, sW3)
            for k in range(KC):
                last(W1e[:, k], eW1[:, k * P:(k + 1) * P, :].rearrange("e p h -> p e h"))
            last(W2e, eW2.rearrange("e p g -> p e g"))
            for q in range(2):
                last(W3e[:, q, :], eW3[2 * q:2 * q + 2].rearrange("e g o -> (e g) o"))
            last(B3[0:NEXP, :], eb3)
            last(B3[NEXP:NEXP + 1, :], sb3.rearrange("(a n) -> a n", a=1))
            last(Wgate, gW.rearrange("(k p) e -> p k e", p=P))
            last(gb_row, gb.partition_broadcast(P))
            last(bp_row, bproj.partition_broadcast(P))
            with nc.allow_non_contiguous_dma("per-channel vectors, a few hundred numbers each"):
                last(bx, col(b_x2i))
                last(b1s, col(sb1))
                last(b2s, col(sb2))
                last(b1e, eb1.rearrange("e p -> p e"))
                for q in range(2):
                    last(b2e[:, q:q + 1], eb2[2 * q:2 * q + 2, :].rearrange("e g -> (e g)").rearrange("(p a) -> p a", a=1))
            assert n_last[0] == LAST_LOADS

            sp.wait_ge(s_scat[1][0], 16 * FS_A * (EC // FS))
            sp.wait_ge(s_scat[1][1], 16 * (FS - FS_A) * (EC // FS))
            sp.dma_start(REC[1][:, :, :], rec_dram[1].rearrange("(p c) w -> p c w", p=P)).then_inc(s_rel[1], 16)

            sp.wait_ge(s_agg[GATHER_ORDER[1]], STEPS)
            sp.wait_ge(s_add[GATHER_ORDER[1]], STEPS)
            for g in range(NG):
                if g:
                    sp.wait_ge(s_out, g)
                b = g * GB + GB - 1
                n = min(P, N - b * P)
                sp.dma_start(X1[:, 0:GB - 1, :], x[g * GN:b * P, :].rearrange("(b p) c -> p b c", p=P)).then_inc(s_xr, 16)
                sp.dma_start(X1[0:n, GB - 1, :], x[b * P:b * P + n, :]).then_inc(s_xr, 16)
                sp.wait_ge(s_out, g + 1)
                sp.dma_start(out[g * GN:b * P, :].rearrange("(b p) c -> p b c", p=P), OUTR[:, 0:GB - 1, :]).then_inc(s_st, 16)
                sp.dma_start(out[b * P:b * P + n, :], OUTR[0:n, GB - 1, :]).then_inc(s_st, 16)
            sp.wait_ge(s_st, 32 * NG)

        @block.gpsimd
        def _(gp):
            ch = Tally(s_gp)
            gp.iota(ramp[:, :], [[1, P]], base=0, channel_multiplier=0, allow_small_or_imprecise_dtypes=True)
            gp.iota(steps_ramp[:, :], [[1, STEPS]], base=0, channel_multiplier=0, allow_small_or_imprecise_dtypes=True)
            gp.memset(eps_col, EPS)
            gp.memset(zero_f, 0.0)
            gp.memset(ident[:, :], 0.0)
            gp.memset(upper[:, :], 1.0)
            gp.memset(diffm[:, :], 0.0)
            gp.memset(headm[:, :], 0.5)
            gp.memset(padneg, 0.0)
            gp.memset(neghalf, -0.5)
            for e in range(NEXP):
                gp.memset(pref[:, e:e + 1], float(NEXP - e))
            gp.memset(t_w5[:, :, NEXP:NEXP + 1], 1.0)
            ch.link(gp, gp.memset(onesm[:, :], 1.0))
            gp.affine_select(out=ident[:, :], in_=ident[:, :], compare_op=ALU.not_equal, fill=1.0, base=0,
                             pattern=[[-1, P]], channel_multiplier=1)
            gp.affine_select(out=upper[:, :], in_=upper[:, :], compare_op=ALU.is_gt, fill=0.0, base=0,
                             pattern=[[1, P]], channel_multiplier=-1)
            gp.affine_select(out=diffm[:, :], in_=diffm[:, :], compare_op=ALU.not_equal, fill=1.0, base=0,
                             pattern=[[-1, NB + 1]], channel_multiplier=1)
            ch.link(gp, gp.affine_select(out=headm[:, :], in_=headm[:, :], compare_op=ALU.is_ge, fill=0.0, base=0,
                                         pattern=[[-HD, P // HD], [0, HD]], channel_multiplier=1))
            gp.affine_select(out=diffm[:, :], in_=diffm[:, :], compare_op=ALU.not_equal, fill=-1.0, base=1,
                             pattern=[[-1, NB + 1]], channel_multiplier=1)
            gp.affine_select(out=headm[:, :], in_=headm[:, :], compare_op=ALU.is_gt, fill=0.0, base=HD,
                             pattern=[[HD, P // HD], [0, HD]], channel_multiplier=-1)
            gp.affine_select(out=padneg[:, NB - 1:NB], in_=padneg[:, NB - 1:NB], compare_op=ALU.is_gt, fill=FAR, base=LAST,
                             pattern=[[0, 1]], channel_multiplier=-1).then_inc(s_const, 1)

            def scatter(d):
                staged, landed = Tally(s_copied[d]), [Tally(s) for s in s_scat[d]]

                def scatter_turn(i):
                    for half, (lo, hi) in enumerate(((0, FS_A), (FS_A, FS))):
                        landed[half].again(gp)
                        apart(gp, i)
                        staged.made(gp.tensor_copy(SREC[:, lo:hi, :], REC[d][:, ds(i * FS + lo, hi - lo), :]))
                        staged.made(gp.tensor_copy(SADR[:, lo:hi], ADDR[d][:, ds(i * FS + lo, hi - lo)]))
                        staged.again(gp)
                        apart(gp, i)
                        for j in range(lo, hi):
                            landed[half].made(gp.indirect_dma_start(
                                rec_dram[d][:, :], On(ap=SADR[:, j:j + 1], axis=0), SREC[:, j, :], None), 16)

                gp.wait_ge(s_addr[d], 1)
                run_turns(gp, EC // FS, scatter_turn, [staged] + landed)

            scatter(1)
            gp.wait_ge(s_flag, 1)
            falls = gp.value_load(unsorted[0:1, 0:1], min_val=0, max_val=E)
            with gp.If(falls > 0):
                gp.wait_ge(s_scat[1][0], 16 * FS_A * (EC // FS))
                gp.wait_ge(s_scat[1][1], 16 * (FS - FS_A) * (EC // FS))
                scatter(0)
                gp.wait_ge(s_scat[0][0], 16 * FS_A * (EC // FS))
                gp.wait_ge(s_scat[0][1], 16 * (FS - FS_A) * (EC // FS))
                gp.dma_start(REC[0][:, :, :], rec_dram[0].rearrange("(p c) w -> p c w", p=P)).then_inc(s_rel[0], 16)
            with gp.If(falls < 1):
                gp.sem_inc(s_rel[0], 16)

            gp.wait_ge(s_tab, 16 * 2 * NG)
            gp.wait_ge(s_ogd, NG)
            for d in GATHER_ORDER:
                picked, rows_read, landed = Tally(s_rr[d]), Tally(s_ri[d]), [Tally(s) for s in s_g[d]]
                if d == GATHER_ORDER[1]:
                    gp.wait_ge(s_agg[GATHER_ORDER[0]], STEPS)

                def gather_turn(i, d=d, picked=picked, rows_read=rows_read, landed=landed):
                    for q in range(4):
                        if q % 2 == 0:
                            picked.want(gp)
                            for t in landed[q:q + 2]:
                                t.again(gp)
                            apart(gp, i)
                            rows_read.made(gp.tensor_copy(IR[:, 4 * q:4 * q + 8], RR[:, 4 * q:4 * q + 8, 0]))
                            rows_read.again(gp)
                            apart(gp, i)
                        if not static(i):
                            gp.wait_ge(s_agg[d], i * GR + (4 * (q + 1) - GR))
                            apart(gp, i)
                        for j in range(4 * q, 4 * q + 4):
                            landed[q].made(gp.indirect_dma_start(
                                GATH[:, j, :], None, table[d][:, :], On(ap=IR[:, j:j + 1], axis=0)), 16)

                run_turns(gp, STEPS // GR, gather_turn, [picked, rows_read] + landed)

            v1 = Tally(s_v1)

            def rstd_turn(g):
                v1.want(gp)
                gp.tensor_tensor(t_rstd, t_var, neghalf, ALU.pow).then_inc(s_r1, 1)

            run_turns(gp, NG, rstd_turn, [v1])

        @block.scalar
        def _(act):
            full, free = [Tally(s) for s in s_full], s_free

            def out_of(b, g=0):
                full[b].want(act)
                if not static(g):
                    apart(act, g)
                return bank[b]

            def transposed(plan, o):
                for k, b in enumerate(plan[:2]):
                    act.activation(o[:, k, 0:GN - P], out_of(b)[:, 0:GN - P], ACT.Copy).then_inc(free[b], 1)
                ps = out_of(plan[2])[:, 0:KC * P].rearrange("p (k n) -> p k n", k=KC)
                act.activation(o[:, :, GN - P:GN], ps, ACT.Copy).then_inc(free[plan[2]], 1)

            act.wait_ge(s_const, 1)
            for n in range(2):
                act.wait_ge(s_var, n + 1)
                act.activation(rstd, var, ACT.Sqrt, bias=eps_col).then_inc(s_sd, 1)

            act.wait_ge(s_xn, 3)
            skip(full, [0, 1, 2, 3] + 2 * [4, 5, 6, 6, 7, 7])

            def stage1(g):
                act.activation(XNR, XROW[:, ds(g * GB, GB), :], ACT.Copy).then_inc(s_xnr, 1)
                for k, b in enumerate(B_XN[:2]):
                    ps = out_of(b, g)
                    act.activation(XH[:, k, ds(g * GN, GN - P)], ps[:, 0:GN - P], ACT.Copy)
                    act.activation(XTR[:, k, 0:GN - P], ps[:, 0:GN - P], ACT.Copy).then_inc(free[b], 1)
                ps = out_of(B_XN[2], g)[:, 0:KC * P].rearrange("p (k n) -> p k n", k=KC)
                act.activation(XH[:, :, ds(g * GN + (GN - P), P)], ps, ACT.Copy).then_inc(s_xh, 1)
                act.activation(XTR[:, :, GN - P:GN], ps, ACT.Copy).then_inc(free[B_XN[2]], 1)
                skip(full, B_XNN)
                for h, b in enumerate(B_HG):
                    act.activation(HG[0:GH, h * HN:(h + 1) * HN], out_of(b)[0:GH, 0:HN], ACT.Gelu,
                                   bias=bg1_c[0:GH, :]).then_inc(free[b], 1)
                skip(full, B_K)
                for q, b in enumerate(B_V):
                    n = min(2, GB - 2 * q)
                    ps = out_of(b, g)[:, 0:n * C].rearrange("p (b k c) -> p b k c", b=n, k=KC)
                    for j in range(n):
                        o = VROW[:, ds(g * GB + 2 * q + j, 1), :, 0:P].rearrange("p a k c -> p (a k) c")
                        last = act.activation(o, ps[:, j], ACT.Copy)
                    last.then_inc(free[b], 1)
                for q, b in enumerate(B_G):
                    m, h = divmod(q, 2)
                    act.activation(OG[:, m, ds(g * GN + h * HN, HN)], out_of(b, g)[:, 0:HN], ACT.Tanh,
                                   bias=bg2_h[:, m:m + 1], scale=0.5).then_inc(free[b], 1)

            run_turns(act, NG, stage1, full)

            act.wait_ge(s_var, 3)
            act.activation(h_scale, bnmv[:, :, 1], ACT.Sqrt, bias=eps_col).then_inc(s_sd, 1)
            act.wait_ge(s_kshift, 1)
            act.activation(KROW, KROW, ACT.Exp).then_inc(s_kexp, 1)
            skip(full, [2, 3, 4, 5])

            ht = Tally(s_ht)

            def stage3(g):
                for q, b in enumerate(B_Q):
                    m, h = divmod(q, 2)
                    act.activation(QT[:, m, h * HN:(h + 1) * HN], out_of(b)[:, 0:HN], ACT.Copy).then_inc(free[b], 1)
                skip(full, B_F + B_O)
                ht.want(act)
                apart(act, g)
                act.activation(XH[:, :, ds(g * GN, GN)], HT, ACT.Copy).then_inc(s_hk, 1)

            run_turns(act, NG, stage3, full + [ht])

            for d in GATHER_ORDER:
                act.wait_ge(s_list[d], 1)
                act.wait_ge(s_rel[d], 16)
                if d == GATHER_ORDER[1]:
                    act.wait_ge(s_ri[GATHER_ORDER[0]], 2 * (STEPS // GR))
                    act.wait_ge(s_m[GATHER_ORDER[0]], STEPS)

                def pick_turn(i, d=d):
                    cols = [act.value_load(tile_no[0:1, d, ds(i * GR + j, 1)], min_val=0, max_val=EC - 1) for j in range(GR)]
                    for h in range(2):
                        if not static(i):
                            act.wait_ge(s_ri[d], i * 2 + (h - 1))
                            act.wait_ge(s_m[d], i * GR + (8 * h - 8))
                            apart(act, i)
                        for j in range(8 * h, 8 * h + 8):
                            last = act.activation(RR[:, j:j + 1, :], REC[d][:, ds(cols[j], 1), :], ACT.Copy)
                        last.then_inc(s_rr[d], 1)

                run_turns(act, STEPS // GR, pick_turn, [])

            gx, g2 = Tally(s_gx), Tally(s_g2)
            act.wait_ge(s_w2, 16 * LAST_LOADS)
            act.activation(bxh, bx[:, 0:2], ACT.Copy, scale=0.5).then_inc(s_act, 1)
            act.wait_ge(s_act, 1)

            def stage5(g):
                for q, b in enumerate(T_X):
                    m, h = divmod(q, 2)
                    o = (IG if m < 2 else GNN)[:, m % 2, h * HN:(h + 1) * HN]
                    bias = bxh[:, m:m + 1] if m < 2 else bx[:, m:m + 1]
                    act.activation(o, out_of(b)[:, 0:HN], ACT.Tanh, bias=bias,
                                   scale=(0.5 if m < 2 else 1.0)).then_inc(free[b], 1)
                act.activation(OGR, OG[:, :, ds(g * GN, GN)], ACT.Copy).then_inc(s_gates, 1)
                skip(full, T_R)
                transposed(T_T, XT1)
                skip(full, T_L)
                gx.want(act)
                act.activation(t_exp, t_log, ACT.Exp).then_inc(s_gexp, 1)
                for q, b in enumerate(T_S1):
                    m, h = divmod(q, 2)
                    act.activation(S1[:, m, h * HN:(h + 1) * HN], out_of(b)[:, 0:HN], ACT.Relu,
                                   bias=b1s[:, m:m + 1]).then_inc(free[b], 1)
                for q, b in enumerate(T_E1):
                    m, h = divmod(q, 2)
                    if h == 0:
                        act.activation(E1[:, m, 0:HN], out_of(b)[:, 0:HN], ACT.Relu, bias=b1e[:, m:m + 1]).then_inc(free[b], 1)
                    else:
                        skip(full, [b])
                g2.want(act)
                act.activation(t_gap_e, t_gap, ACT.Exp).then_inc(s_g2e, 1)
                for h, b in enumerate(T_S2):
                    act.activation(S2[:, h * HN:(h + 1) * HN], out_of(b)[:, 0:HN], ACT.Relu, bias=b2s).then_inc(free[b], 1)
                skip(full, T_E2 + T_W + T_O)

            run_turns(act, NG, stage5, full + [gx, g2])

        @block.tensor
        def _(pe):
            full, free = s_full, [Tally(s) for s in s_free]
            mm = pe.matmul

            def into(b, g=0):
                free[b].again(pe)
                free[b].n += 1
                return bank[b]

            def read_out(plan):
                for b in sorted(set(plan)):
                    free[b].again(pe)

            def product(b, cols, pairs, parts=P):
                ps = into(b)[0:parts, 0:cols]
                for n, (w, m) in enumerate(pairs):
                    last = mm(ps, w, m, start=n == 0, stop=n == len(pairs) - 1)
                last.then_inc(full[b], 1)

            def transposes(plan, rows):
                for k in range(KC):
                    ps = into(plan[k])
                    for j in range(GB - 1):
                        last = pe.transpose(ps[:, j * P:(j + 1) * P], rows[:, j, k * P:(k + 1) * P], ident[:, :])
                    last.then_inc(full[plan[k]], 1)
                ps = into(plan[2])
                for k in range(KC):
                    last = pe.transpose(ps[:, k * P:(k + 1) * P], rows[:, GB - 1, k * P:(k + 1) * P], ident[:, :])
                last.then_inc(full[plan[2]], 1)

            pe.wait_ge(s_const, 1)
            pe.wait_ge(s_edges, 16 * 12)
            pe.wait_ge(s_eflt, 1)
            for a in range(4):
                ps = into(a)
                for q in range(3):
                    pe.transpose(ps[:, q * P:(q + 1) * P], EF[:, a, q, :], ident[:, :])
                r = EC - 3 * P
                pe.transpose(ps[:, 3 * P:EC], EF[0:r, a, 3, :], ident[0:r, 0:r]).then_inc(full[a], 1)
            K = NB + 1
            for n in range(2):
                pe.wait_ge(s_cnt, 4 * n + 1)
                product(4, K, [(upper[:, :], cnt[:, 0:K])])
                product(5, K + 1, [(onesm[:, :], cnt)])
                pe.wait_ge(s_cnt, 4 * n + 2)
                product(6, 1, [(upper[0:K, 0:K], colw[0:K, 3:4])], parts=K)
                pe.wait_ge(s_cnt, 4 * n + 3)
                product(7, 1, [(diffm[:, :], colw[0:K, 5:6])], parts=K)
                pe.wait_ge(s_cnt, 4 * n + 4)
                product(6, STEPS, [(ddrep, GT)])
                product(7, STEPS, [(onesm[0:K, :], GT)])

            xnr, xnnr = Tally(s_xnr), Tally(s_xnnr)
            pe.wait_ge(s_w1, 16 * FIRST_LOADS)

            def stage1(g):
                xnr.want(pe)
                transposes(B_XN, XNR)
                xnnr.want(pe)
                transposes(B_XNN, XNNR)
                read_out(B_XNN)
                for h, b in enumerate(B_HG):
                    product(b, HN, [(Wg1s[:, k, :], XNT[:, k, h * HN:(h + 1) * HN]) for k in range(KC)], parts=GH)
                read_out(B_XN)
                for first_col, plan in ((C, B_K), (2 * C, B_V)):
                    for q, b in enumerate(plan):
                        ps = into(b)
                        for j in range(2 * q, min(2 * q + 2, GB)):
                            for k in range(KC):
                                last = mm(ps[:, (j % 2) * C:(j % 2 + 1) * C], XTR[:, k, j * P:(j + 1) * P],
                                          Wq[:, k, first_col:first_col + C], start=k == 0, stop=k == KC - 1)
                        last.then_inc(full[b], 1)
                read_out(B_HG)
                for q, b in enumerate(B_G):
                    m, h = divmod(q, 2)
                    product(b, HN, [(Wg2s[0:GH, m * P:(m + 1) * P], HG[0:GH, h * HN:(h + 1) * HN])])

            run_turns(pe, NG, stage1, free + [xnr, xnnr])

            pe.wait_ge(s_kmax, 1)
            ps = into(2)
            for k in range(KC):
                last = pe.transpose(ps[:, k * P:(k + 1) * P], KMAX[:, k * P:(k + 1) * P], ident[:, :])
            last.then_inc(full[2], 1)
            pe.wait_ge(s_kmax, 2)
            ps = into(3)
            for k in range(KC):
                last = mm(ps[:, k * P:(k + 1) * P], onesm[:, :], CTX[:, k, :], start=True, stop=True)
            last.then_inc(full[3], 1)
            pe.wait_ge(s_kexp, 1)
            read_out(B_V)
            pe.wait_ge(s_vrow, 1)
            for m in range(KC):
                product(4 + m, P + 1, [(KROW[:, b, m * P:(m + 1) * P], VROW[:, b, m, :]) for b in range(NB)])

            ht = Tally(s_ht)

            def stage3(g):
                for q, b in enumerate(B_Q):
                    m, h = divmod(q, 2)
                    product(b, HN, [(Wq[:, k, m * P:(m + 1) * P], XH[:, k, ds(g * GN + h * HN, HN)]) for k in range(KC)])
                ht.want(pe)
                for j, b in enumerate(B_F):
                    product(b, 2 * C, [(HT[:, k, j * P:(j + 1) * P], Wio[:, k, :]) for k in range(KC)])
                read_out(B_Q)
                for q, b in enumerate(B_O):
                    m, h = divmod(q, 2)
                    product(b, HN, [(CTX[:, m, :], QT[:, m, h * HN:(h + 1) * HN])])

            pe.wait_ge(s_xh, NG)
            read_out([4, 5])
            run_turns(pe, NG, stage3, free + [ht])
            read_out(range(8))

            for d in GATHER_ORDER:
                got, onehot = [Tally(s) for s in s_g[d]], Tally(s_m[d])
                if d == GATHER_ORDER[1]:
                    pe.wait_ge(s_add[GATHER_ORDER[0]], STEPS)

                def multiply_turn(i, d=d, got=got, onehot=onehot):
                    for j in range(GR):
                        if j % 4 == 0:
                            got[j // 4].want(pe, 16 * 4)
                        onehot.want(pe)
                        if not static(i) or j >= 8:
                            pe.wait_ge(s_add[d], i * GR + (j - 7))
                        ps = bank[j % 8]
                        for k in range(KC):
                            last = mm(ps[:, k * P:(k + 1) * P], GATH[:, j, k * P:(k + 1) * P], ONEHOT[:, j % 8, :],
                                      start=True, stop=True)
                        last.then_inc(s_agg[d], 1)

                run_turns(pe, STEPS // GR, multiply_turn, [onehot] + got)

            gates, gnn, xn1, wg = (Tally(s) for s in (s_gates, s_gnn, s_xn1, s_wg))
            pe.wait_ge(s_w2, 16 * LAST_LOADS)
            pe.wait_ge(s_add[GATHER_ORDER[1]], STEPS)
            pe.wait_ge(s_hk, NG)

            def stage5(g):
                def seg(t, k, h):
                    return t[:, k, ds(g * GN + h * HN, HN)]

                for q, b in enumerate(T_X):
                    m, h = divmod(q, 2)
                    cols = slice(m * P, (m + 1) * P)
                    product(b, HN, [(Wx[:, 2 * s + k, cols], seg(t, k, h))
                                    for s, t in enumerate((AGG[0], AGG[1], XH)) for k in range(KC)])
                gates.want(pe)
                gnn.want(pe)
                for j, b in enumerate(T_R):
                    ps = into(b)
                    for k in range(KC):
                        mm(ps[:, 0:C], OGR[:, k, j * P:(j + 1) * P], Wp[:, k, :], start=k == 0, stop=False)
                    for k in range(KC):
                        last = mm(ps[:, k * P:(k + 1) * P], GNN[:, k, j * P:(j + 1) * P], ident[:, :],
                                  start=False, stop=k == KC - 1)
                    last.then_inc(full[b], 1)
                xn1.want(pe)
                transposes(T_T, XN1)
                read_out(T_T)
                ps = into(T_L[0])
                for j in range(GB):
                    for k in range(KC):
                        last = mm(ps[:, j * NEXP:(j + 1) * NEXP], XT1[:, k, j * P:(j + 1) * P], Wgate[:, k, :],
                                  start=k == 0, stop=k == KC - 1)
                last.then_inc(full[T_L[0]], 1)
                for q, b in enumerate(T_S1):
                    m, h = divmod(q, 2)
                    product(b, HN, [(W1s[:, k, m * P:(m + 1) * P], XT1[:, k, h * HN:(h + 1) * HN]) for k in range(KC)])
                for q, b in enumerate(T_E1):
                    m, h = divmod(q, 2)
                    product(b, HN, [(W1e[:, k, m, :], XT1[:, k, h * HN:(h + 1) * HN]) for k in range(KC)])
                read_out(T_S1)
                for h, b in enumerate(T_S2):
                    product(b, HN, [(W2s[:, k, :], S1[:, k, h * HN:(h + 1) * HN]) for k in range(2)])
                read_out(T_E1[3:])
                for q, b in enumerate(T_E2):
                    m, h = divmod(q, 2)
                    ps = into(b)
                    for e in range(2):
                        last = mm(ps[e * EH2:(e + 1) * EH2, 0:HN], W2e[:, 2 * m + e, :],
                                  E1[:, 2 * m + e, h * HN:(h + 1) * HN], start=True, stop=True)
                    last.then_inc(full[b], 1)
                wg.want(pe)
                transposes(T_W[0:3], WGX.rearrange("p j m c -> p j (m c)"))
                for b, js in ((T_W[3], range(GB - 1)), (T_W[4], range(GB - 1, GB))):
                    ps = into(b)
                    for n, j in enumerate(js):
                        last = pe.transpose(ps[0:NEXP + 1, n * P:(n + 1) * P], t_w5[:, j, :], ident[:, :])
                    last.then_inc(full[b], 1)
                read_out(T_S2 + T_E2 + T_W)
                for j, b in enumerate(T_O):
                    n = slice(j * P, (j + 1) * P)
                    product(b, C, [(S2[:, n], W3s), (E2[:, 0, n], W3e[:, 0, :]), (E2[:, 1, n], W3e[:, 1, :]),
                                   (WGT[0:NEXP + 1, n], B3[0:NEXP + 1, :])])

            run_turns(pe, NG, stage5, free + [gates, gnn, xn1, wg])

        @block.vector
        def _(dve):
            full, free = [Tally(s) for s in s_full], s_free
            steps = Tally(s_dve)
            v = nc.vector

            def link(ins):
                steps.link(dve, ins)

            def out_of(b):
                full[b].want(dve)
                return bank[b]

            def landed(b):
                dve.wait_ge(free[b], full[b].value())

            def flat(t3):
                return t3.rearrange("p a c -> p (a c)")

            def row_stats(st, m, va, a, c):
                v.tensor_tensor(a, st[:, :, 1], st[:, :, 4], ALU.subtract)
                v.tensor_tensor(c, st[:, :, 2], st[:, :, 5], ALU.add)
                link(v.tensor_tensor(m, st[:, :, 1], st[:, :, 4], ALU.add))
                v.tensor_scalar(m, m, 0.5, None, ALU.mult)
                link(v.scalar_tensor_tensor(a, a, 0.25, a, ALU.mult, ALU.mult))
                link(v.scalar_tensor_tensor(va, c, 1.0 / C, a, ALU.mult, ALU.add))

            v.memset(EI[:, :, 3, :], NP - 1)
            v.memset(SEQ[1], NP - 1)
            v.memset(EF[:, 2:4, 3, :], 0.0).then_inc(s_pad, 1)
            v.memset(XROW[:, NB - 1, :], 0.0).then_inc(s_xz, 1)
            v.memset(ZERO, 0.0)
            v.memset(cnt[:, NB:NB + 2], 0.0)
            dve.wait_ge(s_edges, 16 * 12)
            v.tensor_copy(EF[:, 0:2, :, :], EI[:, :, :, :]).then_inc(s_eflt, 1)
            ps = out_of(0)
            v.tensor_copy(REC[0][:, :, 0], ps[:, 0:EC])
            v.tensor_copy(REC[1][:, :, 1], ps[:, 0:EC]).then_inc(free[0], 1)
            ps = out_of(1)
            v.tensor_copy(REC[0][:, :, 1], ps[:, 0:EC])
            v.tensor_copy(REC[1][:, :, 0], ps[:, 0:EC]).then_inc(free[1], 1)
            v.tensor_copy(REC[0][:, :, 2], out_of(2)[:, 0:EC]).then_inc(free[2], 1)
            v.tensor_copy(REC[1][:, :, 2], out_of(3)[:, 0:EC]).then_inc(free[3], 1)
            landed(3)

            dve.wait_ge(s_const, 1)
            def places(d, link):
                for b in range(NB):
                    s = SCAN[b % 2]
                    link(v.tensor_tensor_scan(s, ONEB[:, b, :], ZERO, base[:, b:b + 1], ALU.add, ALU.add))
                    link(v.tensor_tensor(s, s, ONEB[:, b, :], ALU.mult))
                    link(v.tensor_tensor(SLOT, SLOT, s, ALU.add))
                link(v.tensor_copy(KEYI, SLOT))
                v.tensor_scalar(LOI, KEYI, P - 1, None, ALU.bitwise_and)
                link(v.tensor_scalar(HII, KEYI, 7, None, ALU.arith_shift_right))
                v.scalar_tensor_tensor(ADDR[d][:, :], LOI, float(EC), HII, ALU.mult, ALU.add).then_inc(s_addr[d], 1)

            dve.wait_ge(s_seq, 48)
            link(v.tensor_tensor(FALL, SEQ[0], SEQ[1], ALU.is_gt))
            link(v.tensor_reduce(cnt[0:E // SQ, NB + 1:NB + 2], FALL, AX.X, ALU.add))
            K = NB + 1
            for d in SORT_ORDER:
                link(v.tensor_copy(KEYI, REC[d][:, :, 1]))
                link(v.tensor_scalar(KEYI, KEYI, 7, None, ALU.arith_shift_right))
                link(v.tensor_copy(KEYB, KEYI))
                for b in range(NB):
                    last = v.tensor_scalar(ONEB[:, b, :], KEYB, float(b), None, ALU.is_equal, ALU.add,
                                           accum_out=cnt[:, b:b + 1])
                last.then_inc(s_cnt, 1)
                v.memset(SLOT, 0.0)
                before, tot = out_of(4), out_of(5)
                link(v.tensor_copy(total, tot[:, 0:K]))
                if d == 0:
                    v.tensor_copy(unsorted[:, :], tot[0:1, K:K + 1]).then_inc(s_flag, 1)
                    dve.wait_ge(s_flag, 1)
                dve.sem_inc(free[5], 1)
                link(v.tensor_tensor_scan(incl, total, zero_f, 0.0, ALU.add, ALU.add))
                link(v.tensor_tensor(total, incl, total, ALU.subtract))
                v.scalar_tensor_tensor(base, total, -1.0, before[:, 0:K], ALU.add, ALU.add).then_inc(free[4], 1)
                link(v.memset(colw, 0.0))
                landed(4)
                if d == 1:
                    places(d, link)
                else:
                    falls = dve.value_load(unsorted[0:1, 0:1], min_val=0, max_val=E)
                    with dve.If(falls > 0):
                        rank = Tally(s_rank)
                        places(d, lambda ins: rank.link(dve, ins))

                v.tensor_tensor(SCAN[0][0:K, 0:K], total[0:K, :], ident[0:K, 0:K], ALU.mult)
                link(v.tensor_tensor(SCAN[1][0:K, 0:K], incl[0:K, :], ident[0:K, 0:K], ALU.mult))
                v.tensor_reduce(colw[0:K, 0:1], SCAN[0][0:K, 0:K], AX.X, ALU.add)
                link(v.tensor_reduce(colw[0:K, 1:2], SCAN[1][0:K, 0:K], AX.X, ALU.add))
                v.tensor_copy(coli[0:K, 0:1], colw[0:K, 0:1])
                link(v.tensor_scalar(coli[0:K, 1:2], colw[0:K, 1:2], float(P - 1), None, ALU.add))
                link(v.tensor_scalar(coli[0:K, 0:2], coli[0:K, 0:2], 7, None, ALU.arith_shift_right))
                link(v.tensor_copy(colw[0:K, 1:3], coli[0:K, 0:2]))
                v.tensor_tensor(colw[0:K, 3:4], colw[0:K, 2:3], colw[0:K, 1:2], ALU.subtract).then_inc(s_cnt, 1)
                ps = out_of(6)
                link(v.tensor_copy(colw[0:K, 4:5], ps[0:K, 0:1]))
                dve.sem_inc(free[6], 1)
                v.tensor_tensor(colw[0:K, 5:6], colw[0:K, 1:2], colw[0:K, 4:5], ALU.subtract).then_inc(s_cnt, 1)
                ps = out_of(7)
                v.tensor_scalar(ddrep, onesm[0:K, :], ps[0:K, 0:1], None, ALU.mult).then_inc(free[7], 1)
                v.tensor_scalar(GT, steps_ramp[0:K, :], colw[0:K, 4:5], None, ALU.is_ge).then_inc(s_cnt, 1)
                ps = out_of(6)
                v.tensor_tensor(GTMP, ps[0:1, 0:STEPS], steps_ramp[0:1, :], ALU.add).then_inc(free[6], 1)
                ps = out_of(7)
                v.tensor_scalar(step_off[d][:, :], ps[:, 0:STEPS], float(P), float(-P), ALU.mult, ALU.add).then_inc(free[7], 1)
                landed(6)
                landed(7)
                link(v.tensor_scalar(GTMP, GTMP, float(EC - 1), 0.0, ALU.min, ALU.max))
                v.tensor_copy(tile_no[0:1, d, :], GTMP)
                v.tensor_scalar(acc_col[0:1, d, :], step_off[d][0:1, :], float((NB - 1) * P), None, ALU.min).then_inc(s_list[d], 1)

            dve.wait_ge(s_x, 32)
            for n in range(2):
                with dve.Fori(0, NB) as b:
                    v.bn_stats(stats[:, ds(b, 1), :].rearrange("p a s -> p (a s)"), XROW[:, ds(b, 1), :].rearrange("p a c -> p (a c)"))
                link(dve.drain())
                row_stats(stats, mean, var, ws1, ws2)
                dve.sem_inc(s_var, 1)
                dve.wait_ge(s_sd, n + 1)
                link(v.reciprocal(rstd, rstd))
                if n == 0:
                    with dve.Fori(0, NB) as b:
                        v.tensor_scalar(XROW[:, ds(b, 1), :].rearrange("p a c -> p (a c)"),
                                        XROW[:, ds(b, 1), :].rearrange("p a c -> p (a c)"),
                                        mean[:, ds(b, 1)], rstd[:, ds(b, 1)], ALU.subtract, ALU.mult)
                    link(dve.drain())
                dve.sem_inc(s_xn, 1)

            dve.wait_ge(s_w1, 16 * FIRST_LOADS)
            v.tensor_scalar(bg2_h, bg2_c, 0.5, None, ALU.mult)
            for k in range(KC):
                v.tensor_scalar(VROW[:, :, k, P], padneg, 0.0, None, ALU.is_ge)
            v.memset(KMAX[:, :], FAR).then_inc(s_vrow, 1)
            dve.wait_ge(s_vrow, 1)
            dve.sem_inc(s_xn, 1)

            def stage1(g):
                skip(full, B_XN)
                for j in range(GB):
                    b = ds(g * GB + j, 1)
                    last = v.tensor_scalar(XNNR[:, j, :], XROW[:, b, :].rearrange("p a c -> p (a c)"), mean[:, b], rstd[:, b],
                                           ALU.subtract, ALU.mult)
                last.then_inc(s_xnnr, 1)
                for k in range(KC):
                    v.tensor_scalar(XNT[:, k, 0:GN - P], out_of(B_XNN[k])[:, 0:GN - P], lng_c[:, k:k + 1], lnb_c[:, k:k + 1],
                                    ALU.mult, ALU.add).then_inc(free[B_XNN[k]], 1)
                ps = out_of(B_XNN[2])
                for k in range(KC):
                    last = v.tensor_scalar(XNT[:, k, GN - P:GN], ps[:, k * P:(k + 1) * P], lng_c[:, k:k + 1], lnb_c[:, k:k + 1],
                                           ALU.mult, ALU.add)
                last.then_inc(free[B_XNN[2]], 1)
                skip(full, B_HG)
                for q, b in enumerate(B_K):
                    ps = out_of(b)
                    n = min(2, GB - 2 * q)
                    for j in range(n):
                        blk = ds(g * GB + 2 * q + j, 1)
                        v.tensor_scalar(KROW[:, blk, :].rearrange("p a c -> p (a c)"), ps[:, j * C:(j + 1) * C],
                                        padneg[:, blk], None, ALU.add)
                        last = v.scalar_tensor_tensor(KMAX[:, :], ps[:, j * C:(j + 1) * C], padneg[:, blk], KMAX[:, :],
                                                      ALU.add, ALU.max)
                        if j < n - 1:
                            link(last)
                    last.then_inc(free[b], 1)
                    landed(b)

                skip(full, B_V + B_G)

            run_turns(dve, NG, stage1, full + [steps])

            link(dve.drain())
            dve.wait_ge(s_xh, NG)
            for k in range(KC):
                width = -(-N // 7)
                for n in range(7):
                    v.bn_stats(cs[:, n, :], XH[:, k, n * width:min(N, (n + 1) * width)])
                link(dve.drain())
                link(v.bn_aggr(bnmv[:, k, :], cs))
            dve.sem_inc(s_var, 1)
            dve.sem_inc(s_kmax, 1)
            ps = out_of(2)
            link(v.tensor_reduce(rsum, ps[:, 0:KC * P].rearrange("p (k n) -> p k n", k=KC), AX.X, ALU.max))
            dve.sem_inc(free[2], 1)
            for k in range(KC):
                last = v.tensor_scalar(CTX[:, k, :], ident[:, :], rsum[:, k:k + 1], None, ALU.mult)
            last.then_inc(s_kmax, 1)
            ps = out_of(3)
            link(v.tensor_copy(KMAX[:, :], ps[:, 0:C]))
            dve.sem_inc(free[3], 1)
            v.tensor_tensor(KROW, KROW, KMAX[:, :].unsqueeze(1).to_broadcast([P, NB, C]), ALU.subtract).then_inc(s_kshift, 1)
            dve.wait_ge(s_sd, 3)
            link(v.reciprocal(h_scale, h_scale))
            link(v.tensor_tensor(h_scale, h_scale, gamma_c, ALU.mult))
            link(v.tensor_tensor(h_shift, bnmv[:, :, 0], h_scale, ALU.mult))
            link(v.tensor_tensor(h_shift, beta_c, h_shift, ALU.subtract))
            for m in range(KC):
                ps = out_of(4 + m)
                link(v.reciprocal(rsum[:, m:m + 1], ps[:, P:P + 1]))
                v.scalar_tensor_tensor(CTX[:, m, :], ps[:, 0:P], rsum[:, m:m + 1], headm[:, :],
                                       ALU.mult, ALU.mult).then_inc(free[4 + m], 1)
            v.memset(FLAT[0], 0.0)
            link(v.memset(FLAT[1], 0.0))

            def stage3(g):
                skip(full, B_Q)
                if not static(g):
                    dve.wait_ge(s_hk, g)
                for k in range(KC):
                    last = v.tensor_scalar(HT[:, k, :], XH[:, k, ds(g * GN, GN)], h_scale[:, k:k + 1], h_shift[:, k:k + 1],
                                           ALU.mult, ALU.add)
                last.then_inc(s_ht, 1)
                if not static(g):
                    dve.wait_ge(s_tab, g * 32)
                for j, b in enumerate(B_F):
                    v.tensor_tensor(FSTAGE[:, j, :], out_of(b)[:, :], bio, ALU.add).then_inc(free[b], 1)
                dve.drain().then_inc(s_fst, 1)
                for q, b in enumerate(B_O):
                    m, h = divmod(q, 2)
                    o = OG[:, m, ds(g * GN + h * HN, HN)]
                    v.scalar_tensor_tensor(o, o, 1.0, out_of(b)[:, 0:HN], ALU.add, ALU.mult).then_inc(free[b], 1)
                dve.drain().then_inc(s_ogd, 1)

            run_turns(dve, NG, stage3, full + [steps])

            for d in GATHER_ORDER:
                picked, product, added = Tally(s_rr[d]), Tally(s_agg[d]), Tally(s_add[d])

                def add_turn(i, d=d, picked=picked, product=product, added=added):
                    for h in range(2):
                        picked.want(dve)
                        link(v.tensor_tensor(REL[:, 8 * h:8 * h + 8], RR[:, 8 * h:8 * h + 8, 1],
                                             step_off[d][:, ds(i * GR + 8 * h, 8)], ALU.subtract))
                        for j in range(8 * h, 8 * h + 8):
                            v.tensor_scalar(ONEHOT[:, j % 8, :], ramp[:, :], REL[:, j:j + 1], RR[:, j, 2:3],
                                            ALU.is_equal, ALU.mult).then_inc(s_m[d], 1)
                        for j in range(8 * h, 8 * h + 8):
                            col = dve.value_load(acc_col[0:1, d, ds(i * GR + j, 1)], min_val=0, max_val=(NB - 1) * P)
                            o = AGG[d][:, :, ds(col, P)]
                            added.again(dve)
                            product.want(dve)
                            added.made(v.tensor_tensor(o, o, bank[j % 8][:, 0:KC * P].rearrange("p (k n) -> p k n", k=KC),
                                                       ALU.add))

                run_turns(dve, STEPS // GR, add_turn, [steps, picked, product, added])

            xr, r1, gates, gexp, g2e = (Tally(s) for s in (s_xr, s_r1, s_gates, s_gexp, s_g2e))
            dve.wait_ge(s_w2, 16 * LAST_LOADS)

            def each(t2, n=NEXP):
                return t2.unsqueeze(2).to_broadcast([P, GB, n])

            def first_of(o, score, best):
                link(v.tensor_tensor(o, score, each(best), ALU.is_equal))
                link(v.tensor_tensor(o, o, pref.unsqueeze(1).to_broadcast([P, GB, NEXP]), ALU.mult))
                link(v.tensor_reduce(t_m, o, AX.X, ALU.max))
                link(v.tensor_tensor(o, o, each(t_m), ALU.is_equal))

            def stage5(g):
                skip(full, T_X)
                xr.want(dve, 32)
                link(v.tensor_tensor(X1, X1, bp_row.unsqueeze(1).to_broadcast([P, GB, C]), ALU.add))
                gates.want(dve)
                link(v.tensor_tensor(S1, XH[:, :, ds(g * GN, GN)], GNN, ALU.subtract))
                link(v.scalar_tensor_tensor(S1, IG, 1.0, S1, ALU.add, ALU.mult))
                v.scalar_tensor_tensor(GNN, S1, 0.5, GNN, ALU.mult, ALU.add).then_inc(s_gnn, 1)
                for j, b in enumerate(T_R):
                    v.tensor_tensor(X1[:, j, :], X1[:, j, :], out_of(b)[:, 0:C], ALU.add).then_inc(free[b], 1)
                    landed(b)
                    v.bn_stats(stats[:, j, :], X1[:, j, :])
                link(dve.drain())
                row_stats(stats[:, 0:GB], t_mean, t_var, t_a, t_c)
                v.tensor_scalar(t_var, t_var, EPS, None, ALU.add).then_inc(s_v1, 1)
                if not static(g):
                    dve.wait_ge(s_st, g * 32)
                r1.want(dve)
                for j in range(GB):
                    last = v.tensor_scalar(XN1[:, j, :], X1[:, j, :], t_mean[:, j:j + 1], t_rstd[:, j:j + 1],
                                           ALU.subtract, ALU.mult)
                last.then_inc(s_xn1, 1)
                skip(full, T_T)
                ps = out_of(T_L[0])
                link(v.tensor_tensor(t_log, ps[:, 0:GB * NEXP].rearrange("p (j e) -> p j e", e=NEXP),
                                     gb_row.unsqueeze(1).to_broadcast([P, GB, NEXP]), ALU.add))
                dve.sem_inc(free[T_L[0]], 1)
                link(v.tensor_reduce(t_m, t_log, AX.X, ALU.max))
                v.tensor_tensor(t_log, t_log, each(t_m), ALU.subtract).then_inc(s_gx, 1)
                gexp.want(dve)
                link(v.tensor_reduce(t_m, t_exp, AX.X, ALU.add))
                link(v.reciprocal(t_m, t_m))
                link(v.tensor_tensor(t_g, t_exp, each(t_m), ALU.mult))
                link(v.tensor_reduce(t_m1, t_g, AX.X, ALU.max))
                first_of(t_o1, t_g, t_m1)
                link(v.scalar_tensor_tensor(t_sc, t_o1, -2.0, t_g, ALU.mult, ALU.add))
                link(v.tensor_reduce(t_m2, t_sc, AX.X, ALU.max))
                v.tensor_tensor(t_gap, t_m2, t_m1, ALU.subtract).then_inc(s_g2, 1)
                skip(full, T_S1)
                for q, b in enumerate(T_E1):
                    m, h = divmod(q, 2)
                    if h == 0:
                        skip(full, [b])
                    else:
                        v.tensor_scalar(E1[:, m, HN:GN], out_of(b)[:, 0:HN], b1e[:, m:m + 1], 0.0,
                                        ALU.add, ALU.max).then_inc(free[b], 1)
                first_of(t_o2, t_sc, t_m2)
                g2e.want(dve)
                link(v.tensor_scalar(t_m, t_gap_e, 1.0, None, ALU.add))
                link(v.reciprocal(t_m, t_m))
                link(v.tensor_tensor(t_wt, t_gap_e, t_m, ALU.mult))
                v.tensor_tensor(t_o1, t_o1, each(t_m), ALU.mult)
                link(v.tensor_tensor(t_o2, t_o2, each(t_wt), ALU.mult))
                link(v.tensor_tensor(t_w5[:, :, 0:NEXP], t_o1, t_o2, ALU.add))
                for j in range(GB):
                    last = v.tensor_copy(WGX[:, j].rearrange("p m c -> p (m c)").rearrange("p (e c) -> p e c", e=NEXP),
                                         t_w5[:, j, 0:NEXP].unsqueeze(2).to_broadcast([P, NEXP, EH2]))
                last.then_inc(s_wg, 1)
                skip(full, T_S2)
                for q, b in enumerate(T_E2):
                    m, h = divmod(q, 2)
                    v.tensor_scalar(E2[:, m, h * HN:(h + 1) * HN], out_of(b)[:, 0:HN], b2e[:, m:m + 1], 0.0,
                                    ALU.add, ALU.max).then_inc(free[b], 1)
                for b in T_E2:
                    landed(b)
                for k in range(KC):
                    b = T_W[k]
                    v.tensor_tensor(E2[:, k, 0:GN - P], E2[:, k, 0:GN - P], out_of(b)[:, 0:GN - P], ALU.mult).then_inc(free[b], 1)
                b = T_W[2]
                v.tensor_tensor(E2[:, :, GN - P:GN], E2[:, :, GN - P:GN],
                                out_of(b)[:, 0:KC * P].rearrange("p (k n) -> p k n", k=KC), ALU.mult).then_inc(free[b], 1)
                for b, (lo, hi) in zip(T_W[3:], ((0, GN - P), (GN - P, GN))):
                    v.tensor_copy(WGT[0:NEXP + 1, lo:hi], out_of(b)[0:NEXP + 1, 0:hi - lo]).then_inc(free[b], 1)
                for j, b in enumerate(T_O):
                    v.tensor_tensor(OUTR[:, j, :], out_of(b)[:, 0:C], X1[:, j, :], ALU.add).then_inc(free[b], 1)
                dve.drain().then_inc(s_out, 1)

            run_turns(dve, NG, stage5, full + [steps, xr, r1, gates, gexp, g2e])


def kernel(**inputs):
    import numpy as np
    import concourse.bacc as bacc
    from concourse import mybir
    from concourse.bass_utils import run_bass_kernel_spmd

    nc = bacc.Bacc("TRN2", target_bir_lowering=False, num_devices=1)
    names = ("x src dst edge_weight edge_weight_n2 L0_gnn_gamma L0_gnn_beta L0_gnn_W_in L0_gnn_b_in L0_gnn_W_out "
             "L0_gnn_b_out L0_gnn_W_x2i L0_gnn_b_x2i L0_gnn_W_h2h L0_mix_Wqkv L0_mix_Wproj L0_mix_bproj L0_mix_ln_g "
             "L0_mix_ln_b L0_mix_Wg1 L0_mix_bg1 L0_mix_Wg2 L0_mix_bg2 L0_ffn_sW1 L0_ffn_sb1 L0_ffn_sW2 L0_ffn_sb2 "
             "L0_ffn_sW3 L0_ffn_sb3 L0_ffn_eW1 L0_ffn_eb1 L0_ffn_eW2 L0_ffn_eb2 L0_ffn_eW3 L0_ffn_eb3 L0_ffn_gW "
             "L0_ffn_gb").split()
    arrays, args = {}, []
    for name in names:
        a = np.ascontiguousarray(inputs[name])
        arrays[f"in_{name}"] = a
        args.append(nc.dram_tensor(f"in_{name}", a.shape, mybir.dt.from_np(a.dtype), kind="ExternalInput").ap())
    args.append(nc.dram_tensor("out0", (N, C), mybir.dt.float32, kind="ExternalOutput").ap())
    gps_layer(nc, *args)
    result = run_bass_kernel_spmd(nc, [arrays], core_ids=[0])
    return result.results[0]["out0"]
```

```python
import concourse.bass as bass
from concourse import mybir
from contextlib import ExitStack

N, C, E = 3125, 256, 50000
P = 128
NB = -(-N // P)
NP = NB * P
LAST = N - (NB - 1) * P
KC = C // P
GB = 5
NG = NB // GB
GN = GB * P
HN = GN // 2
EC = -(-E // P)
STEPS = EC + NB
NEXP, EH1, EH2 = 4, 128, 64
GH = C // 4
HEADS, HD = 8, 32
FS = 23
FS_A = 12
SQ = 400
EPS = 1e-5
FAR = -1e30
FIRST_LOADS, LAST_LOADS = 13, 22
TURN = 32
UNITS = 10
SORT_ORDER = (1, 0)
GATHER_ORDER = (0, 1)


class Tally:

    def __init__(self, sem):
        self.sem, self.n, self.i, self.per = sem, 0, None, 0

    def value(self):
        return self.n if self.i is None else self.i * self.per + (self.n - self.per)

    def made(self, ins, k=1):
        ins.then_inc(self.sem, k)
        self.n += k
        return ins

    def want(self, eng, k=1):
        self.n += k
        eng.wait_ge(self.sem, self.value())

    def again(self, eng, k=0):
        if self.i is not None or self.n > k:
            eng.wait_ge(self.sem, self.value() - k if k else self.value())

    def link(self, eng, ins):
        self.made(ins)
        eng.wait_ge(self.sem, self.value())


def run_turns(eng, turns, body, tallies):
    before = [t.n for t in tallies]
    body(0)
    pers = [t.n - n for t, n in zip(tallies, before)]
    with eng.Fori(1, turns) as i:
        starts = [t.n for t in tallies]
        for t, per in zip(tallies, pers):
            t.i, t.per = i, per
        body(i)
        for t, per, n in zip(tallies, pers, starts):
            assert t.n - n == per
            t.i = None
    for t, per in zip(tallies, pers):
        t.n += per * (turns - 2)


def gps_layer(nc, x, src, dst, ew_in, ew_out, gamma, beta, W_in, b_in, W_out, b_out, W_x2i, b_x2i,
              W_h2h, Wqkv, Wproj, bproj, ln_g, ln_b, Wg1, bg1, Wg2, bg2, sW1, sb1, sW2, sb2, sW3,
              sb3, eW1, eb1, eW2, eb2, eW3, eb3, gW, gb, out):
    f32, i32, bf16 = mybir.dt.float32, mybir.dt.int32, mybir.dt.bfloat16
    ALU, ACT, AX = mybir.AluOpType, mybir.ActivationFunctionType, mybir.AxisListType
    On = bass.IndirectOffsetOnAxis
    ds = bass.ds
    ctx = ExitStack()
    with ctx:
        def sb(name, shape, dt=f32):
            return ctx.enter_context(nc.sbuf_tensor(name, shape, dt))

        def sem(name):
            return ctx.enter_context(nc.semaphore(name))

        rec_dram = [nc.dram_tensor(f"rec_{d}", (P * EC, 3), f32, kind="Internal").ap() for d in ("to_dst", "to_src")]
        h_dram = nc.dram_tensor("h_kept", (NG, P, KC * GN), f32, kind="Internal").ap()
        table = [nc.dram_tensor(f"table_{d}", (NP, C), f32, kind="Internal").ap() for d in ("in", "out")]

        XH = sb("XH", [P, KC, NP])
        OG = sb("OG", [P, KC, NP])
        AGG = [sb("AGG_in", [P, KC, NP]), sb("AGG_out", [P, KC, NP + NB])]
        FLAT = [a[:, :, :].rearrange("p k n -> p (k n)") for a in AGG]
        KROW = FLAT[0].rearrange("p (b c) -> p b c", b=NB)
        VROW = FLAT[1].rearrange("p (b k c) -> p b k c", b=NB, k=KC)
        ident = sb("ident", [P, P])
        ramp = sb("ramp", [P, P])
        steps_ramp = sb("steps_ramp", [P, STEPS])
        edge_work = sb("edge_work", [P, 2 * (4 * EC + STEPS)])
        REC = [edge_work[:, o:o + 3 * EC].rearrange("p (c w) -> p c w", w=3) for o in (0, 3 * EC)]
        ADDR = [edge_work[:, o:o + EC].bitcast(i32) for o in (6 * EC, 7 * EC)]
        step_off = [edge_work[:, o:o + STEPS] for o in (8 * EC, 8 * EC + STEPS)]
        unsorted = sb("unsorted", [1, 1], i32)
        tile_no = sb("tile_no", [1, 2, STEPS], i32)
        acc_col = sb("acc_col", [1, 2, STEPS], i32)
        SREC = sb("SREC", [P, FS, 3])
        SADR = sb("SADR", [P, FS], i32)
        small = sb("small", [P, 900])
        upper = sb("upper", [P, P])
        onesm = sb("onesm", [P, P])
        diffm = sb("diffm", [NB + 1, NB + 1])
        headm = sb("headm", [P, P])
        CTX = sb("CTX", [P, KC, P])
        KMAX = sb("KMAX", [P, C])

        RSIZE = 19000
        R = sb("region", [P, RSIZE])

        def cutter(*spans):
            state = [list(s) for s in spans]

            def cut(*shape):
                size = 1
                for n in shape:
                    size *= n
                for s in state:
                    if s[0] + size <= s[1]:
                        v = R[:, s[0]:s[0] + size]
                        s[0] += size
                        if len(shape) == 2:
                            v = v.rearrange("p (a b) -> p a b", a=shape[0])
                        if len(shape) == 3:
                            v = v.rearrange("p (a b c) -> p a b c", a=shape[0], b=shape[1])
                        return v
                raise ValueError(shape)
            return cut

        cut = cutter((0, RSIZE))
        XROW = cut(NB, C)
        Wq = cut(KC, 3 * C)
        Wg1s = cut(KC, GH)
        Wg2s = cut(C)
        Wio = cut(KC, 2 * C)
        bio = cut(2 * C)
        XNR = cut(GB, C)
        XNNR = cut(GB, C)
        XTR = cut(KC, GN)
        XNT = cut(KC, GN)
        HG = cut(GN)
        QT = XNR.rearrange("p a b -> p (a b)").rearrange("p (k n) -> p k n", k=KC)
        HT = XNNR.rearrange("p a b -> p (a b)").rearrange("p (k n) -> p k n", k=KC)
        cut = cutter((0, NB * C))
        FSTAGE = cut(GB, 2 * C)
        LW = 9400
        cut = cutter((0, LW))
        GATH = cut(TURN, C)
        ONEHOT = cut(8, P)
        RR = cut(TURN, 3)
        REL = cut(TURN)
        IR = cut(TURN).bitcast(i32)
        cut = cutter((LW, LW + 6700))
        Wx = cut(6, 2 * C)
        Wp = cut(KC, C)
        W1s = cut(KC, 256)
        W2s = cut(2, 128)
        W3s = cut(C)
        W1e = cut(KC, NEXP, EH1)
        W2e = cut(NEXP, EH2)
        W3e = cut(2, C)
        B3 = cut(C)
        Wgate = cut(KC, NEXP)
        gb_row = cut(NEXP)
        bx = cut(4)
        bp = cut(KC)
        b1s = cut(2)
        b2s = cut(1)
        b1e = cut(NEXP)
        b2e = cut(2)
        cut = cutter((0, LW), (LW + 6700, RSIZE))
        E1 = cut(NEXP, GN)
        GNN = cut(KC, GN)
        X1 = cut(GB, C)
        XN1 = cut(GB, C)
        OUTR = XN1
        XT1 = cut(KC, GN)
        WGX = XT1.rearrange("p k n -> p (k n)").rearrange("p (j m c) -> p j m c", j=GB, m=2)
        S1 = cut(2, GN)
        S2 = cut(GN)
        E2 = cut(2, GN)
        WGT = cut(GN)
        IG, HB = (edge_work[:, o * GN:(o + 2) * GN].rearrange("p (k n) -> p k n", k=KC) for o in (0, 2))
        XL = edge_work[:, 4 * GN:6 * GN].rearrange("p (j c) -> p j c", j=GB)

        ONEB = FLAT[0][:, 0:(NB * EC + 1) // 2].bitcast(bf16)[:, 0:NB * EC].rearrange("p (b c) -> p b c", b=NB)
        GT = FLAT[0][0:NB + 1, 4900:4900 + STEPS]
        ddrep = FLAT[0][0:NB + 1, 5400:5400 + P]
        GTMP = FLAT[0][0:1, 5600:5600 + STEPS]
        EF = FLAT[1][:, 0:2048].rearrange("p (a b c) -> p a b c", a=4, b=4)
        EI = FLAT[1].bitcast(i32)[:, 2048:3072].rearrange("p (a b c) -> p a b c", a=2, b=4)
        KEYI, LOI, HII = (FLAT[1].bitcast(i32)[:, o:o + EC] for o in (3072, 5472, 5872))
        KEYB, ZERO, SLOT = (FLAT[1][:, o:o + EC] for o in (3472, 3872, 5072))
        SCAN = [FLAT[1][:, o:o + EC] for o in (4272, 4672)]

        SEQ = [XTR.rearrange("p k n -> p (k n)").bitcast(i32)[0:E // SQ, o:o + SQ] for o in (0, SQ)]

        FALL = XNT.rearrange("p k n -> p (k n)")[0:E // SQ, 0:SQ]

        at = [0]

        def few(n):
            at[0] += n
            assert at[0] <= 900
            return small[:, at[0] - n:at[0]]

        stats = few(NB * 6).rearrange("p (b s) -> p b s", s=6)
        mean, var, rstd, ws1, ws2 = few(NB), few(NB), few(NB), few(NB), few(NB)
        padneg, eps_col = few(NB), few(1)
        cnt = few(NB + 2)
        total, incl, base, zero_f = (few(NB + 1) for _ in range(4))
        colw = few(8)
        coli = few(2).bitcast(i32)
        gamma_c, beta_c, lng_c, lnb_c = few(KC), few(KC), few(KC), few(KC)
        bg1_c, bg2_c, bg2_h = few(1), few(KC), few(KC)
        h_scale, h_shift, rsum = few(KC), few(KC), few(KC)
        cs = few(7 * 6).rearrange("p (b s) -> p b s", s=6)
        bnmv = few(KC * 2).rearrange("p (k s) -> p k s", s=2)
        neghalf = few(GB)
        pref = few(NEXP)
        t_log, t_exp, t_g, t_sc, t_o1, t_o2, t_w = (few(GB * NEXP).rearrange("p (j e) -> p j e", e=NEXP) for _ in range(7))
        t_w5 = few(GB * (NEXP + 1)).rearrange("p (j e) -> p j e", e=NEXP + 1)
        t_m, t_m1, t_m2, t_gap, t_gap_e, t_wt = (few(GB) for _ in range(6))
        t_mean, t_var, t_rstd, t_a, t_c = (few(GB) for _ in range(5))

        bank = [ctx.enter_context(nc.psum_tensor(f"bank{b}", [P, 512], f32)) for b in range(8)]

        s_full = [sem(f"bank_full{b}") for b in range(8)]
        s_free = [sem(f"bank_free{b}") for b in range(8)]
        both = ("in", "out")
        s_const = sem("constants_ready")
        s_pad = sem("edge_pads_set")
        s_xz = sem("x_pad_zeroed")
        s_edges = sem("edges_loaded")
        s_eflt = sem("edges_float")
        s_seq = sem("dst_sequence_loaded")
        s_flag = sem("unsorted_known")
        s_rank = sem("in_rank_steps")
        s_x = sem("x_loaded")
        s_w1 = sem("first_weights_loaded")
        s_w2 = sem("last_weights_loaded")
        s_cnt = sem("counts_ready")
        s_list = [sem(f"work_list_ready_{d}") for d in both]
        s_addr = [sem(f"places_ready_{d}") for d in both]
        s_copied = [sem(f"records_staged_{d}") for d in both]
        s_scat = [[sem(f"scattered_{d}{h}") for h in "ab"] for d in both]
        s_rel = [sem(f"ordered_{d}") for d in both]
        s_gp = sem("gpsimd_steps")
        s_dve = sem("vector_steps")
        s_act = sem("scalar_steps")
        s_apart = sem("standalone_waits")
        s_var = sem("variances_ready")
        s_sd = sem("deviations_ready")
        s_xn = sem("xn_ready")
        s_xnr = sem("xn_rows_staged")
        s_xnnr = sem("xnn_rows_staged")
        s_xh = sem("xn_kept")
        s_kmax = sem("kmax_ready")
        s_kshift = sem("k_shifted")
        s_kexp = sem("k_exp_done")
        s_vrow = sem("v_rows_done")
        s_ht = sem("h_group_ready")
        s_hk = sem("h_kept")
        s_hs = sem("h_stored")
        s_ogd = sem("gated_output_done")
        s_fst = sem("table_rows_staged")
        s_tab = sem("table_written")
        s_g = [[sem(f"gathered_{d}{k}") for k in range(TURN // 4)] for d in both]
        s_rr = [sem(f"step_records_{d}") for d in both]
        s_ri = [sem(f"step_rows_{d}") for d in both]
        s_m = [sem(f"onehot_{d}") for d in both]
        s_agg = [sem(f"tile_multiplied_{d}") for d in both]
        s_add = [sem(f"tile_added_{d}") for d in both]
        s_gates = sem("gates_ready")
        s_gnn = sem("gnn_ready")
        s_xr = sem("x_rows_back")
        s_hr = sem("h_back")
        s_v1 = sem("ffn_variance_ready")
        s_r1 = sem("ffn_rstd_ready")
        s_xn1 = sem("ffn_rows_ready")
        s_gx = sem("gate_logits_shifted")
        s_gexp = sem("gate_exp")
        s_g2 = sem("gate_gap")
        s_g2e = sem("gate_gap_exp")
        s_wg = sem("expert_weights_ready")
        s_out = sem("out_rows_ready")
        s_st = sem("out_stored")

        block = ctx.enter_context(nc.Block())

        B_XN, B_XNN, B_HG = [0, 1, 2], [3, 4, 5], [6, 7]
        B_K, B_V, B_G = [0, 1, 2], [3, 4, 5], [6, 7, 0, 1]
        B_Q, B_F, B_O = [0, 1, 2, 3], [4, 5, 6, 7, 0], [1, 2, 3, 4]
        T_X = [5, 6, 7, 0, 1, 2, 3, 4]
        T_R = [0, 1, 2, 3, 4]
        T_T = [5, 6, 7]
        T_L = [0]
        T_S1 = [1, 2, 3, 4]
        T_E1 = [5, 6, 7, 0, 1, 2, 3, 4]
        T_S2 = [5, 6]
        T_E2 = [7, 0, 1, 2]
        T_W = [3, 4, 5, 6, 7]
        T_O = [0, 1, 2, 3, 4]

        def tallies(sems):
            return [Tally(s) for s in sems]

        def skip(full, plan):
            for b in plan:
                full[b].n += 1

        def static(i):
            return isinstance(i, int)

        def at_least(eng, sem, value):
            if not static(value) or value > 0:
                eng.wait_ge(sem, value)

        def gather_turns(eng, d, turn, tallies):
            units = UNITS if d == GATHER_ORDER[1] else 0
            if units:
                run_turns(eng, units, lambda i: turn(i * TURN, i), tallies)
            run_turns(eng, STEPS // TURN - units - 1, lambda i: turn(i * TURN + units * TURN, None), tallies)
            turn(STEPS - TURN, None)

        def apart(eng, i):
            if not static(i):
                eng.sem_inc(s_apart, 1)

        def col(v, c=P):
            return v.rearrange("(k p) -> p k", p=c)

        @block.sync
        def _(sp):
            sp.wait_ge(s_pad, 1)
            for k, (a, tile) in enumerate(((src, EI[:, 0]), (dst, EI[:, 1]), (ew_in, EF[:, 2]), (ew_out, EF[:, 3]))):
                whole = P * P * 3
                rest = (E - whole) // P
                sp.dma_start(tile[:, 0:3, :], a[0:whole].rearrange("(b q r) -> q b r", b=3, q=P)).then_inc(s_edges, 16)
                sp.dma_start(tile[0:rest, 3, :], a[whole:whole + rest * P].rearrange("(q r) -> q r", r=P)).then_inc(s_edges, 16)
                sp.dma_start(tile[rest:rest + 1, 3, 0:E - whole - rest * P],
                             a[whole + rest * P:E].rearrange("(a r) -> a r", a=1)).then_inc(s_edges, 16)
            sp.dma_start(SEQ[0], dst[0:E].rearrange("(q r) -> q r", r=SQ)).then_inc(s_seq, 16)
            sp.dma_start(SEQ[1][0:E // SQ - 1, :], dst[1:E - SQ + 1].rearrange("(q r) -> q r", r=SQ)).then_inc(s_seq, 16)
            sp.dma_start(SEQ[1][E // SQ - 1:E // SQ, 0:SQ - 1], dst[E - SQ + 1:E].rearrange("(a r) -> a r", a=1)).then_inc(s_seq, 16)
            sp.wait_ge(s_xz, 1)
            sp.dma_start(XROW[:, 0:NB - 1, :], x[0:(NB - 1) * P, :].rearrange("(b p) c -> p b c", p=P)).then_inc(s_x, 16)
            sp.dma_start(XROW[0:LAST, NB - 1, :], x[(NB - 1) * P:N, :]).then_inc(s_x, 16)

            def first(dst_, src_):
                sp.dma_start(dst_, src_).then_inc(s_w1, 16)

            first(Wq, Wqkv.rearrange("(k p) n -> p k n", p=P))
            first(Wg1s, Wg1.rearrange("(k p) n -> p k n", p=P))
            first(Wg2s[0:GH, :], Wg2)
            first(Wio[:, :, 0:C], W_in.rearrange("(k p) n -> p k n", p=P))
            first(Wio[:, :, C:2 * C], W_out.rearrange("(k p) n -> p k n", p=P))
            first(bio[:, 0:C], b_in.partition_broadcast(P))
            first(bio[:, C:2 * C], b_out.partition_broadcast(P))
            with nc.allow_non_contiguous_dma("per-channel vectors, a few hundred numbers each"):
                for t, v in ((gamma_c, gamma), (beta_c, beta), (lng_c, ln_g), (lnb_c, ln_b), (bg2_c, bg2)):
                    first(t, col(v))
                first(bg1_c[0:GH, :], col(bg1, GH))

            rows = [t.rearrange("(b p) c -> p b c", p=P) for t in table]
            fst = Tally(s_fst)
            for g in range(NG):
                sp.wait_ge(s_ht, g + 1)
                sp.dma_start(h_dram[g], HT.rearrange("p k n -> p (k n)")).then_inc(s_hs, 16)
                fst.want(sp)
                for d in range(2):
                    sp.dma_start(rows[d][:, g * GB:(g + 1) * GB, :], FSTAGE[:, :, d * C:(d + 1) * C]).then_inc(s_tab, 16)

            sp.wait_ge(s_ogd, NG)
            sp.wait_ge(s_hk, NG)
            sp.wait_ge(s_hs, 16 * NG)
            n_last = [0]

            def last(dst_, src_):
                sp.dma_start(dst_, src_).then_inc(s_w2, 16)
                n_last[0] += 1

            last(Wx[:, 0:4, :], W_x2i.rearrange("(k p) n -> p k n", p=P))
            last(Wx[:, 4:6, :], W_h2h.rearrange("(k p) n -> p k n", p=P))
            last(Wp, Wproj.rearrange("(k p) n -> p k n", p=P))
            last(W1s, sW1.rearrange("(k p) n -> p k n", p=P))
            last(W2s, sW2.rearrange("(k p) n -> p k n", p=P))
            last(W3s, sW3)
            for k in range(KC):
                last(W1e[:, k], eW1[:, k * P:(k + 1) * P, :].rearrange("e p h -> p e h"))
            last(W2e, eW2.rearrange("e p g -> p e g"))
            for q in range(2):
                last(W3e[:, q, :], eW3[2 * q:2 * q + 2].rearrange("e g o -> (e g) o"))
            last(B3[0:NEXP, :], eb3)
            last(B3[NEXP:NEXP + 1, :], sb3.rearrange("(a n) -> a n", a=1))
            last(Wgate, gW.rearrange("(k p) e -> p k e", p=P))
            last(gb_row, gb.partition_broadcast(P))
            with nc.allow_non_contiguous_dma("per-channel vectors, a few hundred numbers each"):
                last(bx, col(b_x2i))
                last(bp, col(bproj))
                last(b1s, col(sb1))
                last(b2s, col(sb2))
                last(b1e, eb1.rearrange("e p -> p e"))
                for q in range(2):
                    last(b2e[:, q:q + 1], eb2[2 * q:2 * q + 2, :].rearrange("e g -> (e g)").rearrange("(p a) -> p a", a=1))
            assert n_last[0] == LAST_LOADS

            sp.wait_ge(s_scat[1][0], 16 * FS_A * (EC // FS))
            sp.wait_ge(s_scat[1][1], 16 * (FS - FS_A) * (EC // FS))
            sp.dma_start(REC[1][:, :, :], rec_dram[1].rearrange("(p c) w -> p c w", p=P)).then_inc(s_rel[1], 16)

            sp.wait_ge(s_agg[GATHER_ORDER[1]], STEPS)
            sp.wait_ge(s_add[GATHER_ORDER[1]], STEPS)

            def rows_of(g):
                b = g * GB + GB - 1
                return slice(g * GN, b * P), slice(b * P, min(N, b * P + P)), min(P, N - b * P)

            def load(g):
                full_, rest, n = rows_of(g)
                if g:
                    sp.wait_ge(s_gnn, g)
                sp.dma_start(HB, h_dram[g].rearrange("p (k n) -> p k n", k=KC)).then_inc(s_hr, 16)
                if g:
                    sp.wait_ge(s_v1, g)
                sp.dma_start(XL[:, 0:GB - 1, :], x[full_, :].rearrange("(b p) c -> p b c", p=P)).then_inc(s_xr, 16)
                sp.dma_start(XL[0:n, GB - 1, :], x[rest, :]).then_inc(s_xr, 16)

            load(0)
            for g in range(NG):
                if g < NG - 1:
                    load(g + 1)
                full_, rest, n = rows_of(g)
                sp.wait_ge(s_out, g + 1)
                sp.dma_start(out[full_, :].rearrange("(b p) c -> p b c", p=P), OUTR[:, 0:GB - 1, :]).then_inc(s_st, 16)
                sp.dma_start(out[rest, :], OUTR[0:n, GB - 1, :]).then_inc(s_st, 16)
            sp.wait_ge(s_st, 32 * NG)

        @block.gpsimd
        def _(gp):
            ch = Tally(s_gp)
            gp.iota(ramp[:, :], [[1, P]], base=0, channel_multiplier=0, allow_small_or_imprecise_dtypes=True)
            gp.iota(steps_ramp[:, :], [[1, STEPS]], base=0, channel_multiplier=0, allow_small_or_imprecise_dtypes=True)
            gp.memset(eps_col, EPS)
            gp.memset(zero_f, 0.0)
            gp.memset(ident[:, :], 0.0)
            gp.memset(upper[:, :], 1.0)
            gp.memset(diffm[:, :], 0.0)
            gp.memset(headm[:, :], 0.5)
            gp.memset(padneg, 0.0)
            gp.memset(neghalf, -0.5)
            for e in range(NEXP):
                gp.memset(pref[:, e:e + 1], float(NEXP - e))
            gp.memset(t_w5[:, :, NEXP:NEXP + 1], 1.0)
            ch.link(gp, gp.memset(onesm[:, :], 1.0))
            gp.affine_select(out=ident[:, :], in_=ident[:, :], compare_op=ALU.not_equal, fill=1.0, base=0,
                             pattern=[[-1, P]], channel_multiplier=1)
            gp.affine_select(out=upper[:, :], in_=upper[:, :], compare_op=ALU.is_gt, fill=0.0, base=0,
                             pattern=[[1, P]], channel_multiplier=-1)
            gp.affine_select(out=diffm[:, :], in_=diffm[:, :], compare_op=ALU.not_equal, fill=1.0, base=0,
                             pattern=[[-1, NB + 1]], channel_multiplier=1)
            ch.link(gp, gp.affine_select(out=headm[:, :], in_=headm[:, :], compare_op=ALU.is_ge, fill=0.0, base=0,
                                         pattern=[[-HD, P // HD], [0, HD]], channel_multiplier=1))
            gp.affine_select(out=diffm[:, :], in_=diffm[:, :], compare_op=ALU.not_equal, fill=-1.0, base=1,
                             pattern=[[-1, NB + 1]], channel_multiplier=1)
            gp.affine_select(out=headm[:, :], in_=headm[:, :], compare_op=ALU.is_gt, fill=0.0, base=HD,
                             pattern=[[HD, P // HD], [0, HD]], channel_multiplier=-1)
            gp.affine_select(out=padneg[:, NB - 1:NB], in_=padneg[:, NB - 1:NB], compare_op=ALU.is_gt, fill=FAR, base=LAST,
                             pattern=[[0, 1]], channel_multiplier=-1).then_inc(s_const, 1)

            def scatter(d):
                staged, landed = Tally(s_copied[d]), [Tally(s) for s in s_scat[d]]

                def scatter_turn(i):
                    for half, (lo, hi) in enumerate(((0, FS_A), (FS_A, FS))):
                        landed[half].again(gp)
                        apart(gp, i)
                        staged.made(gp.tensor_copy(SREC[:, lo:hi, :], REC[d][:, ds(i * FS + lo, hi - lo), :]))
                        staged.made(gp.tensor_copy(SADR[:, lo:hi], ADDR[d][:, ds(i * FS + lo, hi - lo)]))
                        staged.again(gp)
                        apart(gp, i)
                        for j in range(lo, hi):
                            landed[half].made(gp.indirect_dma_start(
                                rec_dram[d][:, :], On(ap=SADR[:, j:j + 1], axis=0), SREC[:, j, :], None), 16)

                gp.wait_ge(s_addr[d], 1)
                run_turns(gp, EC // FS, scatter_turn, [staged] + landed)

            scatter(1)
            gp.wait_ge(s_flag, 1)
            falls = gp.value_load(unsorted[0:1, 0:1], min_val=0, max_val=E)
            with gp.If(falls > 0):
                gp.wait_ge(s_scat[1][0], 16 * FS_A * (EC // FS))
                gp.wait_ge(s_scat[1][1], 16 * (FS - FS_A) * (EC // FS))
                scatter(0)
                gp.wait_ge(s_scat[0][0], 16 * FS_A * (EC // FS))
                gp.wait_ge(s_scat[0][1], 16 * (FS - FS_A) * (EC // FS))
                gp.dma_start(REC[0][:, :, :], rec_dram[0].rearrange("(p c) w -> p c w", p=P)).then_inc(s_rel[0], 16)
            with gp.If(falls < 1):
                gp.sem_inc(s_rel[0], 16)

            gp.wait_ge(s_tab, 16 * 2 * NG)
            gp.wait_ge(s_ogd, NG)
            for d in GATHER_ORDER:
                picked, landed = Tally(s_ri[d]), [Tally(s) for s in s_g[d]]

                def gather_turn(base, unit, d=d, picked=picked, landed=landed):
                    for j in range(TURN):
                        if j % 8 == 0:
                            picked.want(gp)
                            apart(gp, base)
                        landed[j // 4].made(gp.indirect_dma_start(
                            GATH[:, j, :], None, table[d][:, :], On(ap=IR[:, j:j + 1], axis=0)), 16)

                gather_turns(gp, d, gather_turn, [picked] + landed)

            v1 = Tally(s_v1)

            def rstd_turn(g):
                v1.want(gp)
                gp.tensor_tensor(t_rstd, t_var, neghalf, ALU.pow).then_inc(s_r1, 1)

            run_turns(gp, NG, rstd_turn, [v1])

        @block.scalar
        def _(act):
            full, free = [Tally(s) for s in s_full], s_free

            def out_of(b, g=0):
                full[b].want(act)
                if not static(g):
                    apart(act, g)
                return bank[b]

            def transposed(plan, o):
                for k, b in enumerate(plan[:2]):
                    act.activation(o[:, k, 0:GN - P], out_of(b)[:, 0:GN - P], ACT.Copy).then_inc(free[b], 1)
                ps = out_of(plan[2])[:, 0:KC * P].rearrange("p (k n) -> p k n", k=KC)
                act.activation(o[:, :, GN - P:GN], ps, ACT.Copy).then_inc(free[plan[2]], 1)

            act.wait_ge(s_const, 1)
            for n in range(2):
                act.wait_ge(s_var, n + 1)
                act.activation(rstd, var, ACT.Sqrt, bias=eps_col).then_inc(s_sd, 1)

            act.wait_ge(s_xn, 3)
            skip(full, [0, 1, 2, 3] + 2 * [4, 5, 6, 6, 7, 7])

            def stage1(g):
                act.activation(XNR, XROW[:, ds(g * GB, GB), :], ACT.Copy).then_inc(s_xnr, 1)
                for k, b in enumerate(B_XN[:2]):
                    ps = out_of(b, g)
                    act.activation(XH[:, k, ds(g * GN, GN - P)], ps[:, 0:GN - P], ACT.Copy)
                    act.activation(XTR[:, k, 0:GN - P], ps[:, 0:GN - P], ACT.Copy).then_inc(free[b], 1)
                ps = out_of(B_XN[2], g)[:, 0:KC * P].rearrange("p (k n) -> p k n", k=KC)
                act.activation(XH[:, :, ds(g * GN + (GN - P), P)], ps, ACT.Copy).then_inc(s_xh, 1)
                act.activation(XTR[:, :, GN - P:GN], ps, ACT.Copy).then_inc(free[B_XN[2]], 1)
                skip(full, B_XNN)
                for h, b in enumerate(B_HG):
                    act.activation(HG[0:GH, h * HN:(h + 1) * HN], out_of(b)[0:GH, 0:HN], ACT.Gelu,
                                   bias=bg1_c[0:GH, :]).then_inc(free[b], 1)
                skip(full, B_K)
                for q, b in enumerate(B_V):
                    n = min(2, GB - 2 * q)
                    ps = out_of(b, g)[:, 0:n * C].rearrange("p (b k c) -> p b k c", b=n, k=KC)
                    for j in range(n):
                        o = VROW[:, ds(g * GB + 2 * q + j, 1), :, 0:P].rearrange("p a k c -> p (a k) c")
                        last = act.activation(o, ps[:, j], ACT.Copy)
                    last.then_inc(free[b], 1)
                for q, b in enumerate(B_G):
                    m, h = divmod(q, 2)
                    act.activation(OG[:, m, ds(g * GN + h * HN, HN)], out_of(b, g)[:, 0:HN], ACT.Tanh,
                                   bias=bg2_h[:, m:m + 1], scale=0.5).then_inc(free[b], 1)

            run_turns(act, NG, stage1, full)

            act.wait_ge(s_var, 3)
            act.activation(h_scale, bnmv[:, :, 1], ACT.Sqrt, bias=eps_col).then_inc(s_sd, 1)
            act.wait_ge(s_kshift, 1)
            act.activation(KROW, KROW, ACT.Exp).then_inc(s_kexp, 1)
            skip(full, [2, 3, 4, 5])

            ht = Tally(s_ht)

            def stage3(g):
                for q, b in enumerate(B_Q):
                    m, h = divmod(q, 2)
                    act.activation(QT[:, m, h * HN:(h + 1) * HN], out_of(b)[:, 0:HN], ACT.Copy).then_inc(free[b], 1)
                skip(full, B_F + B_O)
                ht.want(act)
                apart(act, g)
                act.activation(XH[:, :, ds(g * GN, GN)], HT, ACT.Copy).then_inc(s_hk, 1)

            run_turns(act, NG, stage3, full + [ht])

            act.wait_ge(s_ogd, NG)
            for d in GATHER_ORDER:
                picked = Tally(s_rr[d])
                act.wait_ge(s_list[d], 1)
                act.wait_ge(s_rel[d], 16)

                def unit_sums(unit, ns):
                    seg = ds(unit * HN, HN)
                    for n in ns:
                        full[4 + n % 4].want(act)
                    apart(act, unit)
                    for n in ns:
                        if n < 4:
                            o, bias = (XH, AGG[0])[n // 2][:, n % 2, seg], bx[:, n:n + 1]
                        else:
                            o, bias = OG[:, n - 4, seg], bp[:, n - 4:n - 3]
                        b = 4 + n % 4
                        act.activation(o, bank[b][:, 0:HN], ACT.Identity, bias=bias).then_inc(free[b], 1)

                def pick_turn(base, unit, d=d, picked=picked):
                    for h in range(TURN // 8):
                        cols = [act.value_load(tile_no[0:1, d, ds(base + j, 1)], min_val=0, max_val=EC - 1)
                                for j in range(8 * h, 8 * h + 8)]
                        if static(base) and base == 0 and d == GATHER_ORDER[1]:
                            act.wait_ge(s_agg[GATHER_ORDER[0]], STEPS - TURN + 8 * (h + 1))
                        at_least(act, s_agg[d], base + (8 * (h + 1) - TURN))
                        apart(act, base)
                        for j, c in zip(range(8 * h, 8 * h + 8), cols):
                            last = act.activation(RR[:, j:j + 1, :], REC[d][:, ds(c, 1), :], ACT.Copy)
                        picked.made(last)
                        picked.again(act)
                        act.activation(IR[:, 8 * h:8 * h + 8], RR[:, 8 * h:8 * h + 8, 0], ACT.Copy).then_inc(s_ri[d], 1)
                        if unit is not None and h >= 2:
                            unit_sums(unit, range(4) if h == 2 else range(4, 6))

                if d == GATHER_ORDER[0]:
                    gather_turns(act, d, pick_turn, [picked])
                else:
                    act.wait_ge(s_w2, 16 * LAST_LOADS)
                    pick_turn(0, None)
                    run_turns(act, UNITS, lambda i: pick_turn(i * TURN + TURN, i), [picked] + full)
                    for t in range(UNITS + 1, STEPS // TURN):
                        pick_turn(t * TURN, None)

            gx, g2 = Tally(s_gx), Tally(s_g2)
            act.wait_ge(s_w2, 16 * LAST_LOADS)

            def gates_of_next():
                skip(full, T_X)

                def tanh():
                    for q, o, scale in ((3, IG, 0.5), (7, GNN, 1.0)):
                        act.wait_ge(free[T_X[q]], full[T_X[q]].value())
                        last = act.activation(o, o, ACT.Tanh, scale=scale)
                    last.then_inc(s_gates, 1)
                return tanh

            def stage5(g, more=True):
                skip(full, T_R)
                tanh = gates_of_next() if more else None
                transposed(T_T, XT1)
                if more:
                    tanh()
                skip(full, T_L)
                gx.want(act)
                act.activation(t_exp, t_log, ACT.Exp).then_inc(s_gexp, 1)
                for q, b in enumerate(T_S1):
                    m, h = divmod(q, 2)
                    act.activation(S1[:, m, h * HN:(h + 1) * HN], out_of(b)[:, 0:HN], ACT.Relu,
                                   bias=b1s[:, m:m + 1]).then_inc(free[b], 1)
                for q, b in enumerate(T_E1):
                    m, h = divmod(q, 2)
                    if h == 0:
                        act.activation(E1[:, m, 0:HN], out_of(b)[:, 0:HN], ACT.Relu, bias=b1e[:, m:m + 1]).then_inc(free[b], 1)
                    else:
                        skip(full, [b])
                g2.want(act)
                act.activation(t_gap_e, t_gap, ACT.Exp).then_inc(s_g2e, 1)
                for h, b in enumerate(T_S2):
                    act.activation(S2[:, h * HN:(h + 1) * HN], out_of(b)[:, 0:HN], ACT.Relu, bias=b2s).then_inc(free[b], 1)
                skip(full, T_E2 + T_W + T_O)

            gates_of_next()()
            run_turns(act, NG - 1, stage5, full + [gx, g2])
            stage5(NG - 1, more=False)

        @block.tensor
        def _(pe):
            full, free = s_full, [Tally(s) for s in s_free]
            mm = pe.matmul

            def into(b, g=0):
                free[b].again(pe)
                free[b].n += 1
                return bank[b]

            def read_out(plan):
                for b in sorted(set(plan)):
                    free[b].again(pe)

            def product(b, cols, pairs, parts=P):
                ps = into(b)[0:parts, 0:cols]
                for n, (w, m) in enumerate(pairs):
                    last = mm(ps, w, m, start=n == 0, stop=n == len(pairs) - 1)
                last.then_inc(full[b], 1)

            def transposes(plan, rows):
                for k in range(KC):
                    ps = into(plan[k])
                    for j in range(GB - 1):
                        last = pe.transpose(ps[:, j * P:(j + 1) * P], rows[:, j, k * P:(k + 1) * P], ident[:, :])
                    last.then_inc(full[plan[k]], 1)
                ps = into(plan[2])
                for k in range(KC):
                    last = pe.transpose(ps[:, k * P:(k + 1) * P], rows[:, GB - 1, k * P:(k + 1) * P], ident[:, :])
                last.then_inc(full[plan[2]], 1)

            pe.wait_ge(s_const, 1)
            pe.wait_ge(s_edges, 16 * 12)
            pe.wait_ge(s_eflt, 1)
            for a in range(4):
                ps = into(a)
                for q in range(3):
                    pe.transpose(ps[:, q * P:(q + 1) * P], EF[:, a, q, :], ident[:, :])
                r = EC - 3 * P
                pe.transpose(ps[:, 3 * P:EC], EF[0:r, a, 3, :], ident[0:r, 0:r]).then_inc(full[a], 1)
            K = NB + 1
            for n in range(2):
                pe.wait_ge(s_cnt, 4 * n + 1)
                product(4, K, [(upper[:, :], cnt[:, 0:K])])
                product(5, K + 1, [(onesm[:, :], cnt)])
                pe.wait_ge(s_cnt, 4 * n + 2)
                product(6, 1, [(upper[0:K, 0:K], colw[0:K, 3:4])], parts=K)
                pe.wait_ge(s_cnt, 4 * n + 3)
                product(7, 1, [(diffm[:, :], colw[0:K, 5:6])], parts=K)
                pe.wait_ge(s_cnt, 4 * n + 4)
                product(6, STEPS, [(ddrep, GT)])
                product(7, STEPS, [(onesm[0:K, :], GT)])

            xnr, xnnr = Tally(s_xnr), Tally(s_xnnr)
            pe.wait_ge(s_w1, 16 * FIRST_LOADS)

            def stage1(g):
                xnr.want(pe)
                transposes(B_XN, XNR)
                xnnr.want(pe)
                transposes(B_XNN, XNNR)
                read_out(B_XNN)
                for h, b in enumerate(B_HG):
                    product(b, HN, [(Wg1s[:, k, :], XNT[:, k, h * HN:(h + 1) * HN]) for k in range(KC)], parts=GH)
                read_out(B_XN)
                for first_col, plan in ((C, B_K), (2 * C, B_V)):
                    for q, b in enumerate(plan):
                        ps = into(b)
                        for j in range(2 * q, min(2 * q + 2, GB)):
                            for k in range(KC):
                                last = mm(ps[:, (j % 2) * C:(j % 2 + 1) * C], XTR[:, k, j * P:(j + 1) * P],
                                          Wq[:, k, first_col:first_col + C], start=k == 0, stop=k == KC - 1)
                        last.then_inc(full[b], 1)
                read_out(B_HG)
                for q, b in enumerate(B_G):
                    m, h = divmod(q, 2)
                    product(b, HN, [(Wg2s[0:GH, m * P:(m + 1) * P], HG[0:GH, h * HN:(h + 1) * HN])])

            run_turns(pe, NG, stage1, free + [xnr, xnnr])

            pe.wait_ge(s_kmax, 1)
            ps = into(2)
            for k in range(KC):
                last = pe.transpose(ps[:, k * P:(k + 1) * P], KMAX[:, k * P:(k + 1) * P], ident[:, :])
            last.then_inc(full[2], 1)
            pe.wait_ge(s_kmax, 2)
            ps = into(3)
            for k in range(KC):
                last = mm(ps[:, k * P:(k + 1) * P], onesm[:, :], CTX[:, k, :], start=True, stop=True)
            last.then_inc(full[3], 1)
            pe.wait_ge(s_kexp, 1)
            read_out(B_V)
            pe.wait_ge(s_vrow, 1)
            for m in range(KC):
                product(4 + m, P + 1, [(KROW[:, b, m * P:(m + 1) * P], VROW[:, b, m, :]) for b in range(NB)])

            ht = Tally(s_ht)

            def stage3(g):
                for q, b in enumerate(B_Q):
                    m, h = divmod(q, 2)
                    product(b, HN, [(Wq[:, k, m * P:(m + 1) * P], XH[:, k, ds(g * GN + h * HN, HN)]) for k in range(KC)])
                ht.want(pe)
                for j, b in enumerate(B_F):
                    product(b, 2 * C, [(HT[:, k, j * P:(j + 1) * P], Wio[:, k, :]) for k in range(KC)])
                read_out(B_Q)
                for q, b in enumerate(B_O):
                    m, h = divmod(q, 2)
                    product(b, HN, [(CTX[:, m, :], QT[:, m, h * HN:(h + 1) * HN])])

            pe.wait_ge(s_xh, NG)
            read_out([4, 5])
            run_turns(pe, NG, stage3, free + [ht])
            read_out(range(8))

            for d in GATHER_ORDER:
                got, onehot = [Tally(s) for s in s_g[d]], Tally(s_m[d])
                def multiply(base, j, d=d, got=got, onehot=onehot):
                    if j % 4 == 0:
                        got[j // 4].want(pe, 16 * 4)
                    onehot.want(pe)
                    if j % 2 == 0:
                        if static(base) and base == 0 and d == GATHER_ORDER[1] and j < 8:
                            pe.wait_ge(s_add[GATHER_ORDER[0]], STEPS - 6 + j)
                        at_least(pe, s_add[d], base + (j - 6))
                    ps = bank[j // 2 % 4][:, j % 2 * C:(j % 2 + 1) * C]
                    for k in range(KC):
                        last = mm(ps[:, k * P:(k + 1) * P], GATH[:, j, k * P:(k + 1) * P], ONEHOT[:, j % 8, :],
                                  start=True, stop=True)
                    last.then_inc(s_agg[d], 1)

                def unit_products(u):
                    seg = ds(u * HN, HN)
                    for m in range(4):
                        ps = into(4 + m)[:, 0:HN]
                        for n, (s, t) in enumerate(((0, AGG[0]), (2, XH))):
                            for k in range(KC):
                                last = mm(ps, Wx[:, 2 * s + k, m * P:(m + 1) * P], t[:, k, seg],
                                          start=n + k == 0, stop=n + k == 2)
                                if n + k == 2:
                                    last.then_inc(full[4 + m], 1)
                                yield
                    for m in range(KC):
                        ps = into(4 + m)[:, 0:HN]
                        for k in range(KC):
                            last = mm(ps, Wp[:, k, m * P:(m + 1) * P], OG[:, k, seg], start=k == 0, stop=k == 1)
                            if k == 1:
                                last.then_inc(full[4 + m], 1)
                            yield

                def multiply_turn(base, unit):
                    products = None if unit is None else unit_products(unit)
                    for j in range(TURN):
                        multiply(base, j)
                        if products and (2 <= j < 22 and j % 5 != 1 or 26 <= j < 30):
                            next(products)

                if d == GATHER_ORDER[1]:
                    pe.wait_ge(s_w2, 16 * LAST_LOADS)
                gather_turns(pe, d, multiply_turn, [onehot] + got + free)

            gnn, xn1, wg = (Tally(s) for s in (s_gnn, s_xn1, s_wg))
            pe.wait_ge(s_add[GATHER_ORDER[1]], STEPS)
            pe.wait_ge(s_hk, NG)

            def update_sums(first_node):
                for q, b in enumerate(T_X):
                    m, h = divmod(q, 2)
                    product(b, HN, [(Wx[:, KC + k, m * P:(m + 1) * P], AGG[1][:, k, ds(first_node + h * HN, HN)])
                                    for k in range(KC)])

            def stage5(g, more=True):
                gnn.want(pe)
                for j, b in enumerate(T_R):
                    ps = into(b)
                    for k in range(KC):
                        last = pe.transpose(ps[:, k * P:(k + 1) * P], GNN[:, k, j * P:(j + 1) * P], ident[:, :])
                    last.then_inc(full[b], 1)
                if more:
                    update_sums(g * GN + GN)
                xn1.want(pe)
                transposes(T_T, XN1)
                read_out(T_T)
                ps = into(T_L[0])
                for j in range(GB):
                    for k in range(KC):
                        last = mm(ps[:, j * NEXP:(j + 1) * NEXP], XT1[:, k, j * P:(j + 1) * P], Wgate[:, k, :],
                                  start=k == 0, stop=k == KC - 1)
                last.then_inc(full[T_L[0]], 1)
                for q, b in enumerate(T_S1):
                    m, h = divmod(q, 2)
                    product(b, HN, [(W1s[:, k, m * P:(m + 1) * P], XT1[:, k, h * HN:(h + 1) * HN]) for k in range(KC)])
                for q, b in enumerate(T_E1):
                    m, h = divmod(q, 2)
                    product(b, HN, [(W1e[:, k, m, :], XT1[:, k, h * HN:(h + 1) * HN]) for k in range(KC)])
                read_out(T_S1)
                for h, b in enumerate(T_S2):
                    product(b, HN, [(W2s[:, k, :], S1[:, k, h * HN:(h + 1) * HN]) for k in range(2)])
                read_out(T_E1[3:])
                for q, b in enumerate(T_E2):
                    m, h = divmod(q, 2)
                    ps = into(b)
                    for e in range(2):
                        last = mm(ps[e * EH2:(e + 1) * EH2, 0:HN], W2e[:, 2 * m + e, :],
                                  E1[:, 2 * m + e, h * HN:(h + 1) * HN], start=True, stop=True)
                    last.then_inc(full[b], 1)
                wg.want(pe)
                transposes(T_W[0:3], WGX.rearrange("p j m c -> p j (m c)"))
                for b, js in ((T_W[3], range(GB - 1)), (T_W[4], range(GB - 1, GB))):
                    ps = into(b)
                    for n, j in enumerate(js):
                        last = pe.transpose(ps[0:NEXP + 1, n * P:(n + 1) * P], t_w5[:, j, :], ident[:, :])
                    last.then_inc(full[b], 1)
                read_out(T_S2 + T_E2 + T_W)
                for j, b in enumerate(T_O):
                    n = slice(j * P, (j + 1) * P)
                    product(b, C, [(S2[:, n], W3s), (E2[:, 0, n], W3e[:, 0, :]), (E2[:, 1, n], W3e[:, 1, :]),
                                   (WGT[0:NEXP + 1, n], B3[0:NEXP + 1, :])])

            update_sums(0)
            run_turns(pe, NG - 1, stage5, free + [gnn, xn1, wg])
            stage5(NG - 1, more=False)

        @block.vector
        def _(dve):
            full, free = [Tally(s) for s in s_full], s_free
            steps = Tally(s_dve)
            v = nc.vector

            def link(ins):
                steps.link(dve, ins)

            def out_of(b):
                full[b].want(dve)
                return bank[b]

            def landed(b):
                dve.wait_ge(free[b], full[b].value())

            def flat(t3):
                return t3.rearrange("p a c -> p (a c)")

            def row_stats(st, m, va, a, c):
                v.tensor_tensor(a, st[:, :, 1], st[:, :, 4], ALU.subtract)
                v.tensor_tensor(c, st[:, :, 2], st[:, :, 5], ALU.add)
                link(v.tensor_tensor(m, st[:, :, 1], st[:, :, 4], ALU.add))
                v.tensor_scalar(m, m, 0.5, None, ALU.mult)
                link(v.scalar_tensor_tensor(a, a, 0.25, a, ALU.mult, ALU.mult))
                link(v.scalar_tensor_tensor(va, c, 1.0 / C, a, ALU.mult, ALU.add))

            v.memset(EI[:, :, 3, :], NP - 1)
            v.memset(SEQ[1], NP - 1)
            v.memset(EF[:, 2:4, 3, :], 0.0).then_inc(s_pad, 1)
            v.memset(XROW[:, NB - 1, :], 0.0).then_inc(s_xz, 1)
            v.memset(ZERO, 0.0)
            v.memset(cnt[:, NB:NB + 2], 0.0)
            dve.wait_ge(s_edges, 16 * 12)
            v.tensor_copy(EF[:, 0:2, :, :], EI[:, :, :, :]).then_inc(s_eflt, 1)
            ps = out_of(0)
            v.tensor_copy(REC[0][:, :, 0], ps[:, 0:EC])
            v.tensor_copy(REC[1][:, :, 1], ps[:, 0:EC]).then_inc(free[0], 1)
            ps = out_of(1)
            v.tensor_copy(REC[0][:, :, 1], ps[:, 0:EC])
            v.tensor_copy(REC[1][:, :, 0], ps[:, 0:EC]).then_inc(free[1], 1)
            v.tensor_copy(REC[0][:, :, 2], out_of(2)[:, 0:EC]).then_inc(free[2], 1)
            v.tensor_copy(REC[1][:, :, 2], out_of(3)[:, 0:EC]).then_inc(free[3], 1)
            landed(3)

            dve.wait_ge(s_const, 1)
            def places(d, link):
                for b in range(NB):
                    s = SCAN[b % 2]
                    link(v.tensor_tensor_scan(s, ONEB[:, b, :], ZERO, base[:, b:b + 1], ALU.add, ALU.add))
                    link(v.copy_predicated(SLOT, ONEB[:, b, :].bitcast(mybir.dt.uint16), s))
                link(v.tensor_copy(KEYI, SLOT))
                v.tensor_scalar(LOI, KEYI, P - 1, None, ALU.bitwise_and)
                link(v.tensor_scalar(HII, KEYI, 7, None, ALU.arith_shift_right))
                v.scalar_tensor_tensor(ADDR[d][:, :], LOI, float(EC), HII, ALU.mult, ALU.add).then_inc(s_addr[d], 1)

            dve.wait_ge(s_seq, 48)
            link(v.tensor_tensor(FALL, SEQ[0], SEQ[1], ALU.is_gt))
            link(v.tensor_reduce(cnt[0:E // SQ, NB + 1:NB + 2], FALL, AX.X, ALU.add))
            K = NB + 1
            for d in SORT_ORDER:
                link(v.tensor_copy(KEYI, REC[d][:, :, 1]))
                link(v.tensor_scalar(KEYI, KEYI, 7, None, ALU.arith_shift_right))
                link(v.tensor_copy(KEYB, KEYI))
                for b in range(NB):
                    last = v.tensor_scalar(ONEB[:, b, :], KEYB, float(b), None, ALU.is_equal, ALU.add,
                                           accum_out=cnt[:, b:b + 1])
                last.then_inc(s_cnt, 1)
                v.memset(SLOT, 0.0)
                before, tot = out_of(4), out_of(5)
                link(v.tensor_copy(total, tot[:, 0:K]))
                if d == 0:
                    v.tensor_copy(unsorted[:, :], tot[0:1, K:K + 1]).then_inc(s_flag, 1)
                    dve.wait_ge(s_flag, 1)
                dve.sem_inc(free[5], 1)
                link(v.tensor_tensor_scan(incl, total, zero_f, 0.0, ALU.add, ALU.add))
                link(v.tensor_tensor(total, incl, total, ALU.subtract))
                v.scalar_tensor_tensor(base, total, -1.0, before[:, 0:K], ALU.add, ALU.add).then_inc(free[4], 1)
                link(v.memset(colw, 0.0))
                landed(4)
                if d == 1:
                    places(d, link)
                else:
                    falls = dve.value_load(unsorted[0:1, 0:1], min_val=0, max_val=E)
                    with dve.If(falls > 0):
                        rank = Tally(s_rank)
                        places(d, lambda ins: rank.link(dve, ins))

                v.tensor_tensor(SCAN[0][0:K, 0:K], total[0:K, :], ident[0:K, 0:K], ALU.mult)
                link(v.tensor_tensor(SCAN[1][0:K, 0:K], incl[0:K, :], ident[0:K, 0:K], ALU.mult))
                v.tensor_reduce(colw[0:K, 0:1], SCAN[0][0:K, 0:K], AX.X, ALU.add)
                link(v.tensor_reduce(colw[0:K, 1:2], SCAN[1][0:K, 0:K], AX.X, ALU.add))
                v.tensor_copy(coli[0:K, 0:1], colw[0:K, 0:1])
                link(v.tensor_scalar(coli[0:K, 1:2], colw[0:K, 1:2], float(P - 1), None, ALU.add))
                link(v.tensor_scalar(coli[0:K, 0:2], coli[0:K, 0:2], 7, None, ALU.arith_shift_right))
                link(v.tensor_copy(colw[0:K, 1:3], coli[0:K, 0:2]))
                v.tensor_tensor(colw[0:K, 3:4], colw[0:K, 2:3], colw[0:K, 1:2], ALU.subtract).then_inc(s_cnt, 1)
                ps = out_of(6)
                link(v.tensor_copy(colw[0:K, 4:5], ps[0:K, 0:1]))
                dve.sem_inc(free[6], 1)
                v.tensor_tensor(colw[0:K, 5:6], colw[0:K, 1:2], colw[0:K, 4:5], ALU.subtract).then_inc(s_cnt, 1)
                ps = out_of(7)
                v.tensor_scalar(ddrep, onesm[0:K, :], ps[0:K, 0:1], None, ALU.mult).then_inc(free[7], 1)
                v.tensor_scalar(GT, steps_ramp[0:K, :], colw[0:K, 4:5], None, ALU.is_ge).then_inc(s_cnt, 1)
                ps = out_of(6)
                v.tensor_tensor(GTMP, ps[0:1, 0:STEPS], steps_ramp[0:1, :], ALU.add).then_inc(free[6], 1)
                ps = out_of(7)
                v.tensor_scalar(step_off[d][:, :], ps[:, 0:STEPS], float(P), float(-P), ALU.mult, ALU.add).then_inc(free[7], 1)
                landed(6)
                landed(7)
                link(v.tensor_scalar(GTMP, GTMP, float(EC - 1), 0.0, ALU.min, ALU.max))
                v.tensor_copy(tile_no[0:1, d, :], GTMP)
                v.tensor_scalar(acc_col[0:1, d, :], step_off[d][0:1, :], float((NB - 1) * P), None, ALU.min).then_inc(s_list[d], 1)

            dve.wait_ge(s_x, 32)
            for n in range(2):
                with dve.Fori(0, NB) as b:
                    v.bn_stats(stats[:, ds(b, 1), :].rearrange("p a s -> p (a s)"), XROW[:, ds(b, 1), :].rearrange("p a c -> p (a c)"))
                link(dve.drain())
                row_stats(stats, mean, var, ws1, ws2)
                dve.sem_inc(s_var, 1)
                dve.wait_ge(s_sd, n + 1)
                link(v.reciprocal(rstd, rstd))
                if n == 0:
                    with dve.Fori(0, NB) as b:
                        v.tensor_scalar(XROW[:, ds(b, 1), :].rearrange("p a c -> p (a c)"),
                                        XROW[:, ds(b, 1), :].rearrange("p a c -> p (a c)"),
                                        mean[:, ds(b, 1)], rstd[:, ds(b, 1)], ALU.subtract, ALU.mult)
                    link(dve.drain())
                dve.sem_inc(s_xn, 1)

            dve.wait_ge(s_w1, 16 * FIRST_LOADS)
            v.tensor_scalar(bg2_h, bg2_c, 0.5, None, ALU.mult)
            for k in range(KC):
                v.tensor_scalar(VROW[:, :, k, P], padneg, 0.0, None, ALU.is_ge)
            v.memset(KMAX[:, :], FAR).then_inc(s_vrow, 1)
            dve.wait_ge(s_vrow, 1)
            dve.sem_inc(s_xn, 1)

            def stage1(g):
                skip(full, B_XN)
                for j in range(GB):
                    b = ds(g * GB + j, 1)
                    last = v.tensor_scalar(XNNR[:, j, :], XROW[:, b, :].rearrange("p a c -> p (a c)"), mean[:, b], rstd[:, b],
                                           ALU.subtract, ALU.mult)
                last.then_inc(s_xnnr, 1)
                for k in range(KC):
                    v.tensor_scalar(XNT[:, k, 0:GN - P], out_of(B_XNN[k])[:, 0:GN - P], lng_c[:, k:k + 1], lnb_c[:, k:k + 1],
                                    ALU.mult, ALU.add).then_inc(free[B_XNN[k]], 1)
                ps = out_of(B_XNN[2])
                for k in range(KC):
                    last = v.tensor_scalar(XNT[:, k, GN - P:GN], ps[:, k * P:(k + 1) * P], lng_c[:, k:k + 1], lnb_c[:, k:k + 1],
                                           ALU.mult, ALU.add)
                last.then_inc(free[B_XNN[2]], 1)
                skip(full, B_HG)
                for q, b in enumerate(B_K):
                    ps = out_of(b)
                    n = min(2, GB - 2 * q)
                    for j in range(n):
                        blk = ds(g * GB + 2 * q + j, 1)
                        v.tensor_scalar(KROW[:, blk, :].rearrange("p a c -> p (a c)"), ps[:, j * C:(j + 1) * C],
                                        padneg[:, blk], None, ALU.add)
                        last = v.scalar_tensor_tensor(KMAX[:, :], ps[:, j * C:(j + 1) * C], padneg[:, blk], KMAX[:, :],
                                                      ALU.add, ALU.max)
                        if j < n - 1:
                            link(last)
                    last.then_inc(free[b], 1)
                    landed(b)

                skip(full, B_V + B_G)

            run_turns(dve, NG, stage1, full + [steps])

            link(dve.drain())
            dve.wait_ge(s_xh, NG)
            for k in range(KC):
                width = -(-N // 7)
                for n in range(7):
                    v.bn_stats(cs[:, n, :], XH[:, k, n * width:min(N, (n + 1) * width)])
                link(dve.drain())
                link(v.bn_aggr(bnmv[:, k, :], cs))
            dve.sem_inc(s_var, 1)
            dve.sem_inc(s_kmax, 1)
            ps = out_of(2)
            link(v.tensor_reduce(rsum, ps[:, 0:KC * P].rearrange("p (k n) -> p k n", k=KC), AX.X, ALU.max))
            dve.sem_inc(free[2], 1)
            for k in range(KC):
                last = v.tensor_scalar(CTX[:, k, :], ident[:, :], rsum[:, k:k + 1], None, ALU.mult)
            last.then_inc(s_kmax, 1)
            ps = out_of(3)
            link(v.tensor_copy(KMAX[:, :], ps[:, 0:C]))
            dve.sem_inc(free[3], 1)
            v.tensor_tensor(KROW, KROW, KMAX[:, :].unsqueeze(1).to_broadcast([P, NB, C]), ALU.subtract).then_inc(s_kshift, 1)
            dve.wait_ge(s_sd, 3)
            link(v.reciprocal(h_scale, h_scale))
            link(v.tensor_tensor(h_scale, h_scale, gamma_c, ALU.mult))
            link(v.tensor_tensor(h_shift, bnmv[:, :, 0], h_scale, ALU.mult))
            link(v.tensor_tensor(h_shift, beta_c, h_shift, ALU.subtract))
            for m in range(KC):
                ps = out_of(4 + m)
                link(v.reciprocal(rsum[:, m:m + 1], ps[:, P:P + 1]))
                v.scalar_tensor_tensor(CTX[:, m, :], ps[:, 0:P], rsum[:, m:m + 1], headm[:, :],
                                       ALU.mult, ALU.mult).then_inc(free[4 + m], 1)
            v.memset(FLAT[0], 0.0)
            link(v.memset(FLAT[1], 0.0))

            def stage3(g):
                skip(full, B_Q)
                if not static(g):
                    dve.wait_ge(s_hk, g)
                    dve.wait_ge(s_hs, g * 16)
                for k in range(KC):
                    last = v.tensor_scalar(HT[:, k, :], XH[:, k, ds(g * GN, GN)], h_scale[:, k:k + 1], h_shift[:, k:k + 1],
                                           ALU.mult, ALU.add)
                last.then_inc(s_ht, 1)
                if not static(g):
                    dve.wait_ge(s_tab, g * 32)
                for j, b in enumerate(B_F):
                    v.tensor_tensor(FSTAGE[:, j, :], out_of(b)[:, :], bio, ALU.add).then_inc(free[b], 1)
                dve.drain().then_inc(s_fst, 1)
                for q, b in enumerate(B_O):
                    m, h = divmod(q, 2)
                    o = OG[:, m, ds(g * GN + h * HN, HN)]
                    v.scalar_tensor_tensor(o, o, 1.0, out_of(b)[:, 0:HN], ALU.add, ALU.mult).then_inc(free[b], 1)
                dve.drain().then_inc(s_ogd, 1)

            run_turns(dve, NG, stage3, full + [steps])

            for d in GATHER_ORDER:
                picked, product, added = Tally(s_rr[d]), Tally(s_agg[d]), Tally(s_add[d])

                def targets(at, r, d=d, picked=picked):
                    picked.want(dve)
                    link(v.tensor_tensor(REL[:, r:r + 8], RR[:, r:r + 8, 1], step_off[d][:, ds(at, 8)], ALU.subtract))

                def onehot(j, d=d):
                    v.tensor_scalar(ONEHOT[:, j % 8, :], ramp[:, :], REL[:, j:j + 1], RR[:, j, 2:3],
                                    ALU.is_equal, ALU.mult).then_inc(s_m[d], 1)

                def add_turn(base, unit, d=d, product=product, added=added):
                    for j in range(TURN):
                        more = not (static(base) and base == STEPS - TURN and j >= TURN - 8)
                        if more and j % 8 == 0:
                            targets(base + (j + 8), (j + 8) % TURN)
                        c = dve.value_load(acc_col[0:1, d, ds(base + j, 1)], min_val=0, max_val=(NB - 1) * P)
                        o = AGG[d][:, :, ds(c, P)]
                        added.again(dve)
                        if j % 2 == 0:
                            product.want(dve, 2)
                        ps = bank[j // 2 % 4][:, j % 2 * C:(j % 2 + 1) * C]
                        added.made(v.tensor_tensor(o, o, ps.rearrange("p (k n) -> p k n", k=KC), ALU.add))
                        if more:
                            onehot((j + 8) % TURN)

                targets(0, 0)
                for j in range(8):
                    onehot(j)
                gather_turns(dve, d, add_turn, [steps, picked, product, added])
            for u in range(UNITS):
                skip(full, [4, 5, 6, 7, 4, 5])

            dve.wait_ge(s_w2, 16 * LAST_LOADS)
            xr, hr, r1, gates, gexp, g2e = (Tally(s) for s in (s_xr, s_hr, s_r1, s_gates, s_gexp, s_g2e))

            def each(t2, n=NEXP):
                return t2.unsqueeze(2).to_broadcast([P, GB, n])

            def first_of(o, score, best):
                link(v.tensor_tensor(o, score, each(best), ALU.is_equal))
                link(v.tensor_tensor(o, o, pref.unsqueeze(1).to_broadcast([P, GB, NEXP]), ALU.mult))
                link(v.tensor_reduce(t_m, o, AX.X, ALU.max))
                link(v.tensor_tensor(o, o, each(t_m), ALU.is_equal))

            def update_sums(first_node, qs):
                for q in qs:
                    b, (m, h) = T_X[q], divmod(q, 2)
                    v.tensor_tensor((IG, GNN)[m // 2][:, m % 2, h * HN:(h + 1) * HN], out_of(b)[:, 0:HN],
                                    (XH, AGG[0])[m // 2][:, m % 2, ds(first_node + h * HN, HN)], ALU.add).then_inc(free[b], 1)

            def update(first_node):
                hr.want(dve, 16)
                gates.want(dve)
                link(v.tensor_tensor(HB, HB, GNN, ALU.subtract))
                link(v.scalar_tensor_tensor(HB, IG, 1.0, HB, ALU.add, ALU.mult))
                link(v.scalar_tensor_tensor(GNN, HB, 0.5, GNN, ALU.mult, ALU.add))
                v.tensor_tensor(GNN, GNN, OG[:, :, ds(first_node, GN)], ALU.add).then_inc(s_gnn, 1)

            def stage5(g, more=True):
                xr.want(dve, 32)
                for j, b in enumerate(T_R):
                    v.tensor_tensor(X1[:, j, :], XL[:, j, :], out_of(b)[:, 0:C], ALU.add).then_inc(free[b], 1)
                    if j:
                        landed(T_R[j - 1])
                        v.bn_stats(stats[:, j - 1, :], X1[:, j - 1, :])
                landed(T_R[-1])
                v.bn_stats(stats[:, GB - 1, :], X1[:, GB - 1, :])
                link(dve.drain())
                row_stats(stats[:, 0:GB], t_mean, t_var, t_a, t_c)
                v.tensor_scalar(t_var, t_var, EPS, None, ALU.add).then_inc(s_v1, 1)
                if more:
                    update_sums(g * GN + GN, range(0, 4))
                if not static(g) or g > 0:
                    dve.wait_ge(s_st, g * 32)
                r1.want(dve)
                for j in range(GB):
                    last = v.tensor_scalar(XN1[:, j, :], X1[:, j, :], t_mean[:, j:j + 1], t_rstd[:, j:j + 1],
                                           ALU.subtract, ALU.mult)
                last.then_inc(s_xn1, 1)
                if more:
                    update_sums(g * GN + GN, range(4, 8))
                skip(full, T_T)
                ps = out_of(T_L[0])
                link(v.tensor_tensor(t_log, ps[:, 0:GB * NEXP].rearrange("p (j e) -> p j e", e=NEXP),
                                     gb_row.unsqueeze(1).to_broadcast([P, GB, NEXP]), ALU.add))
                dve.sem_inc(free[T_L[0]], 1)
                link(v.tensor_reduce(t_m, t_log, AX.X, ALU.max))
                v.tensor_tensor(t_log, t_log, each(t_m), ALU.subtract).then_inc(s_gx, 1)
                gexp.want(dve)
                link(v.tensor_reduce(t_m, t_exp, AX.X, ALU.add))
                link(v.reciprocal(t_m, t_m))
                link(v.tensor_tensor(t_g, t_exp, each(t_m), ALU.mult))
                link(v.tensor_reduce(t_m1, t_g, AX.X, ALU.max))
                first_of(t_o1, t_g, t_m1)
                link(v.scalar_tensor_tensor(t_sc, t_o1, -2.0, t_g, ALU.mult, ALU.add))
                link(v.tensor_reduce(t_m2, t_sc, AX.X, ALU.max))
                v.tensor_tensor(t_gap, t_m2, t_m1, ALU.subtract).then_inc(s_g2, 1)
                if more:
                    update(g * GN + GN)
                skip(full, T_S1)
                for q, b in enumerate(T_E1):
                    m, h = divmod(q, 2)
                    if h == 0:
                        skip(full, [b])
                    else:
                        v.tensor_scalar(E1[:, m, HN:GN], out_of(b)[:, 0:HN], b1e[:, m:m + 1], 0.0,
                                        ALU.add, ALU.max).then_inc(free[b], 1)
                first_of(t_o2, t_sc, t_m2)
                g2e.want(dve)
                link(v.tensor_scalar(t_m, t_gap_e, 1.0, None, ALU.add))
                link(v.reciprocal(t_m, t_m))
                link(v.tensor_tensor(t_wt, t_gap_e, t_m, ALU.mult))
                v.tensor_tensor(t_o1, t_o1, each(t_m), ALU.mult)
                link(v.tensor_tensor(t_o2, t_o2, each(t_wt), ALU.mult))
                link(v.tensor_tensor(t_w5[:, :, 0:NEXP], t_o1, t_o2, ALU.add))
                for j in range(GB):
                    last = v.tensor_copy(WGX[:, j].rearrange("p m c -> p (m c)").rearrange("p (e c) -> p e c", e=NEXP),
                                         t_w5[:, j, 0:NEXP].unsqueeze(2).to_broadcast([P, NEXP, EH2]))
                last.then_inc(s_wg, 1)
                skip(full, T_S2)
                for q, b in enumerate(T_E2):
                    m, h = divmod(q, 2)
                    v.tensor_scalar(E2[:, m, h * HN:(h + 1) * HN], out_of(b)[:, 0:HN], b2e[:, m:m + 1], 0.0,
                                    ALU.add, ALU.max).then_inc(free[b], 1)
                for b in T_E2:
                    landed(b)
                for k in range(KC):
                    b = T_W[k]
                    v.tensor_tensor(E2[:, k, 0:GN - P], E2[:, k, 0:GN - P], out_of(b)[:, 0:GN - P], ALU.mult).then_inc(free[b], 1)
                b = T_W[2]
                v.tensor_tensor(E2[:, :, GN - P:GN], E2[:, :, GN - P:GN],
                                out_of(b)[:, 0:KC * P].rearrange("p (k n) -> p k n", k=KC), ALU.mult).then_inc(free[b], 1)
                for b, (lo, hi) in zip(T_W[3:], ((0, GN - P), (GN - P, GN))):
                    v.tensor_copy(WGT[0:NEXP + 1, lo:hi], out_of(b)[0:NEXP + 1, 0:hi - lo]).then_inc(free[b], 1)
                for j, b in enumerate(T_O):
                    v.tensor_tensor(OUTR[:, j, :], out_of(b)[:, 0:C], X1[:, j, :], ALU.add).then_inc(free[b], 1)
                dve.drain().then_inc(s_out, 1)

            update_sums(0, range(8))
            update(0)
            run_turns(dve, NG - 1, stage5, full + [steps, xr, hr, r1, gates, gexp, g2e])
            stage5(NG - 1, more=False)


def kernel(**inputs):
    import numpy as np
    import concourse.bacc as bacc
    from concourse import mybir
    from concourse.bass_utils import run_bass_kernel_spmd

    nc = bacc.Bacc("TRN2", target_bir_lowering=False, num_devices=1)
    names = ("x src dst edge_weight edge_weight_n2 L0_gnn_gamma L0_gnn_beta L0_gnn_W_in L0_gnn_b_in L0_gnn_W_out "
             "L0_gnn_b_out L0_gnn_W_x2i L0_gnn_b_x2i L0_gnn_W_h2h L0_mix_Wqkv L0_mix_Wproj L0_mix_bproj L0_mix_ln_g "
             "L0_mix_ln_b L0_mix_Wg1 L0_mix_bg1 L0_mix_Wg2 L0_mix_bg2 L0_ffn_sW1 L0_ffn_sb1 L0_ffn_sW2 L0_ffn_sb2 "
             "L0_ffn_sW3 L0_ffn_sb3 L0_ffn_eW1 L0_ffn_eb1 L0_ffn_eW2 L0_ffn_eb2 L0_ffn_eW3 L0_ffn_eb3 L0_ffn_gW "
             "L0_ffn_gb").split()
    arrays, args = {}, []
    for name in names:
        a = np.ascontiguousarray(inputs[name])
        arrays[f"in_{name}"] = a
        args.append(nc.dram_tensor(f"in_{name}", a.shape, mybir.dt.from_np(a.dtype), kind="ExternalInput").ap())
    args.append(nc.dram_tensor("out0", (N, C), mybir.dt.float32, kind="ExternalOutput").ap())
    gps_layer(nc, *args)
    result = run_bass_kernel_spmd(nc, [arrays], core_ids=[0])
    return result.results[0]["out0"]
```

```python
import concourse.bass as bass
from concourse import mybir
from contextlib import ExitStack

N, C, E = 3125, 256, 50000
P = 128
NB = -(-N // P)
NP = NB * P
LAST = N - (NB - 1) * P
KC = C // P
GB = 5
NG = NB // GB
GN = GB * P
HN = GN // 2
EC = -(-E // P)
STEPS = EC + NB
NEXP, EH1, EH2 = 4, 128, 64
GH = C // 4
HD = 32
FS = 23
FS_A = 12
HALVES = ((0, FS_A), (FS_A, FS))
EARLY = 2
SQ = 400
EPS = 1e-5
FAR = -1e30
FIRST_LOADS, LAST_LOADS = 13, 22
TURN = 32
UNITS = 10
SORT_ORDER = (1, 0)
GATHER_ORDER = (0, 1)


class Tally:

    def __init__(self, sem):
        self.sem, self.n, self.i, self.per = sem, 0, None, 0

    def value(self):
        return self.n if self.i is None else self.i * self.per + (self.n - self.per)

    def made(self, ins, k=1):
        ins.then_inc(self.sem, k)
        self.n += k
        return ins

    def want(self, eng, k=1):
        self.n += k
        eng.wait_ge(self.sem, self.value())

    def again(self, eng, k=0):
        if self.i is not None or self.n > k:
            eng.wait_ge(self.sem, self.value() - k if k else self.value())

    def link(self, eng, ins):
        self.made(ins)
        eng.wait_ge(self.sem, self.value())


def run_turns(eng, turns, body, tallies):
    before = [t.n for t in tallies]
    body(0)
    pers = [t.n - n for t, n in zip(tallies, before)]
    with eng.Fori(1, turns) as i:
        starts = [t.n for t in tallies]
        for t, per in zip(tallies, pers):
            t.i, t.per = i, per
        body(i)
        for t, per, n in zip(tallies, pers, starts):
            assert t.n - n == per
            t.i = None
    for t, per in zip(tallies, pers):
        t.n += per * (turns - 2)


def gps_layer(nc, x, src, dst, ew_in, ew_out, gamma, beta, W_in, b_in, W_out, b_out, W_x2i, b_x2i,
              W_h2h, Wqkv, Wproj, bproj, ln_g, ln_b, Wg1, bg1, Wg2, bg2, sW1, sb1, sW2, sb2, sW3,
              sb3, eW1, eb1, eW2, eb2, eW3, eb3, gW, gb, out):
    f32, i32, bf16 = mybir.dt.float32, mybir.dt.int32, mybir.dt.bfloat16
    ALU, ACT, AX = mybir.AluOpType, mybir.ActivationFunctionType, mybir.AxisListType
    On = bass.IndirectOffsetOnAxis
    ds = bass.ds
    ctx = ExitStack()
    with ctx:
        def sb(name, shape, dt=f32):
            return ctx.enter_context(nc.sbuf_tensor(name, shape, dt))

        def sem(name):
            return ctx.enter_context(nc.semaphore(name))

        rec_dram = [nc.dram_tensor(f"rec_{d}", (P * EC, 3), f32, kind="Internal").ap() for d in ("to_dst", "to_src")]
        h_dram = nc.dram_tensor("h_kept", (NG, P, KC * GN), f32, kind="Internal").ap()
        table = [nc.dram_tensor(f"table_{d}", (NP, C), f32, kind="Internal").ap() for d in ("in", "out")]

        XH = sb("XH", [P, KC, NP])
        OG = sb("OG", [P, KC, NP])
        AGG = [sb("AGG_in", [P, KC, NP]), sb("AGG_out", [P, KC, NP + NB])]
        FLAT = [a[:, :, :].rearrange("p k n -> p (k n)") for a in AGG]
        KROW = FLAT[0].rearrange("p (b c) -> p b c", b=NB)
        VROW = FLAT[1].rearrange("p (b k c) -> p b k c", b=NB, k=KC)
        ident = sb("ident", [P, P])
        ramp = sb("ramp", [P, P])
        steps_ramp = sb("steps_ramp", [P, STEPS])
        edge_work = sb("edge_work", [P, 2 * (4 * EC + STEPS)])
        REC = [edge_work[:, o:o + 3 * EC].rearrange("p (c w) -> p c w", w=3) for o in (0, 3 * EC)]
        ADDR = [edge_work[:, o:o + EC].bitcast(i32) for o in (6 * EC, 7 * EC)]
        step_off = [edge_work[:, o:o + STEPS] for o in (8 * EC, 8 * EC + STEPS)]
        unsorted = sb("unsorted", [1, 1], i32)
        tile_no = sb("tile_no", [1, 2, STEPS], i32)
        acc_col = sb("acc_col", [1, 2, STEPS], i32)
        SREC = sb("SREC", [P, FS, 3])
        SADR = sb("SADR", [P, FS], i32)
        small = sb("small", [P, 900])
        upper = sb("upper", [P, P])
        onesm = sb("onesm", [P, P])
        diffm = sb("diffm", [NB + 1, NB + 1])
        headm = sb("headm", [P, P])
        CTX = sb("CTX", [P, KC, P])
        KMAX = sb("KMAX", [P, C])

        RSIZE = 19300
        R = sb("region", [P, RSIZE])

        def cutter(*spans):
            state = [list(s) for s in spans]

            def cut(*shape):
                size = 1
                for n in shape:
                    size *= n
                for s in state:
                    if s[0] + size <= s[1]:
                        v = R[:, s[0]:s[0] + size]
                        s[0] += size
                        if len(shape) == 2:
                            v = v.rearrange("p (a b) -> p a b", a=shape[0])
                        if len(shape) == 3:
                            v = v.rearrange("p (a b c) -> p a b c", a=shape[0], b=shape[1])
                        return v
                raise ValueError(shape)
            return cut

        cut = cutter((0, RSIZE))
        XROW = cut(NB, C)
        Wq = cut(KC, 3 * C)
        Wg1s = cut(KC, GH)
        Wg2s = cut(C)
        Wio = cut(KC, 2 * C)
        bio = cut(2 * C)
        XNR = cut(GB, C)
        XNNR = cut(GB, C)
        XTR = cut(KC, GN)
        XNT = cut(KC, GN)
        HG = cut(GN)
        QT = XNR.rearrange("p a b -> p (a b)").rearrange("p (k n) -> p k n", k=KC)
        HT = XNNR.rearrange("p a b -> p (a b)").rearrange("p (k n) -> p k n", k=KC)
        cut = cutter((0, NB * C))
        FSTAGE = cut(GB, 2 * C)
        LW = 9600
        cut = cutter((0, LW))
        GATH = cut(TURN, C)
        ONEHOT = cut(8, P)
        RR = cut(TURN, 3)
        REL = cut(TURN)
        IR = cut(TURN).bitcast(i32)
        cut = cutter((LW, LW + 7710))
        Wx = cut(6, 2 * C)
        Wp = cut(KC, C)
        W1s = cut(KC, 256)
        W2s = cut(2, 128)
        W3s = cut(C)
        W1e = cut(KC, NEXP, EH1)
        W2e = cut(NEXP, EH2)
        W3e = cut(2, C)
        B3 = cut(C)
        Wgate = cut(C, NEXP)
        gb_row = cut(NEXP)
        bx = cut(4)
        bp = cut(KC)
        b1s = cut(2)
        b2s = cut(1)
        b1e = cut(NEXP)
        b2e = cut(2)
        cut = cutter((0, LW), (LW + 7710, RSIZE))
        E1 = cut(NEXP, GN)
        GNN = cut(KC, GN)
        X1 = cut(GB, C)
        XN1 = cut(GB, C)
        OUTR = XN1
        XT1 = cut(KC, GN)
        WGX = XT1.rearrange("p k n -> p (k n)").rearrange("p (j m c) -> p j m c", j=GB, m=2)
        S1 = cut(2, GN)
        S2 = cut(GN)
        E2 = cut(2, GN)
        WGT = cut(GN)
        IG, HB = (edge_work[:, o * GN:(o + 2) * GN].rearrange("p (k n) -> p k n", k=KC) for o in (0, 2))
        XL = edge_work[:, 4 * GN:6 * GN].rearrange("p (j c) -> p j c", j=GB)

        ONEB = FLAT[0][:, 0:(NB * EC + 1) // 2].bitcast(bf16)[:, 0:NB * EC].rearrange("p (b c) -> p b c", b=NB)
        GT = FLAT[0][0:NB + 1, 4900:4900 + STEPS]
        ddrep = FLAT[0][0:NB + 1, 5400:5400 + P]
        GTMP = FLAT[0][0:1, 5600:5600 + STEPS]
        EF = FLAT[1][:, 0:2048].rearrange("p (a b c) -> p a b c", a=4, b=4)
        EI = FLAT[1].bitcast(i32)[:, 2048:3072].rearrange("p (a b c) -> p a b c", a=2, b=4)
        KEYI, LOI, HII = (FLAT[1].bitcast(i32)[:, o:o + EC] for o in (3072, 5472, 5872))
        KEYB, ZERO, SLOT = (FLAT[1][:, o:o + EC] for o in (3472, 3872, 5072))
        SCAN = [FLAT[1][:, o:o + EC] for o in (4272, 4672)] + [KEYB]

        SEQ = [XTR.rearrange("p k n -> p (k n)").bitcast(i32)[0:E // SQ, o:o + SQ] for o in (0, SQ)]

        FALL = XNT.rearrange("p k n -> p (k n)")[0:E // SQ, 0:SQ]

        at = [0]

        def few(n):
            at[0] += n
            assert at[0] <= 900
            return small[:, at[0] - n:at[0]]

        stats = few(NB * 6).rearrange("p (b s) -> p b s", s=6)
        mean, var, rstd, ws1, ws2 = few(NB), few(NB), few(NB), few(NB), few(NB)
        padneg, eps_col = few(NB), few(1)
        cnt = few(NB + 2)
        total, incl, base, base_2, zero_f = (few(NB + 1) for _ in range(5))
        colw = few(8)
        coli = few(2).bitcast(i32)
        gamma_c, beta_c, lng_c, lnb_c = few(KC), few(KC), few(KC), few(KC)
        bg1_c, bg2_c, bg2_h = few(1), few(KC), few(KC)
        h_scale, h_shift, rsum = few(KC), few(KC), few(KC)
        cs = few(7 * 6).rearrange("p (b s) -> p b s", s=6)
        bnmv = few(KC * 2).rearrange("p (k s) -> p k s", s=2)
        neghalf = few(GB)
        pref = few(NEXP)
        t_log, t_exp, t_g, t_sc, t_o1, t_o2 = (few(GB * NEXP).rearrange("p (j e) -> p j e", e=NEXP) for _ in range(6))
        t_w5 = few(GB * (NEXP + 1)).rearrange("p (j e) -> p j e", e=NEXP + 1)
        t_m, t_m1, t_m2, t_gap, t_gap_e, t_wt = (few(GB) for _ in range(6))
        t_mean, t_var, t_rstd, t_a, t_c = (few(GB) for _ in range(5))

        bank = [ctx.enter_context(nc.psum_tensor(f"bank{b}", [P, 512], f32)) for b in range(8)]

        s_full = [sem(f"bank_full{b}") for b in range(8)]
        s_free = [sem(f"bank_free{b}") for b in range(8)]
        both = ("in", "out")
        s_const = sem("constants_ready")
        s_pad = sem("edge_pads_set")
        s_xz = sem("x_pad_zeroed")
        s_edges = sem("edges_loaded")
        s_src = sem("src_loaded")
        s_eflt = sem("src_float")
        s_dflt = sem("dst_float")
        s_recs = sem("records_ready")
        s_seq = sem("dst_sequence_loaded")
        s_flag = sem("unsorted_known")
        s_rank = sem("in_rank_steps")
        s_x = sem("x_loaded")
        s_w1 = sem("first_weights_loaded")
        s_w2 = sem("last_weights_loaded")
        s_cnt = sem("counts_ready")
        s_list = [sem(f"work_list_ready_{d}") for d in both]
        s_addr = [sem(f"places_ready_{d}") for d in both]
        s_copied = [[sem(f"records_staged_{d}{h}") for h in "ab"] for d in both]
        s_scat = [[sem(f"scattered_{d}{h}") for h in "ab"] for d in both]
        s_rel = [sem(f"ordered_{d}") for d in both]
        s_gp = sem("gpsimd_steps")
        s_dve = sem("vector_steps")
        s_apart = sem("standalone_waits")
        s_var = sem("variances_ready")
        s_sd = sem("deviations_ready")
        s_xn = sem("xn_ready")
        s_xnr = sem("xn_rows_staged")
        s_xnnr = sem("xnn_rows_staged")
        s_xh = sem("xn_kept")
        s_kmax = sem("kmax_ready")
        s_kshift = sem("k_shifted")
        s_kexp = sem("k_exp_done")
        s_vrow = sem("v_rows_done")
        s_ht = sem("h_group_ready")
        s_hk = sem("h_kept")
        s_hs = sem("h_stored")
        s_ogd = sem("gated_output_done")
        s_fst = sem("table_rows_staged")
        s_tab = sem("table_written")
        s_g = [[sem(f"gathered_{d}{k}") for k in range(TURN // 4)] for d in both]
        s_rr = [sem(f"step_records_{d}") for d in both]
        s_ri = [sem(f"step_rows_{d}") for d in both]
        s_m = [sem(f"onehot_{d}") for d in both]
        s_agg = [sem(f"tile_multiplied_{d}") for d in both]
        s_add = [sem(f"tile_added_{d}") for d in both]
        s_gates = sem("gates_ready")
        s_gnn = sem("gnn_ready")
        s_xr = sem("x_rows_back")
        s_hr = sem("h_back")
        s_dh = sem("h_difference_ready")
        s_mix = sem("h_mixed")
        s_v1 = sem("ffn_variance_ready")
        s_r1 = sem("ffn_rstd_ready")
        s_xn1 = sem("ffn_rows_ready")
        s_gx = sem("gate_logits_shifted")
        s_gexp = sem("gate_exp")
        s_g2 = sem("gate_gap")
        s_g2e = sem("gate_gap_exp")
        s_wg = sem("expert_weights_ready")
        s_out = sem("out_rows_ready")
        s_st = sem("out_stored")

        block = ctx.enter_context(nc.Block())

        B_XN, B_XNN, B_HG = [0, 1, 2], [3, 4, 5], [6, 7]
        B_K, B_V, B_G = [0, 1, 2], [3, 4, 5], [6, 7, 0, 1]
        B_Q, B_F, B_O = [0, 1, 2, 3], [4, 5, 6, 7, 0], [1, 2, 3, 4]
        T_X = [5, 6, 7, 0, 1, 2, 3, 4]
        T_R = [0, 1, 2, 3, 4]
        T_T = [5, 6, 7]
        T_S1 = [1, 2, 3, 4]
        T_E1 = [5, 6, 7, 0, 1, 2, 3, 4]
        T_S2 = [5, 6]
        T_E2 = [7, 0, 1, 2]
        T_W = [3, 4, 5, 6, 7]
        T_O = [0, 1, 2, 3, 4]

        def tallies(sems):
            return [Tally(s) for s in sems]

        def skip(full, plan):
            for b in plan:
                full[b].n += 1

        def static(i):
            return isinstance(i, int)

        def at_least(eng, sem, value):
            if not static(value) or value > 0:
                eng.wait_ge(sem, value)

        def gather_turns(eng, d, turn, tallies):
            units = UNITS if d == GATHER_ORDER[1] else 0
            if units:
                run_turns(eng, units, lambda i: turn(i * TURN, i), tallies)
            run_turns(eng, STEPS // TURN - units - 1, lambda i: turn(i * TURN + units * TURN, None), tallies)
            turn(STEPS - TURN, None)

        def apart(eng, i):
            if not static(i):
                eng.sem_inc(s_apart, 1)

        def col(v, c=P):
            return v.rearrange("(k p) -> p k", p=c)

        @block.sync
        def _(sp):
            sp.wait_ge(s_pad, 1)
            for k, (a, tile) in enumerate(((src, EI[:, 0]), (dst, EI[:, 1]), (ew_in, EF[:, 2]), (ew_out, EF[:, 3]))):
                if k == 1:
                    sp.wait_ge(s_pad, 2)
                loaded = s_src if k == 0 else s_edges
                whole = P * P * 3
                rest = (E - whole) // P
                sp.dma_start(tile[:, 0:3, :], a[0:whole].rearrange("(b q r) -> q b r", b=3, q=P)).then_inc(loaded, 16)
                sp.dma_start(tile[0:rest, 3, :], a[whole:whole + rest * P].rearrange("(q r) -> q r", r=P)).then_inc(loaded, 16)
                sp.dma_start(tile[rest:rest + 1, 3, 0:E - whole - rest * P],
                             a[whole + rest * P:E].rearrange("(a r) -> a r", a=1)).then_inc(loaded, 16)
            sp.dma_start(SEQ[0], dst[0:E].rearrange("(q r) -> q r", r=SQ)).then_inc(s_seq, 16)
            sp.dma_start(SEQ[1][0:E // SQ - 1, :], dst[1:E - SQ + 1].rearrange("(q r) -> q r", r=SQ)).then_inc(s_seq, 16)
            sp.dma_start(SEQ[1][E // SQ - 1:E // SQ, 0:SQ - 1], dst[E - SQ + 1:E].rearrange("(a r) -> a r", a=1)).then_inc(s_seq, 16)
            sp.wait_ge(s_xz, 1)
            sp.dma_start(XROW[:, 0:NB - 1, :], x[0:(NB - 1) * P, :].rearrange("(b p) c -> p b c", p=P)).then_inc(s_x, 16)
            sp.dma_start(XROW[0:LAST, NB - 1, :], x[(NB - 1) * P:N, :]).then_inc(s_x, 16)

            def first(dst_, src_):
                sp.dma_start(dst_, src_).then_inc(s_w1, 16)

            first(Wq, Wqkv.rearrange("(k p) n -> p k n", p=P))
            first(Wg1s, Wg1.rearrange("(k p) n -> p k n", p=P))
            first(Wg2s[0:GH, :], Wg2)
            first(Wio[:, :, 0:C], W_in.rearrange("(k p) n -> p k n", p=P))
            first(Wio[:, :, C:2 * C], W_out.rearrange("(k p) n -> p k n", p=P))
            first(bio[:, 0:C], b_in.partition_broadcast(P))
            first(bio[:, C:2 * C], b_out.partition_broadcast(P))
            with nc.allow_non_contiguous_dma("per-channel vectors, a few hundred numbers each"):
                for t, v in ((gamma_c, gamma), (beta_c, beta), (lng_c, ln_g), (lnb_c, ln_b), (bg2_c, bg2)):
                    first(t, col(v))
                first(bg1_c[0:GH, :], col(bg1, GH))

            staged, landed = ([Tally(s) for s in some[1]] for some in (s_copied, s_scat))

            def stage_turn(i):
                for half, (lo, hi) in enumerate(HALVES):
                    landed[half].again(sp)
                    landed[half].n += 16 * (hi - lo)
                    apart(sp, i)
                    staged[half].made(sp.dma_start(SREC[:, lo:hi, :], REC[1][:, ds(i * FS + lo, hi - lo), :]), 16)
                    staged[half].made(sp.dma_start(SADR[:, lo:hi], ADDR[1][:, ds(i * FS + lo, hi - lo)]), 16)

            sp.wait_ge(s_recs, 1)
            sp.wait_ge(s_addr[1], 1)
            run_turns(sp, EARLY, stage_turn, staged + landed)
            sp.wait_ge(s_addr[1], 2)
            run_turns(sp, EC // FS - EARLY, lambda i: stage_turn(i + EARLY), staged + landed)

            sp.wait_ge(s_ogd, NG)
            sp.wait_ge(s_hk, NG)
            sp.wait_ge(s_hs, 16 * NG)
            n_last = [0]

            def last(dst_, src_):
                sp.dma_start(dst_, src_).then_inc(s_w2, 16)
                n_last[0] += 1

            last(Wx[:, 0:4, :], W_x2i.rearrange("(k p) n -> p k n", p=P))
            last(Wx[:, 4:6, :], W_h2h.rearrange("(k p) n -> p k n", p=P))
            last(Wp, Wproj.rearrange("(k p) n -> p k n", p=P))
            last(W1s, sW1.rearrange("(k p) n -> p k n", p=P))
            last(W2s, sW2.rearrange("(k p) n -> p k n", p=P))
            last(W3s, sW3)
            for k in range(KC):
                last(W1e[:, k], eW1[:, k * P:(k + 1) * P, :].rearrange("e p h -> p e h"))
            last(W2e, eW2.rearrange("e p g -> p e g"))
            for q in range(2):
                last(W3e[:, q, :], eW3[2 * q:2 * q + 2].rearrange("e g o -> (e g) o"))
            last(B3[0:NEXP, :], eb3)
            last(B3[NEXP:NEXP + 1, :], sb3.rearrange("(a n) -> a n", a=1))
            last(Wgate, gW.rearrange("c e -> (c e)").partition_broadcast(P).rearrange("p (c e) -> p c e", e=NEXP))
            last(gb_row, gb.partition_broadcast(P))
            with nc.allow_non_contiguous_dma("per-channel vectors, a few hundred numbers each"):
                last(bx, col(b_x2i))
                last(bp, col(bproj))
                last(b1s, col(sb1))
                last(b2s, col(sb2))
                last(b1e, eb1.rearrange("e p -> p e"))
                for q in range(2):
                    last(b2e[:, q:q + 1], eb2[2 * q:2 * q + 2, :].rearrange("e g -> (e g)").rearrange("(p a) -> p a", a=1))
            assert n_last[0] == LAST_LOADS

            sp.wait_ge(s_scat[1][0], 16 * FS_A * (EC // FS))
            sp.wait_ge(s_scat[1][1], 16 * (FS - FS_A) * (EC // FS))
            sp.dma_start(REC[1][:, :, :], rec_dram[1].rearrange("(p c) w -> p c w", p=P)).then_inc(s_rel[1], 16)

            sp.wait_ge(s_agg[GATHER_ORDER[1]], STEPS)
            sp.wait_ge(s_add[GATHER_ORDER[1]], STEPS)

            def rows_of(g):
                b = g * GB + GB - 1
                return slice(g * GN, b * P), slice(b * P, min(N, b * P + P)), min(P, N - b * P)

            def load(g):
                full_, rest, n = rows_of(g)
                if g:
                    sp.wait_ge(s_gnn, g)
                sp.dma_start(HB, h_dram[g].rearrange("p (k n) -> p k n", k=KC)).then_inc(s_hr, 16)
                if g:
                    sp.wait_ge(s_v1, g)
                sp.dma_start(XL[:, 0:GB - 1, :], x[full_, :].rearrange("(b p) c -> p b c", p=P)).then_inc(s_xr, 16)
                sp.dma_start(XL[0:n, GB - 1, :], x[rest, :]).then_inc(s_xr, 16)

            load(0)
            for g in range(NG):
                if g < NG - 1:
                    load(g + 1)
                full_, rest, n = rows_of(g)
                sp.wait_ge(s_out, g + 1)
                sp.dma_start(out[full_, :].rearrange("(b p) c -> p b c", p=P), OUTR[:, 0:GB - 1, :]).then_inc(s_st, 16)
                sp.dma_start(out[rest, :], OUTR[0:n, GB - 1, :]).then_inc(s_st, 16)
            sp.wait_ge(s_st, 32 * NG)

        @block.gpsimd
        def _(gp):
            ch = Tally(s_gp)
            gp.iota(ramp[:, :], [[1, P]], base=0, channel_multiplier=0, allow_small_or_imprecise_dtypes=True)
            gp.iota(steps_ramp[:, :], [[1, STEPS]], base=0, channel_multiplier=0, allow_small_or_imprecise_dtypes=True)
            gp.memset(eps_col, EPS)
            gp.memset(zero_f, 0.0)
            gp.memset(ident[:, :], 0.0)
            gp.memset(upper[:, :], 1.0)
            gp.memset(diffm[:, :], 0.0)
            gp.memset(headm[:, :], 0.5)
            gp.memset(padneg, 0.0)
            gp.memset(neghalf, -0.5)
            for e in range(NEXP):
                gp.memset(pref[:, e:e + 1], float(NEXP - e))
            gp.memset(t_w5[:, :, NEXP:NEXP + 1], 1.0)
            ch.link(gp, gp.memset(onesm[:, :], 1.0))
            gp.affine_select(out=ident[:, :], in_=ident[:, :], compare_op=ALU.not_equal, fill=1.0, base=0,
                             pattern=[[-1, P]], channel_multiplier=1)
            gp.affine_select(out=upper[:, :], in_=upper[:, :], compare_op=ALU.is_gt, fill=0.0, base=0,
                             pattern=[[1, P]], channel_multiplier=-1)
            gp.affine_select(out=diffm[:, :], in_=diffm[:, :], compare_op=ALU.not_equal, fill=1.0, base=0,
                             pattern=[[-1, NB + 1]], channel_multiplier=1)
            ch.link(gp, gp.affine_select(out=headm[:, :], in_=headm[:, :], compare_op=ALU.is_ge, fill=0.0, base=0,
                                         pattern=[[-HD, P // HD], [0, HD]], channel_multiplier=1))
            gp.affine_select(out=diffm[:, :], in_=diffm[:, :], compare_op=ALU.not_equal, fill=-1.0, base=1,
                             pattern=[[-1, NB + 1]], channel_multiplier=1)
            gp.affine_select(out=headm[:, :], in_=headm[:, :], compare_op=ALU.is_gt, fill=0.0, base=HD,
                             pattern=[[HD, P // HD], [0, HD]], channel_multiplier=-1)
            gp.affine_select(out=padneg[:, NB - 1:NB], in_=padneg[:, NB - 1:NB], compare_op=ALU.is_gt, fill=FAR, base=LAST,
                             pattern=[[0, 1]], channel_multiplier=-1).then_inc(s_const, 1)

            def scatter(d, turns, staging):
                staged, landed = ([Tally(s) for s in some[d]] for some in (s_copied, s_scat))

                def scatter_turn(i):
                    for half, (lo, hi) in enumerate(HALVES):
                        staging(i, lo, hi, staged[half], landed[half])
                        apart(gp, i)
                        for j in range(lo, hi):
                            landed[half].made(gp.indirect_dma_start(
                                rec_dram[d][:, :], On(ap=SADR[:, j:j + 1], axis=0), SREC[:, j, :], None), 16)

                run_turns(gp, turns, scatter_turn, staged + landed)

            def staged_by_sync(i, lo, hi, staged, landed):
                staged.want(gp, 32)

            def own_staging(i, lo, hi, staged, landed):
                landed.again(gp)
                apart(gp, i)
                staged.made(gp.tensor_copy(SREC[:, lo:hi, :], REC[0][:, ds(i * FS + lo, hi - lo), :]))
                staged.made(gp.tensor_copy(SADR[:, lo:hi], ADDR[0][:, ds(i * FS + lo, hi - lo)]))
                staged.again(gp)

            scatter(1, EC // FS, staged_by_sync)
            gp.wait_ge(s_flag, 1)
            falls = gp.value_load(unsorted[0:1, 0:1], min_val=0, max_val=E)
            with gp.If(falls > 0):
                gp.wait_ge(s_scat[1][0], 16 * FS_A * (EC // FS))
                gp.wait_ge(s_scat[1][1], 16 * (FS - FS_A) * (EC // FS))
                gp.wait_ge(s_addr[0], 1)
                scatter(0, EC // FS, own_staging)
                gp.wait_ge(s_scat[0][0], 16 * FS_A * (EC // FS))
                gp.wait_ge(s_scat[0][1], 16 * (FS - FS_A) * (EC // FS))
                gp.dma_start(REC[0][:, :, :], rec_dram[0].rearrange("(p c) w -> p c w", p=P)).then_inc(s_rel[0], 16)
            with gp.If(falls < 1):
                gp.sem_inc(s_rel[0], 16)

            gp.wait_ge(s_tab, 16 * 2 * NG)
            gp.wait_ge(s_ogd, NG)
            for d in GATHER_ORDER:
                picked, landed = Tally(s_ri[d]), [Tally(s) for s in s_g[d]]

                def gather_turn(base, unit, d=d, picked=picked, landed=landed):
                    for j in range(TURN):
                        if j % 8 == 0:
                            picked.want(gp)
                            apart(gp, base)
                        landed[j // 4].made(gp.indirect_dma_start(
                            GATH[:, j, :], None, table[d][:, :], On(ap=IR[:, j:j + 1], axis=0)), 16)

                gather_turns(gp, d, gather_turn, [picked] + landed)

            gates, hr, mixed, v1 = Tally(s_gates), Tally(s_hr), Tally(s_mix), Tally(s_v1)

            def update(g):
                hr.want(gp, 16)
                gates.want(gp)
                for k in range(KC):
                    gp.tensor_tensor(HB[:, k, :], HB[:, k, :], GNN[:, k, :], ALU.subtract).then_inc(s_dh, 1)
                for k in range(KC):
                    mixed.want(gp)
                    apart(gp, g)
                    last = gp.tensor_tensor(GNN[:, k, :], GNN[:, k, :], OG[:, k, ds(g * GN, GN)], ALU.add)
                last.then_inc(s_gnn, 1)

            def rstd():
                v1.want(gp)
                gp.tensor_tensor(t_rstd, t_var, neghalf, ALU.pow).then_inc(s_r1, 1)

            def turn(g):
                rstd()
                update(g + 1)

            update(0)
            run_turns(gp, NG - 1, turn, [gates, hr, mixed, v1])
            rstd()

        @block.scalar
        def _(act):
            full, free = [Tally(s) for s in s_full], s_free

            def out_of(b, g=0):
                full[b].want(act)
                if not static(g):
                    apart(act, g)
                return bank[b]

            def transposed(plan, o):
                for k, b in enumerate(plan[:2]):
                    act.activation(o[:, k, 0:GN - P], out_of(b)[:, 0:GN - P], ACT.Copy).then_inc(free[b], 1)
                ps = out_of(plan[2])[:, 0:KC * P].rearrange("p (k n) -> p k n", k=KC)
                act.activation(o[:, :, GN - P:GN], ps, ACT.Copy).then_inc(free[plan[2]], 1)

            act.wait_ge(s_edges, 16 * 9)
            act.activation(EF[:, 1, :, :], EI[:, 1, :, :], ACT.Copy).then_inc(s_dflt, 1)
            skip(full, [0])
            act.wait_ge(free[0], 1)
            act.activation(REC[0][:, :, 0], REC[1][:, :, 1], ACT.Copy)
            ps = out_of(1)
            act.activation(REC[0][:, :, 1], ps[:, 0:EC], ACT.Copy)
            act.activation(REC[1][:, :, 0], ps[:, 0:EC], ACT.Copy).then_inc(free[1], 1)
            act.activation(REC[0][:, :, 2], out_of(2)[:, 0:EC], ACT.Copy).then_inc(free[2], 1)
            act.activation(REC[1][:, :, 2], out_of(3)[:, 0:EC], ACT.Copy).then_inc(free[3], 1)
            act.wait_ge(free[3], 1)
            act.sem_inc(s_recs, 1)

            act.wait_ge(s_const, 1)
            for n in range(2):
                act.wait_ge(s_var, n + 1)
                act.activation(rstd, var, ACT.Sqrt, bias=eps_col).then_inc(s_sd, 1)

            act.wait_ge(s_xn, 3)
            skip(full, 2 * [4, 5, 6, 6, 7, 7])

            def stage1(g):
                act.activation(XNR, XROW[:, ds(g * GB, GB), :], ACT.Copy).then_inc(s_xnr, 1)
                for k, b in enumerate(B_XN[:2]):
                    ps = out_of(b, g)
                    act.activation(XH[:, k, ds(g * GN, GN - P)], ps[:, 0:GN - P], ACT.Copy)
                    act.activation(XTR[:, k, 0:GN - P], ps[:, 0:GN - P], ACT.Copy).then_inc(free[b], 1)
                ps = out_of(B_XN[2], g)[:, 0:KC * P].rearrange("p (k n) -> p k n", k=KC)
                act.activation(XH[:, :, ds(g * GN + (GN - P), P)], ps, ACT.Copy).then_inc(s_xh, 1)
                act.activation(XTR[:, :, GN - P:GN], ps, ACT.Copy).then_inc(free[B_XN[2]], 1)
                skip(full, B_XNN)
                for h, b in enumerate(B_HG):
                    act.activation(HG[0:GH, h * HN:(h + 1) * HN], out_of(b)[0:GH, 0:HN], ACT.Gelu,
                                   bias=bg1_c[0:GH, :]).then_inc(free[b], 1)
                skip(full, B_K)
                for q, b in enumerate(B_V):
                    n = min(2, GB - 2 * q)
                    ps = out_of(b, g)[:, 0:n * C].rearrange("p (b k c) -> p b k c", b=n, k=KC)
                    for j in range(n):
                        o = VROW[:, ds(g * GB + 2 * q + j, 1), :, 0:P].rearrange("p a k c -> p (a k) c")
                        last = act.activation(o, ps[:, j], ACT.Copy)
                    last.then_inc(free[b], 1)
                for q, b in enumerate(B_G):
                    m, h = divmod(q, 2)
                    act.activation(OG[:, m, ds(g * GN + h * HN, HN)], out_of(b, g)[:, 0:HN], ACT.Tanh,
                                   bias=bg2_h[:, m:m + 1], scale=0.5).then_inc(free[b], 1)

            run_turns(act, NG, stage1, full)

            act.wait_ge(s_var, 3)
            act.activation(h_scale, bnmv[:, :, 1], ACT.Sqrt, bias=eps_col).then_inc(s_sd, 1)
            act.wait_ge(s_kshift, 1)
            act.activation(KROW, KROW, ACT.Exp).then_inc(s_kexp, 1)
            skip(full, [2, 3, 4, 5])

            ht, fst = Tally(s_ht), Tally(s_fst)
            rows = [t.rearrange("(b p) c -> p b c", p=P) for t in table]

            def stage3(g):
                for q, b in enumerate(B_Q):
                    m, h = divmod(q, 2)
                    act.activation(QT[:, m, h * HN:(h + 1) * HN], out_of(b)[:, 0:HN], ACT.Copy).then_inc(free[b], 1)
                skip(full, B_F + B_O)
                ht.want(act)
                apart(act, g)
                act.dma_start(h_dram[ds(g, 1)].rearrange("a p n -> p (a n)"), HT.rearrange("p k n -> p (k n)")).then_inc(s_hs, 16)
                act.activation(XH[:, :, ds(g * GN, GN)], HT, ACT.Copy).then_inc(s_hk, 1)
                fst.want(act)
                apart(act, g)
                for d in range(2):
                    act.dma_start(rows[d][:, ds(g * GB, GB), :], FSTAGE[:, :, d * C:(d + 1) * C]).then_inc(s_tab, 16)

            run_turns(act, NG, stage3, full + [ht, fst])

            act.wait_ge(s_ogd, NG)
            for d in GATHER_ORDER:
                picked = Tally(s_rr[d])
                act.wait_ge(s_list[d], 1)
                act.wait_ge(s_rel[d], 16)

                def unit_sums(unit, ns):
                    seg = ds(unit * HN, HN)
                    for n in ns:
                        full[4 + n % 4].want(act)
                    apart(act, unit)
                    for n in ns:
                        if n < 4:
                            o, bias = (XH, AGG[0])[n // 2][:, n % 2, seg], bx[:, n:n + 1]
                        else:
                            o, bias = OG[:, n - 4, seg], bp[:, n - 4:n - 3]
                        b = 4 + n % 4
                        act.activation(o, bank[b][:, 0:HN], ACT.Identity, bias=bias).then_inc(free[b], 1)

                def pick_turn(base, unit, d=d, picked=picked):
                    for h in range(TURN // 8):
                        cols = [act.value_load(tile_no[0:1, d, ds(base + j, 1)]).with_bounds(min_val=0, max_val=EC - 1)
                                for j in range(8 * h, 8 * h + 8)]
                        if static(base) and base == 0 and d == GATHER_ORDER[1]:
                            act.wait_ge(s_agg[GATHER_ORDER[0]], STEPS - TURN + 8 * (h + 1))
                        at_least(act, s_agg[d], base + (8 * (h + 1) - TURN))
                        apart(act, base)
                        for j, c in zip(range(8 * h, 8 * h + 8), cols):
                            last = act.activation(RR[:, j:j + 1, :], REC[d][:, ds(c, 1), :], ACT.Copy)
                        picked.made(last)
                        picked.again(act)
                        act.activation(IR[:, 8 * h:8 * h + 8], RR[:, 8 * h:8 * h + 8, 0], ACT.Copy).then_inc(s_ri[d], 1)
                        if unit is not None and h >= 2:
                            unit_sums(unit, range(4) if h == 2 else range(4, 6))

                if d == GATHER_ORDER[0]:
                    gather_turns(act, d, pick_turn, [picked])
                else:
                    act.wait_ge(s_w2, 16 * LAST_LOADS)
                    pick_turn(0, None)
                    run_turns(act, UNITS, lambda i: pick_turn(i * TURN + TURN, i), [picked] + full)
                    for t in range(UNITS + 1, STEPS // TURN):
                        pick_turn(t * TURN, None)

            gx, g2 = Tally(s_gx), Tally(s_g2)
            act.wait_ge(s_w2, 16 * LAST_LOADS)

            def gates_of_next():
                skip(full, T_X)

                def tanh():
                    for q, o, scale in ((3, IG, 0.5), (7, GNN, 1.0)):
                        act.wait_ge(free[T_X[q]], full[T_X[q]].value())
                        last = act.activation(o, o, ACT.Tanh, scale=scale)
                    last.then_inc(s_gates, 1)
                return tanh

            def stage5(g, more=True):
                skip(full, T_R)
                tanh = gates_of_next() if more else None
                transposed(T_T, XT1)
                if more:
                    tanh()
                for q, b in enumerate(T_S1):
                    m, h = divmod(q, 2)
                    act.activation(S1[:, m, h * HN:(h + 1) * HN], out_of(b)[:, 0:HN], ACT.Relu,
                                   bias=b1s[:, m:m + 1]).then_inc(free[b], 1)
                gx.want(act)
                act.activation(t_exp, t_log, ACT.Exp).then_inc(s_gexp, 1)
                for q, b in enumerate(T_E1):
                    m, h = divmod(q, 2)
                    act.activation(E1[:, m, h * HN:(h + 1) * HN], out_of(b)[:, 0:HN], ACT.Relu,
                                   bias=b1e[:, m:m + 1]).then_inc(free[b], 1)
                    if q == 5:
                        g2.want(act)
                        act.activation(t_gap_e, t_gap, ACT.Exp).then_inc(s_g2e, 1)
                for h, b in enumerate(T_S2):
                    act.activation(S2[:, h * HN:(h + 1) * HN], out_of(b)[:, 0:HN], ACT.Relu, bias=b2s).then_inc(free[b], 1)
                for q, b in enumerate(T_E2):
                    m, h = divmod(q, 2)
                    act.activation(E2[:, m, h * HN:(h + 1) * HN], out_of(b)[:, 0:HN], ACT.Relu,
                                   bias=b2e[:, m:m + 1]).then_inc(free[b], 1)
                skip(full, T_W[0:3])
                for b, (lo, hi) in zip(T_W[3:], ((0, GN - P), (GN - P, GN))):
                    act.activation(WGT[0:NEXP + 1, lo:hi], out_of(b)[0:NEXP + 1, 0:hi - lo], ACT.Copy).then_inc(free[b], 1)
                skip(full, T_O)

            gates_of_next()()
            run_turns(act, NG - 1, stage5, full + [gx, g2])
            stage5(NG - 1, more=False)

        @block.tensor
        def _(pe):
            full, free = s_full, [Tally(s) for s in s_free]
            mm = pe.matmul

            def into(b, g=0):
                free[b].again(pe)
                free[b].n += 1
                return bank[b]

            def read_out(plan):
                for b in sorted(set(plan)):
                    free[b].again(pe)

            def product(b, cols, pairs, parts=P):
                ps = into(b)[0:parts, 0:cols]
                for n, (w, m) in enumerate(pairs):
                    last = mm(ps, w, m, start=n == 0, stop=n == len(pairs) - 1)
                last.then_inc(full[b], 1)

            def transposes(plan, rows):
                for k in range(KC):
                    ps = into(plan[k])
                    for j in range(GB - 1):
                        last = pe.transpose(ps[:, j * P:(j + 1) * P], rows[:, j, k * P:(k + 1) * P], ident[:, :])
                    last.then_inc(full[plan[k]], 1)
                ps = into(plan[2])
                for k in range(KC):
                    last = pe.transpose(ps[:, k * P:(k + 1) * P], rows[:, GB - 1, k * P:(k + 1) * P], ident[:, :])
                last.then_inc(full[plan[2]], 1)

            pe.wait_ge(s_const, 1)
            for a in range(4):
                if a == 0:
                    pe.wait_ge(s_eflt, 1)
                if a == 1:
                    pe.wait_ge(s_dflt, 1)
                    pe.wait_ge(s_edges, 16 * 9)
                ps = into(a)
                for q in range(3):
                    pe.transpose(ps[:, q * P:(q + 1) * P], EF[:, a, q, :], ident[:, :])
                r = EC - 3 * P
                pe.transpose(ps[:, 3 * P:EC], EF[0:r, a, 3, :], ident[0:r, 0:r]).then_inc(full[a], 1)
            K = NB + 1
            for n in range(2):
                pe.wait_ge(s_cnt, 4 * n + 1)
                product(4, K, [(upper[:, :], cnt[:, 0:K])])
                product(5, K + 1, [(onesm[:, :], cnt)])
                pe.wait_ge(s_cnt, 4 * n + 2)
                product(6, 1, [(upper[0:K, 0:K], colw[0:K, 3:4])], parts=K)
                pe.wait_ge(s_cnt, 4 * n + 3)
                product(7, 1, [(diffm[:, :], colw[0:K, 5:6])], parts=K)
                pe.wait_ge(s_cnt, 4 * n + 4)
                product(6, STEPS, [(ddrep, GT)])
                product(7, STEPS, [(onesm[0:K, :], GT)])

            xnr, xnnr = Tally(s_xnr), Tally(s_xnnr)
            pe.wait_ge(s_w1, 16 * FIRST_LOADS)

            def stage1(g):
                xnr.want(pe)
                transposes(B_XN, XNR)
                xnnr.want(pe)
                transposes(B_XNN, XNNR)
                read_out(B_XNN)
                for h, b in enumerate(B_HG):
                    product(b, HN, [(Wg1s[:, k, :], XNT[:, k, h * HN:(h + 1) * HN]) for k in range(KC)], parts=GH)
                read_out(B_XN)
                for first_col, plan in ((C, B_K), (2 * C, B_V)):
                    for q, b in enumerate(plan):
                        ps = into(b)
                        for j in range(2 * q, min(2 * q + 2, GB)):
                            for k in range(KC):
                                last = mm(ps[:, (j % 2) * C:(j % 2 + 1) * C], XTR[:, k, j * P:(j + 1) * P],
                                          Wq[:, k, first_col:first_col + C], start=k == 0, stop=k == KC - 1)
                        last.then_inc(full[b], 1)
                read_out(B_HG)
                for q, b in enumerate(B_G):
                    m, h = divmod(q, 2)
                    product(b, HN, [(Wg2s[0:GH, m * P:(m + 1) * P], HG[0:GH, h * HN:(h + 1) * HN])])

            run_turns(pe, NG, stage1, free + [xnr, xnnr])

            pe.wait_ge(s_kmax, 1)
            ps = into(2)
            for k in range(KC):
                last = pe.transpose(ps[:, k * P:(k + 1) * P], KMAX[:, k * P:(k + 1) * P], ident[:, :])
            last.then_inc(full[2], 1)
            pe.wait_ge(s_kmax, 2)
            ps = into(3)
            for k in range(KC):
                last = mm(ps[:, k * P:(k + 1) * P], onesm[:, :], CTX[:, k, :], start=True, stop=True)
            last.then_inc(full[3], 1)
            pe.wait_ge(s_kexp, 1)
            read_out(B_V)
            pe.wait_ge(s_vrow, 1)
            for m in range(KC):
                product(4 + m, P + 1, [(KROW[:, b, m * P:(m + 1) * P], VROW[:, b, m, :]) for b in range(NB)])

            ht = Tally(s_ht)

            def stage3(g):
                for q, b in enumerate(B_Q):
                    m, h = divmod(q, 2)
                    product(b, HN, [(Wq[:, k, m * P:(m + 1) * P], XH[:, k, ds(g * GN + h * HN, HN)]) for k in range(KC)])
                ht.want(pe)
                for j, b in enumerate(B_F):
                    product(b, 2 * C, [(HT[:, k, j * P:(j + 1) * P], Wio[:, k, :]) for k in range(KC)])
                read_out(B_Q)
                for q, b in enumerate(B_O):
                    m, h = divmod(q, 2)
                    product(b, HN, [(CTX[:, m, :], QT[:, m, h * HN:(h + 1) * HN])])

            pe.wait_ge(s_xh, NG)
            read_out([4, 5])
            run_turns(pe, NG, stage3, free + [ht])
            read_out(range(8))

            for d in GATHER_ORDER:
                got, onehot = [Tally(s) for s in s_g[d]], Tally(s_m[d])
                def multiply(base, j, d=d, got=got, onehot=onehot):
                    if j % 4 == 0:
                        got[j // 4].want(pe, 16 * 4)
                    onehot.want(pe)
                    if j % 2 == 0:
                        if static(base) and base == 0 and d == GATHER_ORDER[1] and j < 8:
                            pe.wait_ge(s_add[GATHER_ORDER[0]], STEPS - 6 + j)
                        at_least(pe, s_add[d], base + (j - 6))
                    ps = bank[j // 2 % 4][:, j % 2 * C:(j % 2 + 1) * C]
                    for k in range(KC):
                        last = mm(ps[:, k * P:(k + 1) * P], GATH[:, j, k * P:(k + 1) * P], ONEHOT[:, j % 8, :],
                                  start=True, stop=True)
                    last.then_inc(s_agg[d], 1)

                def unit_products(u):
                    seg = ds(u * HN, HN)
                    for m in range(4):
                        ps = into(4 + m)[:, 0:HN]
                        for n, (s, t) in enumerate(((0, AGG[0]), (2, XH))):
                            for k in range(KC):
                                last = mm(ps, Wx[:, 2 * s + k, m * P:(m + 1) * P], t[:, k, seg],
                                          start=n + k == 0, stop=n + k == 2)
                                if n + k == 2:
                                    last.then_inc(full[4 + m], 1)
                                yield
                    for m in range(KC):
                        ps = into(4 + m)[:, 0:HN]
                        for k in range(KC):
                            last = mm(ps, Wp[:, k, m * P:(m + 1) * P], OG[:, k, seg], start=k == 0, stop=k == 1)
                            if k == 1:
                                last.then_inc(full[4 + m], 1)
                            yield

                def multiply_turn(base, unit):
                    products = None if unit is None else unit_products(unit)
                    for j in range(TURN):
                        multiply(base, j)
                        if products and (2 <= j < 22 and j % 5 != 1 or 26 <= j < 30):
                            next(products)

                if d == GATHER_ORDER[1]:
                    pe.wait_ge(s_w2, 16 * LAST_LOADS)
                gather_turns(pe, d, multiply_turn, [onehot] + got + free)

            gnn, xn1, wg = (Tally(s) for s in (s_gnn, s_xn1, s_wg))
            pe.wait_ge(s_add[GATHER_ORDER[1]], STEPS)
            pe.wait_ge(s_hk, NG)

            def update_sums(first_node, qs):
                for q in qs:
                    b, (m, h) = T_X[q], divmod(q, 2)
                    product(b, HN, [(Wx[:, KC + k, m * P:(m + 1) * P], AGG[1][:, k, ds(first_node + h * HN, HN)])
                                    for k in range(KC)])

            def stage5(g, more=True):
                gnn.want(pe)
                for j, b in enumerate(T_R):
                    ps = into(b)
                    for k in range(KC):
                        last = pe.transpose(ps[:, k * P:(k + 1) * P], GNN[:, k, j * P:(j + 1) * P], ident[:, :])
                    last.then_inc(full[b], 1)
                if more:
                    update_sums(g * GN + GN, range(0, 7))
                xn1.want(pe)
                transposes(T_T, XN1)
                if more:
                    update_sums(g * GN + GN, range(7, 8))
                read_out(T_T[:2])
                for q, b in enumerate(T_S1):
                    m, h = divmod(q, 2)
                    if q == 1:
                        read_out(T_T[2:])
                    product(b, HN, [(W1s[:, k, m * P:(m + 1) * P], XT1[:, k, h * HN:(h + 1) * HN]) for k in range(KC)])
                for q, b in enumerate(T_E1):
                    m, h = divmod(q, 2)
                    product(b, HN, [(W1e[:, k, m, :], XT1[:, k, h * HN:(h + 1) * HN]) for k in range(KC)])
                for h, b in enumerate(T_S2):
                    product(b, HN, [(W2s[:, k, :], S1[:, k, h * HN:(h + 1) * HN]) for k in range(2)])
                read_out(T_E1[3:])
                for q, b in enumerate(T_E2):
                    m, h = divmod(q, 2)
                    ps = into(b)
                    for e in range(2):
                        last = mm(ps[e * EH2:(e + 1) * EH2, 0:HN], W2e[:, 2 * m + e, :],
                                  E1[:, 2 * m + e, h * HN:(h + 1) * HN], start=True, stop=True)
                    last.then_inc(full[b], 1)
                wg.want(pe)
                transposes(T_W[0:3], WGX.rearrange("p j m c -> p j (m c)"))
                for b, js in ((T_W[3], range(GB - 1)), (T_W[4], range(GB - 1, GB))):
                    ps = into(b)
                    for n, j in enumerate(js):
                        last = pe.transpose(ps[0:NEXP + 1, n * P:(n + 1) * P], t_w5[:, j, :], ident[:, :])
                    last.then_inc(full[b], 1)
                for j, b in enumerate(T_O):
                    mm(into(b)[:, 0:C], S2[:, j * P:(j + 1) * P], W3s, start=True, stop=False)
                read_out([5, 6, 7])
                for j, b in enumerate(T_O):
                    n = slice(j * P, (j + 1) * P)
                    mm(bank[b][:, 0:C], E2[:, 0, n], W3e[:, 0, :], start=False, stop=False)
                    mm(bank[b][:, 0:C], E2[:, 1, n], W3e[:, 1, :], start=False, stop=False)
                    mm(bank[b][:, 0:C], WGT[0:NEXP + 1, n], B3[0:NEXP + 1, :], start=False, stop=True).then_inc(full[b], 1)

            update_sums(0, range(8))
            run_turns(pe, NG - 1, stage5, free + [gnn, xn1, wg])
            stage5(NG - 1, more=False)

        @block.vector
        def _(dve):
            full, free = [Tally(s) for s in s_full], s_free
            steps = Tally(s_dve)
            v = nc.vector

            def link(ins):
                steps.link(dve, ins)

            def out_of(b):
                full[b].want(dve)
                return bank[b]

            def landed(b):
                dve.wait_ge(free[b], full[b].value())

            def row_stats(st, m, va, a, c):
                v.tensor_tensor(a, st[:, :, 1], st[:, :, 4], ALU.subtract)
                v.tensor_tensor(c, st[:, :, 2], st[:, :, 5], ALU.add)
                link(v.tensor_tensor(m, st[:, :, 1], st[:, :, 4], ALU.add))
                v.tensor_scalar(m, m, 0.5, None, ALU.mult)
                link(v.scalar_tensor_tensor(a, a, 0.25, a, ALU.mult, ALU.mult))
                link(v.scalar_tensor_tensor(va, c, 1.0 / C, a, ALU.mult, ALU.add))

            v.memset(EI[:, :, 3, :], NP - 1).then_inc(s_pad, 1)
            v.memset(SEQ[1], NP - 1)
            v.memset(EF[:, 2:4, 3, :], 0.0).then_inc(s_pad, 1)
            v.memset(XROW[:, NB - 1, :], 0.0).then_inc(s_xz, 1)
            v.memset(ZERO, 0.0)
            v.memset(cnt[:, NB:NB + 2], 0.0)
            dve.wait_ge(s_src, 16 * 3)
            v.tensor_copy(EF[:, 0, :, :], EI[:, 0, :, :]).then_inc(s_eflt, 1)
            v.tensor_copy(REC[1][:, :, 1], out_of(0)[:, 0:EC]).then_inc(free[0], 1)
            landed(0)
            skip(full, [1, 2, 3])
            dve.wait_ge(s_const, 1)

            def places(d, done, lo, hi, start, following=None):
                n = hi - lo
                for b in range(NB + 1):
                    if b < NB:
                        done.made(v.tensor_tensor_scan(SCAN[b % 3][:, 0:n], ONEB[:, b, lo:hi], ZERO[:, 0:n],
                                                       start[:, b:b + 1], ALU.add, ALU.add))
                    if b > 0:
                        done.again(dve, 1 if b < NB else 0)
                        s = SCAN[(b - 1) % 3]
                        if following is not None:
                            v.tensor_copy(following[:, b - 1:b], s[:, n - 1:n])
                        done.made(v.copy_predicated(SLOT[:, lo:hi], ONEB[:, b - 1, lo:hi].bitcast(mybir.dt.uint16), s[:, 0:n]))
                done.again(dve)
                done.link(dve, v.tensor_copy(KEYI[:, lo:hi], SLOT[:, lo:hi]))
                v.tensor_scalar(LOI[:, lo:hi], KEYI[:, lo:hi], P - 1, None, ALU.bitwise_and)
                done.link(dve, v.tensor_scalar(HII[:, lo:hi], KEYI[:, lo:hi], 7, None, ALU.arith_shift_right))
                v.scalar_tensor_tensor(ADDR[d][:, lo:hi], LOI[:, lo:hi], float(EC), HII[:, lo:hi],
                                       ALU.mult, ALU.add).then_inc(s_addr[d], 1)

            K = NB + 1
            for d in SORT_ORDER:
                if d == 0:
                    dve.wait_ge(s_recs, 1)
                    dve.wait_ge(s_seq, 48)
                    link(v.tensor_tensor(FALL, SEQ[0], SEQ[1], ALU.is_gt))
                    link(v.tensor_reduce(cnt[0:E // SQ, NB + 1:NB + 2], FALL, AX.X, ALU.add))
                link(v.tensor_copy(KEYI, REC[d][:, :, 1]))
                link(v.tensor_scalar(KEYI, KEYI, 7, None, ALU.arith_shift_right))
                link(v.tensor_copy(KEYB, KEYI))
                for b in range(NB):
                    last = v.tensor_scalar(ONEB[:, b, :], KEYB, float(b), None, ALU.is_equal, ALU.add,
                                           accum_out=cnt[:, b:b + 1])
                last.then_inc(s_cnt, 1)
                v.memset(SLOT, 0.0)
                before, tot = out_of(4), out_of(5)
                link(v.tensor_copy(total, tot[:, 0:K]))
                if d == 0:
                    v.tensor_copy(unsorted[:, :], tot[0:1, K:K + 1]).then_inc(s_flag, 1)
                    dve.wait_ge(s_flag, 1)
                dve.sem_inc(free[5], 1)
                link(v.tensor_tensor_scan(incl, total, zero_f, 0.0, ALU.add, ALU.add))
                link(v.tensor_tensor(total, incl, total, ALU.subtract))
                v.scalar_tensor_tensor(base, total, -1.0, before[:, 0:K], ALU.add, ALU.add).then_inc(free[4], 1)
                link(v.memset(colw, 0.0))
                landed(4)
                if d == 1:
                    places(d, steps, 0, EARLY * FS, base, base_2)
                    places(d, steps, EARLY * FS, EC, base_2)
                else:
                    falls = dve.value_load(unsorted[0:1, 0:1], min_val=0, max_val=E)
                    with dve.If(falls > 0):
                        places(d, Tally(s_rank), 0, EC, base)

                v.tensor_tensor(SCAN[0][0:K, 0:K], total[0:K, :], ident[0:K, 0:K], ALU.mult)
                link(v.tensor_tensor(SCAN[1][0:K, 0:K], incl[0:K, :], ident[0:K, 0:K], ALU.mult))
                v.tensor_reduce(colw[0:K, 0:1], SCAN[0][0:K, 0:K], AX.X, ALU.add)
                link(v.tensor_reduce(colw[0:K, 1:2], SCAN[1][0:K, 0:K], AX.X, ALU.add))
                v.tensor_copy(coli[0:K, 0:1], colw[0:K, 0:1])
                link(v.tensor_scalar(coli[0:K, 1:2], colw[0:K, 1:2], float(P - 1), None, ALU.add))
                link(v.tensor_scalar(coli[0:K, 0:2], coli[0:K, 0:2], 7, None, ALU.arith_shift_right))
                link(v.tensor_copy(colw[0:K, 1:3], coli[0:K, 0:2]))
                v.tensor_tensor(colw[0:K, 3:4], colw[0:K, 2:3], colw[0:K, 1:2], ALU.subtract).then_inc(s_cnt, 1)
                ps = out_of(6)
                link(v.tensor_copy(colw[0:K, 4:5], ps[0:K, 0:1]))
                dve.sem_inc(free[6], 1)
                v.tensor_tensor(colw[0:K, 5:6], colw[0:K, 1:2], colw[0:K, 4:5], ALU.subtract).then_inc(s_cnt, 1)
                ps = out_of(7)
                v.tensor_scalar(ddrep, onesm[0:K, :], ps[0:K, 0:1], None, ALU.mult).then_inc(free[7], 1)
                v.tensor_scalar(GT, steps_ramp[0:K, :], colw[0:K, 4:5], None, ALU.is_ge).then_inc(s_cnt, 1)
                ps = out_of(6)
                v.tensor_tensor(GTMP, ps[0:1, 0:STEPS], steps_ramp[0:1, :], ALU.add).then_inc(free[6], 1)
                ps = out_of(7)
                v.tensor_scalar(step_off[d][:, :], ps[:, 0:STEPS], float(P), float(-P), ALU.mult, ALU.add).then_inc(free[7], 1)
                landed(6)
                landed(7)
                link(v.tensor_scalar(GTMP, GTMP, float(EC - 1), 0.0, ALU.min, ALU.max))
                v.tensor_copy(tile_no[0:1, d, :], GTMP)
                v.tensor_scalar(acc_col[0:1, d, :], step_off[d][0:1, :], float((NB - 1) * P), None, ALU.min).then_inc(s_list[d], 1)

            dve.wait_ge(s_x, 32)
            for n in range(2):
                with dve.Fori(0, NB) as b:
                    v.bn_stats(stats[:, ds(b, 1), :].rearrange("p a s -> p (a s)"), XROW[:, ds(b, 1), :].rearrange("p a c -> p (a c)"))
                link(dve.drain())
                row_stats(stats, mean, var, ws1, ws2)
                dve.sem_inc(s_var, 1)
                dve.wait_ge(s_sd, n + 1)
                link(v.reciprocal(rstd, rstd))
                if n == 0:
                    with dve.Fori(0, NB) as b:
                        v.tensor_scalar(XROW[:, ds(b, 1), :].rearrange("p a c -> p (a c)"),
                                        XROW[:, ds(b, 1), :].rearrange("p a c -> p (a c)"),
                                        mean[:, ds(b, 1)], rstd[:, ds(b, 1)], ALU.subtract, ALU.mult)
                    link(dve.drain())
                dve.sem_inc(s_xn, 1)

            dve.wait_ge(s_w1, 16 * FIRST_LOADS)
            v.tensor_scalar(bg2_h, bg2_c, 0.5, None, ALU.mult)
            for k in range(KC):
                v.tensor_scalar(VROW[:, :, k, P], padneg, 0.0, None, ALU.is_ge)
            v.memset(KMAX[:, :], FAR).then_inc(s_vrow, 1)
            dve.wait_ge(s_vrow, 1)
            dve.sem_inc(s_xn, 1)

            def stage1(g):
                skip(full, B_XN)
                for j in range(GB):
                    b = ds(g * GB + j, 1)
                    last = v.tensor_scalar(XNNR[:, j, :], XROW[:, b, :].rearrange("p a c -> p (a c)"), mean[:, b], rstd[:, b],
                                           ALU.subtract, ALU.mult)
                last.then_inc(s_xnnr, 1)
                for k in range(KC):
                    v.tensor_scalar(XNT[:, k, 0:GN - P], out_of(B_XNN[k])[:, 0:GN - P], lng_c[:, k:k + 1], lnb_c[:, k:k + 1],
                                    ALU.mult, ALU.add).then_inc(free[B_XNN[k]], 1)
                ps = out_of(B_XNN[2])
                for k in range(KC):
                    last = v.tensor_scalar(XNT[:, k, GN - P:GN], ps[:, k * P:(k + 1) * P], lng_c[:, k:k + 1], lnb_c[:, k:k + 1],
                                           ALU.mult, ALU.add)
                last.then_inc(free[B_XNN[2]], 1)
                skip(full, B_HG)
                for q, b in enumerate(B_K):
                    ps = out_of(b)
                    n = min(2, GB - 2 * q)
                    for j in range(n):
                        blk = ds(g * GB + 2 * q + j, 1)
                        v.tensor_scalar(KROW[:, blk, :].rearrange("p a c -> p (a c)"), ps[:, j * C:(j + 1) * C],
                                        padneg[:, blk], None, ALU.add)
                        last = v.scalar_tensor_tensor(KMAX[:, :], ps[:, j * C:(j + 1) * C], padneg[:, blk], KMAX[:, :],
                                                      ALU.add, ALU.max)
                        if j < n - 1:
                            link(last)
                    last.then_inc(free[b], 1)
                    landed(b)

                skip(full, B_V + B_G)

            run_turns(dve, NG, stage1, full + [steps])

            link(dve.drain())
            dve.wait_ge(s_xh, NG)
            for k in range(KC):
                width = -(-N // 7)
                for n in range(7):
                    v.bn_stats(cs[:, n, :], XH[:, k, n * width:min(N, (n + 1) * width)])
                link(dve.drain())
                link(v.bn_aggr(bnmv[:, k, :], cs))
            dve.sem_inc(s_var, 1)
            dve.sem_inc(s_kmax, 1)
            ps = out_of(2)
            link(v.tensor_reduce(rsum, ps[:, 0:KC * P].rearrange("p (k n) -> p k n", k=KC), AX.X, ALU.max))
            dve.sem_inc(free[2], 1)
            for k in range(KC):
                last = v.tensor_scalar(CTX[:, k, :], ident[:, :], rsum[:, k:k + 1], None, ALU.mult)
            last.then_inc(s_kmax, 1)
            ps = out_of(3)
            link(v.tensor_copy(KMAX[:, :], ps[:, 0:C]))
            dve.sem_inc(free[3], 1)
            v.tensor_tensor(KROW, KROW, KMAX[:, :].unsqueeze(1).to_broadcast([P, NB, C]), ALU.subtract).then_inc(s_kshift, 1)
            dve.wait_ge(s_sd, 3)
            link(v.reciprocal(h_scale, h_scale))
            link(v.tensor_tensor(h_scale, h_scale, gamma_c, ALU.mult))
            link(v.tensor_tensor(h_shift, bnmv[:, :, 0], h_scale, ALU.mult))
            link(v.tensor_tensor(h_shift, beta_c, h_shift, ALU.subtract))
            for m in range(KC):
                ps = out_of(4 + m)
                link(v.reciprocal(rsum[:, m:m + 1], ps[:, P:P + 1]))
                v.scalar_tensor_tensor(CTX[:, m, :], ps[:, 0:P], rsum[:, m:m + 1], headm[:, :],
                                       ALU.mult, ALU.mult).then_inc(free[4 + m], 1)
            v.memset(FLAT[0], 0.0)
            link(v.memset(FLAT[1], 0.0))

            def stage3(g):
                skip(full, B_Q)
                if not static(g):
                    dve.wait_ge(s_hk, g)
                    dve.wait_ge(s_hs, g * 16)
                for k in range(KC):
                    last = v.tensor_scalar(HT[:, k, :], XH[:, k, ds(g * GN, GN)], h_scale[:, k:k + 1], h_shift[:, k:k + 1],
                                           ALU.mult, ALU.add)
                last.then_inc(s_ht, 1)
                if not static(g):
                    dve.wait_ge(s_tab, g * 32)
                for j, b in enumerate(B_F):
                    v.tensor_tensor(FSTAGE[:, j, :], out_of(b)[:, :], bio, ALU.add).then_inc(free[b], 1)
                dve.drain().then_inc(s_fst, 1)
                for q, b in enumerate(B_O):
                    m, h = divmod(q, 2)
                    o = OG[:, m, ds(g * GN + h * HN, HN)]
                    v.scalar_tensor_tensor(o, o, 1.0, out_of(b)[:, 0:HN], ALU.add, ALU.mult).then_inc(free[b], 1)
                dve.drain().then_inc(s_ogd, 1)

            run_turns(dve, NG, stage3, full + [steps])

            for d in GATHER_ORDER:
                picked, product, added = Tally(s_rr[d]), Tally(s_agg[d]), Tally(s_add[d])

                def targets(at, r, d=d, picked=picked):
                    picked.want(dve)
                    link(v.tensor_tensor(REL[:, r:r + 8], RR[:, r:r + 8, 1], step_off[d][:, ds(at, 8)], ALU.subtract))

                def onehot(j, d=d):
                    v.tensor_scalar(ONEHOT[:, j % 8, :], ramp[:, :], REL[:, j:j + 1], RR[:, j, 2:3],
                                    ALU.is_equal, ALU.mult).then_inc(s_m[d], 1)

                def add_turn(base, unit, d=d, product=product, added=added):
                    for j in range(TURN):
                        more = not (static(base) and base == STEPS - TURN and j >= TURN - 8)
                        if more and j % 8 == 0:
                            targets(base + (j + 8), (j + 8) % TURN)
                        c = dve.value_load(acc_col[0:1, d, ds(base + j, 1)]).with_bounds(min_val=0, max_val=(NB - 1) * P)
                        o = AGG[d][:, :, ds(c, P)]
                        added.again(dve)
                        if j % 2 == 0:
                            product.want(dve, 2)
                        ps = bank[j // 2 % 4][:, j % 2 * C:(j % 2 + 1) * C]
                        added.made(v.tensor_tensor(o, o, ps.rearrange("p (k n) -> p k n", k=KC), ALU.add))
                        if more:
                            onehot((j + 8) % TURN)

                targets(0, 0)
                for j in range(8):
                    onehot(j)
                gather_turns(dve, d, add_turn, [steps, picked, product, added])
            for u in range(UNITS):
                skip(full, [4, 5, 6, 7, 4, 5])

            dve.wait_ge(s_w2, 16 * LAST_LOADS)
            xr, dh, r1, xn1, gexp, g2e = (Tally(s) for s in (s_xr, s_dh, s_r1, s_xn1, s_gexp, s_g2e))

            def each(t2, n=NEXP):
                return t2.unsqueeze(2).to_broadcast([P, GB, n])

            def first_of(o, score, best):
                link(v.tensor_tensor(o, score, each(best), ALU.is_equal))
                link(v.tensor_tensor(o, o, pref.unsqueeze(1).to_broadcast([P, GB, NEXP]), ALU.mult))
                link(v.tensor_reduce(t_m, o, AX.X, ALU.max))
                link(v.tensor_tensor(o, o, each(t_m), ALU.is_equal))

            def update_sums(first_node, qs):
                for q in qs:
                    b, (m, h) = T_X[q], divmod(q, 2)
                    v.tensor_tensor((IG, GNN)[m // 2][:, m % 2, h * HN:(h + 1) * HN], out_of(b)[:, 0:HN],
                                    (XH, AGG[0])[m // 2][:, m % 2, ds(first_node + h * HN, HN)], ALU.add).then_inc(free[b], 1)

            def mix(ks):
                for k in ks:
                    dh.want(dve)
                    link(v.scalar_tensor_tensor(HB[:, k, :], IG[:, k, :], 1.0, HB[:, k, :], ALU.add, ALU.mult))
                    v.scalar_tensor_tensor(GNN[:, k, :], HB[:, k, :], 0.5, GNN[:, k, :], ALU.mult, ALU.add).then_inc(s_mix, 1)

            def stage5(g, more=True):
                xr.want(dve, 32)
                for j, b in enumerate(T_R):
                    v.tensor_tensor(X1[:, j, :], XL[:, j, :], out_of(b)[:, 0:C], ALU.add).then_inc(free[b], 1)
                    if j:
                        landed(T_R[j - 1])
                        v.bn_stats(stats[:, j - 1, :], X1[:, j - 1, :])
                landed(T_R[-1])
                v.bn_stats(stats[:, GB - 1, :], X1[:, GB - 1, :])
                link(dve.drain())
                row_stats(stats[:, 0:GB], t_mean, t_var, t_a, t_c)
                v.tensor_scalar(t_var, t_var, EPS, None, ALU.add).then_inc(s_v1, 1)
                if more:
                    update_sums(g * GN + GN, range(0, 3))
                at_least(dve, s_st, g * 32)
                r1.want(dve)
                for j in range(GB):
                    last = v.tensor_scalar(XN1[:, j, :], X1[:, j, :], t_mean[:, j:j + 1], t_rstd[:, j:j + 1],
                                           ALU.subtract, ALU.mult)
                last.then_inc(s_xn1, 1)
                if more:
                    update_sums(g * GN + GN, range(3, 8))
                skip(full, T_T)
                xn1.want(dve)
                for e in range(NEXP):
                    for j in range(GB):
                        last = v.tensor_tensor_reduce(E2.rearrange("p k n -> p (k n)")[:, j * C:(j + 1) * C], XN1[:, j, :],
                                                      Wgate[:, :, e], 1.0, gb_row[:, e:e + 1], ALU.mult, ALU.add,
                                                      t_log[:, j, e:e + 1])
                    link(last)
                link(v.tensor_reduce(t_m, t_log, AX.X, ALU.max))
                v.tensor_tensor(t_log, t_log, each(t_m), ALU.subtract).then_inc(s_gx, 1)
                gexp.want(dve)
                link(v.tensor_reduce(t_m, t_exp, AX.X, ALU.add))
                link(v.reciprocal(t_m, t_m))
                link(v.tensor_tensor(t_g, t_exp, each(t_m), ALU.mult))
                link(v.tensor_reduce(t_m1, t_g, AX.X, ALU.max))
                first_of(t_o1, t_g, t_m1)
                link(v.scalar_tensor_tensor(t_sc, t_o1, -2.0, t_g, ALU.mult, ALU.add))
                link(v.tensor_reduce(t_m2, t_sc, AX.X, ALU.max))
                v.tensor_tensor(t_gap, t_m2, t_m1, ALU.subtract).then_inc(s_g2, 1)
                if more:
                    mix(range(1))
                skip(full, T_S1 + T_E1)
                first_of(t_o2, t_sc, t_m2)
                g2e.want(dve)
                link(v.tensor_scalar(t_m, t_gap_e, 1.0, None, ALU.add))
                link(v.reciprocal(t_m, t_m))
                link(v.tensor_tensor(t_wt, t_gap_e, t_m, ALU.mult))
                v.tensor_tensor(t_o1, t_o1, each(t_m), ALU.mult)
                link(v.tensor_tensor(t_o2, t_o2, each(t_wt), ALU.mult))
                link(v.tensor_tensor(t_w5[:, :, 0:NEXP], t_o1, t_o2, ALU.add))
                dve.wait_ge(s_full[T_E1[-1]], full[T_E1[-1]].value())
                for j in range(GB):
                    last = v.tensor_copy(WGX[:, j].rearrange("p m c -> p (m c)").rearrange("p (e c) -> p e c", e=NEXP),
                                         t_w5[:, j, 0:NEXP].unsqueeze(2).to_broadcast([P, NEXP, EH2]))
                last.then_inc(s_wg, 1)
                if more:
                    mix(range(1, KC))
                skip(full, T_S2 + T_E2)
                for b in T_E2:
                    landed(b)
                for k in range(KC):
                    b = T_W[k]
                    v.tensor_tensor(E2[:, k, 0:GN - P], E2[:, k, 0:GN - P], out_of(b)[:, 0:GN - P], ALU.mult).then_inc(free[b], 1)
                b = T_W[2]
                v.tensor_tensor(E2[:, :, GN - P:GN], E2[:, :, GN - P:GN],
                                out_of(b)[:, 0:KC * P].rearrange("p (k n) -> p k n", k=KC), ALU.mult).then_inc(free[b], 1)
                skip(full, T_W[3:])
                for j, b in enumerate(T_O):
                    v.tensor_tensor(OUTR[:, j, :], out_of(b)[:, 0:C], X1[:, j, :], ALU.add).then_inc(free[b], 1)
                dve.drain().then_inc(s_out, 1)

            update_sums(0, range(8))
            mix(range(KC))
            run_turns(dve, NG - 1, stage5, full + [steps, xr, dh, r1, xn1, gexp, g2e])
            stage5(NG - 1, more=False)


def kernel(**inputs):
    import numpy as np
    import concourse.bacc as bacc
    from concourse import mybir
    from concourse.bass_utils import run_bass_kernel_spmd

    nc = bacc.Bacc("TRN2", target_bir_lowering=False, num_devices=1)
    names = ("x src dst edge_weight edge_weight_n2 L0_gnn_gamma L0_gnn_beta L0_gnn_W_in L0_gnn_b_in L0_gnn_W_out "
             "L0_gnn_b_out L0_gnn_W_x2i L0_gnn_b_x2i L0_gnn_W_h2h L0_mix_Wqkv L0_mix_Wproj L0_mix_bproj L0_mix_ln_g "
             "L0_mix_ln_b L0_mix_Wg1 L0_mix_bg1 L0_mix_Wg2 L0_mix_bg2 L0_ffn_sW1 L0_ffn_sb1 L0_ffn_sW2 L0_ffn_sb2 "
             "L0_ffn_sW3 L0_ffn_sb3 L0_ffn_eW1 L0_ffn_eb1 L0_ffn_eW2 L0_ffn_eb2 L0_ffn_eW3 L0_ffn_eb3 L0_ffn_gW "
             "L0_ffn_gb").split()
    arrays, args = {}, []
    for name in names:
        a = np.ascontiguousarray(inputs[name])
        arrays[f"in_{name}"] = a
        args.append(nc.dram_tensor(f"in_{name}", a.shape, mybir.dt.from_np(a.dtype), kind="ExternalInput").ap())
    args.append(nc.dram_tensor("out0", (N, C), mybir.dt.float32, kind="ExternalOutput").ap())
    gps_layer(nc, *args)
    result = run_bass_kernel_spmd(nc, [arrays], core_ids=[0])
    return result.results[0]["out0"]
```
